# Optimizing a Trainium2 kernel written in Bass

```python
import numpy as np
import jax
import jax.numpy as jnp

def _softmax(x, axis=-1):
    return jax.nn.softmax(x, axis=axis)

def _gelu(x):
    return jax.nn.gelu(x, approximate=True)

def _silu(x):
    return jax.nn.silu(x)

def _sigmoid(x):
    return jax.nn.sigmoid(x)

def _layernorm(x, axis=-1, eps=1e-05):
    m = jnp.mean(x, axis=axis, keepdims=True)
    v = jnp.var(x, axis=axis, keepdims=True)
    return (x - m) / jnp.sqrt(v + eps)

def _scatter_add(tgt, idx, src, axis=0):
    return tgt.at[idx].add(src)

def _segment_sum(src, seg, n):
    return jax.ops.segment_sum(src, seg, n)
kernel_name = 'mk_perceiver_d2_seqx_r8_2aa58b'

def setup_inputs(seed: int=0):
    np.random.seed(seed)
    _w = jnp.asarray

    def _rec_inputs():
        import jax
        import jax.numpy as jnp
        _rk = jax.random.key(seed)
        x = -0.0005207 + 1.001 * jax.random.normal(jax.random.fold_in(_rk, 1), (8, 32, 512), jnp.float32)
        _lenS = 32 - jax.random.randint(jax.random.fold_in(_rk, 7), (8,), 0, max(1, 32 // 4) + 1, jnp.int32)
        _lenS2 = 512 - jax.random.randint(jax.random.fold_in(_rk, 8), (8,), 0, max(1, 512 // 4) + 1, jnp.int32)
        _ctx_4096P = jax.random.normal(jax.random.fold_in(_rk, 11), (8, 16, 512), jnp.float32)
        _ctx_4096c = jax.random.dirichlet(jax.random.fold_in(_rk, 511), 0.3 * jnp.ones((16,), jnp.float32), (8, 512))
        _ctx_4096t = jnp.einsum('bsk,bkd->bsd', _ctx_4096c, _ctx_4096P)
        _ctx_4096t = _ctx_4096t * jax.lax.rsqrt(jnp.mean(jnp.square(_ctx_4096t)) + 1e-12) * 0.953939
        ctx_4096 = -0.00010331 + 0.999899 * (_ctx_4096t + 0.3 * jax.random.normal(jax.random.fold_in(_rk, 611), (8, 512, 512), jnp.float32))
        _validS = jnp.arange(32)[None, :] < _lenS[:, None]
        _validS2 = jnp.arange(512)[None, :] < _lenS2[:, None]
        _causal = jnp.tril(jnp.ones((32, 32), dtype=bool))
        mask_1x1xSxS2_ff0 = jnp.where(jnp.ones((1, 1, 32, 512), dtype=bool), 0.0, -1000000000.0).astype(jnp.float32)
        return (x, ctx_4096, mask_1x1xSxS2_ff0)
    x, ctx_4096, mask_1x1xSxS2_ff0 = _rec_inputs()

    def _L0_xattn_setup():
        import jax, jax.numpy as jnp
        import numpy as np
        HEADS = 32
        KV_HEADS = 8
        HEAD_DIM = 128
        EPS = 1e-06

        def rms_norm(x, w):
            var = jnp.mean(jnp.square(x.astype(jnp.float32)), axis=-1, keepdims=True)
            return (x.astype(jnp.float32) * jax.lax.rsqrt(var + EPS)).astype(x.dtype) * w
        key = jax.random.key(seed)
        ks = jax.random.split(key, 6)
        bsz, n_lat, seq, hidden = (8, 64, 512, 512)
        return {'latents': jax.random.normal(ks[0], (bsz, n_lat, hidden), jnp.float32), 'context': jax.random.normal(ks[1], (bsz, seq, hidden), jnp.float32), 'Wq': jax.random.normal(ks[2], (hidden, HEADS * HEAD_DIM), jnp.float32) * 0.02, 'Wk': jax.random.normal(ks[3], (hidden, KV_HEADS * HEAD_DIM), jnp.float32) * 0.02, 'Wv': jax.random.normal(ks[4], (hidden, KV_HEADS * HEAD_DIM), jnp.float32) * 0.02, 'Wo': jax.random.normal(ks[5], (HEADS * HEAD_DIM, hidden), jnp.float32) * 0.02, 'q_norm_w': jnp.ones((HEAD_DIM,), jnp.float32), 'k_norm_w': jnp.ones((HEAD_DIM,), jnp.float32)}
    _L0_xattn_all = _L0_xattn_setup()
    _L0_xattn_in = {k: v for k, v in _L0_xattn_all.items() if k in ('Wq', 'Wk', 'Wv', 'Wo', 'q_norm_w', 'k_norm_w')}
    del _L0_xattn_all

    def _L0_attn_setup():
        import jax, jax.numpy as jnp
        import numpy as np
        B, T, H, S, F, G = (2, 256, 512, 128, 1248, 6)
        GRAD_ORDER_MIN = 4
        THD = 2.5
        key = jax.random.key(seed)
        ks = jax.random.split(key, 9)
        sc = 0.02
        hidden_states = jax.random.normal(ks[0], (B, T, H), jnp.float32)
        up_w = jax.random.normal(ks[1], (S, H), jnp.float32) * sc
        gate_w = jax.random.normal(ks[2], (S, H), jnp.float32) / np.sqrt(H)
        local_point = jax.random.normal(ks[3], (S,), jnp.float32)
        local_approx_output = jax.random.normal(ks[4], (H, S), jnp.float32) * sc
        fuse_weight = jax.random.normal(ks[5], (H, S, G), jnp.float32) * sc
        discount_factor = jnp.asarray(np.cumsum(np.log(np.arange(1, G + 1, dtype=np.float64))), jnp.float32)
        ffn_gate_w = jax.random.normal(ks[6], (F, H), jnp.float32) * sc
        ffn_up_w = jax.random.normal(ks[7], (F, H), jnp.float32) * sc
        ffn_down_w = jax.random.normal(ks[8], (H, F), jnp.float32) * sc
        return {'hidden_states': hidden_states, 'up_w': up_w, 'gate_w': gate_w, 'local_point': local_point, 'local_approx_output': local_approx_output, 'fuse_weight': fuse_weight, 'discount_factor': discount_factor, 'ffn_gate_w': ffn_gate_w, 'ffn_up_w': ffn_up_w, 'ffn_down_w': ffn_down_w}
    _L0_attn_all = _L0_attn_setup()
    _L0_attn_in = {k: v for k, v in _L0_attn_all.items() if k in ('up_w', 'gate_w', 'local_point', 'local_approx_output', 'fuse_weight', 'discount_factor', 'ffn_gate_w', 'ffn_up_w', 'ffn_down_w')}
    del _L0_attn_all

    def _L0_ffn_setup():
        import jax, jax.numpy as jnp
        import numpy as np
        LORA_SCALING = 1.0 / 2.0

        def _qlora_linear(x, wq, A, B):
            w = jnp.tile(wq, (1, 4))
            base = x @ w.T
            lora = x @ A.T @ B.T
            return base + lora * LORA_SCALING
        key = jax.random.key(seed)
        ks = jax.random.split(key, 10)
        d, h, r = (512, 1376, 2)
        return {'x': jax.random.normal(ks[0], (16, 1, d), dtype=jnp.float32), 'w1q': jax.random.normal(ks[1], (h, d // 4), dtype=jnp.float32) * 0.02, 'a1': jax.random.normal(ks[2], (r, d), dtype=jnp.float32) * 0.02, 'b1': jax.random.normal(ks[3], (h, r), dtype=jnp.float32) * 0.02, 'w3q': jax.random.normal(ks[4], (h, d // 4), dtype=jnp.float32) * 0.02, 'a3': jax.random.normal(ks[5], (r, d), dtype=jnp.float32) * 0.02, 'b3': jax.random.normal(ks[6], (h, r), dtype=jnp.float32) * 0.02, 'w2q': jax.random.normal(ks[7], (d, h // 4), dtype=jnp.float32) * 0.02, 'a2': jax.random.normal(ks[8], (r, h), dtype=jnp.float32) * 0.02, 'b2': jax.random.normal(ks[9], (d, r), dtype=jnp.float32) * 0.02}
    _L0_ffn_all = _L0_ffn_setup()
    _L0_ffn_in = {k: v for k, v in _L0_ffn_all.items() if k in ('w1q', 'a1', 'b1', 'w3q', 'a3', 'b3', 'w2q', 'a2', 'b2')}
    del _L0_ffn_all

    def _L1_xattn_setup():
        import jax, jax.numpy as jnp
        import numpy as np
        B, Q, K, D = (1, 128, 6404, 512)
        H, KVH, HD = (32, 8, 128)
        GROUPS = H // KVH
        EPS = 1e-05

        def _rmsnorm(x, w):
            xf = x.astype(jnp.float32)
            var = jnp.mean(xf * xf, axis=-1, keepdims=True)
            return (xf * jax.lax.rsqrt(var + EPS)).astype(x.dtype) * w
        key = jax.random.key(seed)
        ks = jax.random.split(key, 8)
        s = 0.02
        return {'hidden_states': jax.random.normal(ks[0], (B, Q, D), jnp.float32), 'cross_attention_states': jax.random.normal(ks[1], (B, K, D), jnp.float32), 'attention_mask': jnp.zeros((B, 1, Q, K), jnp.float32), 'Wq': jax.random.normal(ks[2], (H * HD, D), jnp.float32) * s, 'Wk': jax.random.normal(ks[3], (KVH * HD, D), jnp.float32) * s, 'Wv': jax.random.normal(ks[4], (KVH * HD, D), jnp.float32) * s, 'Wo': jax.random.normal(ks[5], (D, H * HD), jnp.float32) * s, 'q_norm_w': jnp.ones((HD,), jnp.float32), 'k_norm_w': jnp.ones((HD,), jnp.float32)}
    _L1_xattn_all = _L1_xattn_setup()
    _L1_xattn_in = {k: v for k, v in _L1_xattn_all.items() if k in ('Wq', 'Wk', 'Wv', 'Wo', 'q_norm_w', 'k_norm_w')}
    del _L1_xattn_all

    def _L1_attn_setup():
        import math
        import jax, jax.numpy as jnp
        import numpy as np
        B, T, E = (2, 256, 512)
        H, HKV = (32, 8)
        DH = E // H
        G = H // HKV
        ROPE_THETA = 500000.0
        ROPE_FACTOR = 32.0
        HI_FREQ_FACTOR = 4.0
        LO_FREQ_FACTOR = 1.0
        ORIG_CTX = 1024

        def _rope_cos_sin(t_len):
            inv_freq = 1.0 / ROPE_THETA ** (jnp.arange(0, DH, 2, dtype=jnp.float32) / DH)
            wavelen = 2.0 * math.pi / inv_freq
            cut_lo = ORIG_CTX / HI_FREQ_FACTOR
            cut_hi = ORIG_CTX / LO_FREQ_FACTOR
            inv_freq = jnp.where(wavelen > cut_hi, inv_freq / ROPE_FACTOR, inv_freq)
            smooth = (ORIG_CTX / wavelen - LO_FREQ_FACTOR) / (HI_FREQ_FACTOR - LO_FREQ_FACTOR)
            smoothed = (1.0 - smooth) * inv_freq / ROPE_FACTOR + smooth * inv_freq
            is_medium = ~(wavelen < cut_hi) & ~(wavelen > cut_lo)
            inv_freq = jnp.where(is_medium, smoothed, inv_freq)
            pos = jnp.arange(t_len, dtype=jnp.float32)
            freqs = pos[:, None] * inv_freq[None, :]
            emb = jnp.concatenate([freqs, freqs], axis=-1)
            return (jnp.cos(emb), jnp.sin(emb))

        def _rotate_half(x):
            x1, x2 = jnp.split(x, 2, axis=-1)
            return jnp.concatenate([-x2, x1], axis=-1)
        key = jax.random.key(seed)
        kx, kq, kk, kv, ko = jax.random.split(key, 5)
        w = lambda k, shape: jax.random.normal(k, shape, jnp.float32) * 0.02
        return {'x': jax.random.normal(kx, (B, T, E), jnp.float32), 'Wq': w(kq, (E, E)), 'Wk': w(kk, (HKV * DH, E)), 'Wv': w(kv, (HKV * DH, E)), 'Wo': w(ko, (E, E))}
    _L1_attn_all = _L1_attn_setup()
    _L1_attn_in = {k: v for k, v in _L1_attn_all.items() if k in ('Wq', 'Wk', 'Wv', 'Wo')}
    del _L1_attn_all

    def _L1_ffn_setup():
        import jax, jax.numpy as jnp
        import numpy as np
        HIDDEN = 512
        MOE_INTER = 128
        SHARED_INTER = 512
        NUM_EXPERTS = 16
        TOP_K = 2

        def _moe_forward(x, gate_w, w_gate_up, w_down, shared_w_gate_up, shared_w_down):
            orig_shape = x.shape
            x2 = x.reshape(-1, orig_shape[-1])
            gu_s = x2 @ shared_w_gate_up.T
            g_s, u_s = jnp.split(gu_s, 2, axis=-1)
            shared_out = jax.nn.silu(g_s) * u_s @ shared_w_down.T
            logits = x2 @ gate_w.T
            probs = jax.nn.softmax(logits, axis=-1)
            topk_vals, topk_idx = jax.lax.top_k(probs, TOP_K)
            topk_vals = topk_vals / jnp.sum(topk_vals, axis=-1, keepdims=True)
            combine = jnp.sum(jax.nn.one_hot(topk_idx, NUM_EXPERTS, dtype=x2.dtype) * topk_vals[..., None], axis=1)
            gu = jnp.einsum('th,eih->eti', x2, w_gate_up)
            g, u = jnp.split(gu, 2, axis=-1)
            act = jax.nn.silu(g) * u
            out_e = jnp.einsum('eti,ehi->eth', act, w_down)
            moe_out = jnp.einsum('eth,te->th', out_e, combine)
            return (moe_out + shared_out).reshape(orig_shape)
        key = jax.random.key(seed)
        ks = jax.random.split(key, 6)
        s = 0.02
        hidden_states = jax.random.normal(ks[0], (2, 256, HIDDEN), dtype=jnp.float32)
        gate_w = jax.random.normal(ks[1], (NUM_EXPERTS, HIDDEN), dtype=jnp.float32) * s
        w_gate_up = jax.random.normal(ks[2], (NUM_EXPERTS, 2 * MOE_INTER, HIDDEN), dtype=jnp.float32) * s
        w_down = jax.random.normal(ks[3], (NUM_EXPERTS, HIDDEN, MOE_INTER), dtype=jnp.float32) * s
        shared_w_gate_up = jax.random.normal(ks[4], (2 * SHARED_INTER, HIDDEN), dtype=jnp.float32) * s
        shared_w_down = jax.random.normal(ks[5], (HIDDEN, SHARED_INTER), dtype=jnp.float32) * s
        return {'hidden_states': hidden_states, 'gate_w': gate_w, 'w_gate_up': w_gate_up, 'w_down': w_down, 'shared_w_gate_up': shared_w_gate_up, 'shared_w_down': shared_w_down}
    _L1_ffn_all = _L1_ffn_setup()
    _L1_ffn_in = {k: v for k, v in _L1_ffn_all.items() if k in ('gate_w', 'w_gate_up', 'w_down', 'shared_w_gate_up', 'shared_w_down')}
    del _L1_ffn_all
    return {'x': x, 'ctx_4096': ctx_4096, 'mask_1x1xSxS2_ff0': mask_1x1xSxS2_ff0, 'L0_xattn_Wq': _L0_xattn_in['Wq'], 'L0_xattn_Wk': _L0_xattn_in['Wk'], 'L0_xattn_Wv': _L0_xattn_in['Wv'], 'L0_xattn_Wo': _L0_xattn_in['Wo'], 'L0_xattn_q_norm_w': _L0_xattn_in['q_norm_w'], 'L0_xattn_k_norm_w': _L0_xattn_in['k_norm_w'], 'L0_attn_up_w': _L0_attn_in['up_w'], 'L0_attn_gate_w': _L0_attn_in['gate_w'], 'L0_attn_local_point': _L0_attn_in['local_point'], 'L0_attn_local_approx_output': _L0_attn_in['local_approx_output'], 'L0_attn_fuse_weight': _L0_attn_in['fuse_weight'], 'L0_attn_discount_factor': _L0_attn_in['discount_factor'], 'L0_attn_ffn_gate_w': _L0_attn_in['ffn_gate_w'], 'L0_attn_ffn_up_w': _L0_attn_in['ffn_up_w'], 'L0_attn_ffn_down_w': _L0_attn_in['ffn_down_w'], 'L0_ffn_w1q': _L0_ffn_in['w1q'], 'L0_ffn_a1': _L0_ffn_in['a1'], 'L0_ffn_b1': _L0_ffn_in['b1'], 'L0_ffn_w3q': _L0_ffn_in['w3q'], 'L0_ffn_a3': _L0_ffn_in['a3'], 'L0_ffn_b3': _L0_ffn_in['b3'], 'L0_ffn_w2q': _L0_ffn_in['w2q'], 'L0_ffn_a2': _L0_ffn_in['a2'], 'L0_ffn_b2': _L0_ffn_in['b2'], 'L1_xattn_Wq': _L1_xattn_in['Wq'], 'L1_xattn_Wk': _L1_xattn_in['Wk'], 'L1_xattn_Wv': _L1_xattn_in['Wv'], 'L1_xattn_Wo': _L1_xattn_in['Wo'], 'L1_xattn_q_norm_w': _L1_xattn_in['q_norm_w'], 'L1_xattn_k_norm_w': _L1_xattn_in['k_norm_w'], 'L1_attn_Wq': _L1_attn_in['Wq'], 'L1_attn_Wk': _L1_attn_in['Wk'], 'L1_attn_Wv': _L1_attn_in['Wv'], 'L1_attn_Wo': _L1_attn_in['Wo'], 'L1_ffn_gate_w': _L1_ffn_in['gate_w'], 'L1_ffn_w_gate_up': _L1_ffn_in['w_gate_up'], 'L1_ffn_w_down': _L1_ffn_in['w_down'], 'L1_ffn_shared_w_gate_up': _L1_ffn_in['shared_w_gate_up'], 'L1_ffn_shared_w_down': _L1_ffn_in['shared_w_down']}

def reference(x, ctx_4096, mask_1x1xSxS2_ff0, L0_xattn_Wq, L0_xattn_Wk, L0_xattn_Wv, L0_xattn_Wo, L0_xattn_q_norm_w, L0_xattn_k_norm_w, L0_attn_up_w, L0_attn_gate_w, L0_attn_local_point, L0_attn_local_approx_output, L0_attn_fuse_weight, L0_attn_discount_factor, L0_attn_ffn_gate_w, L0_attn_ffn_up_w, L0_attn_ffn_down_w, L0_ffn_w1q, L0_ffn_a1, L0_ffn_b1, L0_ffn_w3q, L0_ffn_a3, L0_ffn_b3, L0_ffn_w2q, L0_ffn_a2, L0_ffn_b2, L1_xattn_Wq, L1_xattn_Wk, L1_xattn_Wv, L1_xattn_Wo, L1_xattn_q_norm_w, L1_xattn_k_norm_w, L1_attn_Wq, L1_attn_Wk, L1_attn_Wv, L1_attn_Wo, L1_ffn_gate_w, L1_ffn_w_gate_up, L1_ffn_w_down, L1_ffn_shared_w_gate_up, L1_ffn_shared_w_down):
    import jax
    import jax.numpy as jnp

    def _L0_xattn_ref(latents, context, Wq, Wk, Wv, Wo, q_norm_w, k_norm_w):
        import jax, jax.numpy as jnp
        import numpy as np
        HEADS = 32
        KV_HEADS = 8
        HEAD_DIM = 128
        EPS = 1e-06

        def rms_norm(x, w):
            var = jnp.mean(jnp.square(x.astype(jnp.float32)), axis=-1, keepdims=True)
            return (x.astype(jnp.float32) * jax.lax.rsqrt(var + EPS)).astype(x.dtype) * w
        bsz, q_len, hidden = latents.shape
        kv = jnp.concatenate([context, latents], axis=1)
        kv_len = kv.shape[1]
        groups = HEADS // KV_HEADS
        q = (latents @ Wq).reshape(bsz, q_len, HEADS, HEAD_DIM).transpose(0, 2, 1, 3)
        k = (kv @ Wk).reshape(bsz, kv_len, KV_HEADS, HEAD_DIM).transpose(0, 2, 1, 3)
        v = (kv @ Wv).reshape(bsz, kv_len, KV_HEADS, HEAD_DIM).transpose(0, 2, 1, 3)
        q = rms_norm(q, q_norm_w)
        k = rms_norm(k, k_norm_w)
        qg = q.reshape(bsz, KV_HEADS, groups, q_len, HEAD_DIM)
        scale = 1.0 / np.sqrt(HEAD_DIM)
        scores = jnp.einsum('bhgqd,bhkd->bhgqk', qg, k) * scale
        probs = jax.nn.softmax(scores.astype(jnp.float32), axis=-1).astype(q.dtype)
        out = jnp.einsum('bhgqk,bhkd->bhgqd', probs, v)
        out = out.reshape(bsz, HEADS, q_len, HEAD_DIM).transpose(0, 2, 1, 3)
        out = out.reshape(bsz, q_len, HEADS * HEAD_DIM)
        return out @ Wo

    def _L0_attn_ref(hidden_states, up_w, gate_w, local_point, local_approx_output, fuse_weight, discount_factor, ffn_gate_w, ffn_up_w, ffn_down_w):
        import jax, jax.numpy as jnp
        import numpy as np
        B, T, H, S, F, G = (2, 256, 512, 128, 1248, 6)
        GRAD_ORDER_MIN = 4
        THD = 2.5
        approx_up = hidden_states @ up_w.T
        gate_pre = hidden_states @ gate_w.T
        delta = gate_pre - local_point
        neg_factor = jnp.where(delta > 0, 1.0, -1.0).astype(hidden_states.dtype)
        delta_abs = jnp.abs(delta)
        log_delta = jnp.log(delta_abs)
        keep = (delta_abs <= THD).astype(hidden_states.dtype)
        approx_out = approx_up @ local_approx_output.T
        for idx in range(G):
            m = idx + 1
            dterm = jnp.exp(log_delta * m - discount_factor[idx])
            if m % 2 == 1:
                dterm = dterm * neg_factor
            tmp = dterm * approx_up
            if m > GRAD_ORDER_MIN:
                tmp = tmp * keep
            approx_out = approx_out + tmp @ fuse_weight[:, :, idx].T
        ffn_out = jax.nn.silu(hidden_states @ ffn_gate_w.T) * (hidden_states @ ffn_up_w.T) @ ffn_down_w.T
        return approx_out + ffn_out

    def _L0_ffn_ref(x, w1q, a1, b1, w3q, a3, b3, w2q, a2, b2):
        import jax, jax.numpy as jnp
        import numpy as np
        LORA_SCALING = 1.0 / 2.0

        def _qlora_linear(x, wq, A, B):
            w = jnp.tile(wq, (1, 4))
            base = x @ w.T
            lora = x @ A.T @ B.T
            return base + lora * LORA_SCALING
        gate = jax.nn.silu(_qlora_linear(x, w1q, a1, b1))
        up = _qlora_linear(x, w3q, a3, b3)
        return _qlora_linear(gate * up, w2q, a2, b2)

    def _L1_xattn_ref(hidden_states, cross_attention_states, attention_mask, Wq, Wk, Wv, Wo, q_norm_w, k_norm_w):
        import jax, jax.numpy as jnp
        import numpy as np
        B, Q, K, D = (1, 128, 6404, 512)
        H, KVH, HD = (32, 8, 128)
        GROUPS = H // KVH
        EPS = 1e-05

        def _rmsnorm(x, w):
            xf = x.astype(jnp.float32)
            var = jnp.mean(xf * xf, axis=-1, keepdims=True)
            return (xf * jax.lax.rsqrt(var + EPS)).astype(x.dtype) * w
        bsz, q_len, _ = hidden_states.shape
        kv_len = cross_attention_states.shape[1]
        q = (hidden_states @ Wq.T).reshape(bsz, q_len, H, HD).transpose(0, 2, 1, 3)
        k = (cross_attention_states @ Wk.T).reshape(bsz, kv_len, KVH, HD).transpose(0, 2, 1, 3)
        v = (cross_attention_states @ Wv.T).reshape(bsz, kv_len, KVH, HD).transpose(0, 2, 1, 3)
        q = _rmsnorm(q, q_norm_w)
        k = jnp.repeat(k, GROUPS, axis=1)
        v = jnp.repeat(v, GROUPS, axis=1)
        k = _rmsnorm(k, k_norm_w)
        scale = 1.0 / np.sqrt(HD)
        scores = jnp.einsum('bhqd,bhkd->bhqk', q, k) * scale
        scores = scores + attention_mask[:, :, :, :kv_len]
        probs = jax.nn.softmax(scores.astype(jnp.float32), axis=-1).astype(q.dtype)
        out = jnp.einsum('bhqk,bhkd->bhqd', probs, v)
        out = out.transpose(0, 2, 1, 3).reshape(bsz, q_len, H * HD)
        return out @ Wo.T

    def _L1_attn_ref(x, Wq, Wk, Wv, Wo):
        import math
        import jax, jax.numpy as jnp
        import numpy as np
        B, T, E = (2, 256, 512)
        H, HKV = (32, 8)
        DH = E // H
        G = H // HKV
        ROPE_THETA = 500000.0
        ROPE_FACTOR = 32.0
        HI_FREQ_FACTOR = 4.0
        LO_FREQ_FACTOR = 1.0
        ORIG_CTX = 1024

        def _rope_cos_sin(t_len):
            inv_freq = 1.0 / ROPE_THETA ** (jnp.arange(0, DH, 2, dtype=jnp.float32) / DH)
            wavelen = 2.0 * math.pi / inv_freq
            cut_lo = ORIG_CTX / HI_FREQ_FACTOR
            cut_hi = ORIG_CTX / LO_FREQ_FACTOR
            inv_freq = jnp.where(wavelen > cut_hi, inv_freq / ROPE_FACTOR, inv_freq)
            smooth = (ORIG_CTX / wavelen - LO_FREQ_FACTOR) / (HI_FREQ_FACTOR - LO_FREQ_FACTOR)
            smoothed = (1.0 - smooth) * inv_freq / ROPE_FACTOR + smooth * inv_freq
            is_medium = ~(wavelen < cut_hi) & ~(wavelen > cut_lo)
            inv_freq = jnp.where(is_medium, smoothed, inv_freq)
            pos = jnp.arange(t_len, dtype=jnp.float32)
            freqs = pos[:, None] * inv_freq[None, :]
            emb = jnp.concatenate([freqs, freqs], axis=-1)
            return (jnp.cos(emb), jnp.sin(emb))

        def _rotate_half(x):
            x1, x2 = jnp.split(x, 2, axis=-1)
            return jnp.concatenate([-x2, x1], axis=-1)
        b, t, _ = x.shape
        q = (x @ Wq.T).reshape(b, t, H, DH).transpose(0, 2, 1, 3)
        k = (x @ Wk.T).reshape(b, t, HKV, DH).transpose(0, 2, 1, 3)
        v = (x @ Wv.T).reshape(b, t, HKV, DH).transpose(0, 2, 1, 3)
        cos, sin = _rope_cos_sin(t)
        cos = cos.astype(x.dtype)[None, None]
        sin = sin.astype(x.dtype)[None, None]
        q = q * cos + _rotate_half(q) * sin
        k = k * cos + _rotate_half(k) * sin
        qg = q.reshape(b, HKV, G, t, DH)
        scores = jnp.einsum('bhgtd,bhkd->bhgtk', qg.astype(jnp.float32), k.astype(jnp.float32)) / math.sqrt(DH)
        causal = jnp.tril(jnp.ones((t, t), dtype=bool))
        scores = jnp.where(causal[None, None, None], scores, jnp.finfo(jnp.float32).min)
        attn = jax.nn.softmax(scores, axis=-1).astype(x.dtype)
        ctx = jnp.einsum('bhgtk,bhkd->bhgtd', attn, v)
        out = ctx.reshape(b, H, t, DH).transpose(0, 2, 1, 3).reshape(b, t, E)
        return out @ Wo.T

    def _L1_ffn_ref(hidden_states, gate_w, w_gate_up, w_down, shared_w_gate_up, shared_w_down):
        import jax, jax.numpy as jnp
        import numpy as np
        HIDDEN = 512
        MOE_INTER = 128
        SHARED_INTER = 512
        NUM_EXPERTS = 16
        TOP_K = 2

        def _moe_forward(x, gate_w, w_gate_up, w_down, shared_w_gate_up, shared_w_down):
            orig_shape = x.shape
            x2 = x.reshape(-1, orig_shape[-1])
            gu_s = x2 @ shared_w_gate_up.T
            g_s, u_s = jnp.split(gu_s, 2, axis=-1)
            shared_out = jax.nn.silu(g_s) * u_s @ shared_w_down.T
            logits = x2 @ gate_w.T
            probs = jax.nn.softmax(logits, axis=-1)
            topk_vals, topk_idx = jax.lax.top_k(probs, TOP_K)
            topk_vals = topk_vals / jnp.sum(topk_vals, axis=-1, keepdims=True)
            combine = jnp.sum(jax.nn.one_hot(topk_idx, NUM_EXPERTS, dtype=x2.dtype) * topk_vals[..., None], axis=1)
            gu = jnp.einsum('th,eih->eti', x2, w_gate_up)
            g, u = jnp.split(gu, 2, axis=-1)
            act = jax.nn.silu(g) * u
            out_e = jnp.einsum('eti,ehi->eth', act, w_down)
            moe_out = jnp.einsum('eth,te->th', out_e, combine)
            return (moe_out + shared_out).reshape(orig_shape)
        return _moe_forward(hidden_states, gate_w, w_gate_up, w_down, shared_w_gate_up, shared_w_down)
    x = x + _L0_xattn_ref(_layernorm(x, axis=-1), ctx_4096, L0_xattn_Wq, L0_xattn_Wk, L0_xattn_Wv, L0_xattn_Wo, L0_xattn_q_norm_w, L0_xattn_k_norm_w)
    x = x + _L0_attn_ref(_layernorm(x, axis=-1), L0_attn_up_w, L0_attn_gate_w, L0_attn_local_point, L0_attn_local_approx_output, L0_attn_fuse_weight, L0_attn_discount_factor, L0_attn_ffn_gate_w, L0_attn_ffn_up_w, L0_attn_ffn_down_w)
    x = x + _L0_ffn_ref(_layernorm(x, axis=-1), L0_ffn_w1q, L0_ffn_a1, L0_ffn_b1, L0_ffn_w3q, L0_ffn_a3, L0_ffn_b3, L0_ffn_w2q, L0_ffn_a2, L0_ffn_b2)
    x = x + _L1_xattn_ref(_layernorm(x, axis=-1), ctx_4096, mask_1x1xSxS2_ff0, L1_xattn_Wq, L1_xattn_Wk, L1_xattn_Wv, L1_xattn_Wo, L1_xattn_q_norm_w, L1_xattn_k_norm_w)
    x = x + _L1_attn_ref(_layernorm(x, axis=-1), L1_attn_Wq, L1_attn_Wk, L1_attn_Wv, L1_attn_Wo)
    x = x + _L1_ffn_ref(_layernorm(x, axis=-1), L1_ffn_gate_w, L1_ffn_w_gate_up, L1_ffn_w_down, L1_ffn_shared_w_gate_up, L1_ffn_shared_w_down)
    return x

_drawn_inputs = setup_inputs


def setup_inputs(seed=0):
    import zlib

    import numpy as np

    out = dict(_drawn_inputs(seed))
    spreads = {'L0_xattn_q_norm_w': (1.0, 0.6),
     'L0_xattn_k_norm_w': (1.0, 0.6),
     'L1_xattn_q_norm_w': (1.0, 0.6),
     'L1_xattn_k_norm_w': (1.0, 0.6)}
    factors = {'L0_ffn_a1': 8.0,
     'L0_ffn_b1': 8.0,
     'L0_ffn_a3': 8.0,
     'L0_ffn_b3': 8.0,
     'L0_ffn_a2': 8.0,
     'L0_ffn_b2': 8.0,
     'L1_attn_Wq': 5.713,
     'L1_attn_Wk': 4.981,
     'L1_ffn_gate_w': 4.109,
     'L1_ffn_w_gate_up': 3.793,
     'L1_ffn_w_down': 3.824}
    for name, (base, spread) in spreads.items():
        noise = np.random.default_rng([zlib.crc32(name.encode()), seed]).standard_normal(out[name].shape)
        drawn = base * np.exp(spread * noise) if base else spread * noise
        out[name] = jnp.asarray(drawn.astype(out[name].dtype))
    for name, factor in factors.items():
        out[name] = (out[name] * factor).astype(out[name].dtype)
    return out
```

```python
from contextlib import ExitStack

import numpy as np

import concourse.bass as bass
from concourse import mybir

ALU = mybir.AluOpType
ACT = mybir.ActivationFunctionType
AX = mybir.AxisListType
F32 = mybir.dt.float32
F32R = mybir.dt.float32r

P = 128
B, SEQ, D = 8, 32, 512
TOK = B * SEQ
TT = TOK // P
BT = P // SEQ
DC = D // P
CTX = 512
CT = CTX // P
HEADS, KVH, HD = 32, 8, 128
GROUP = HEADS // KVH
UNIT_H = 4
UNITS = B * KVH // UNIT_H
UW = UNIT_H * HD
TAYLOR = 6
TAYLOR_MIN, TAYLOR_KEEP = 4, 2.5
EPS_LN = 1e-5


def need(eng, sem, value):
    if isinstance(value, int) and value <= 0:
        return
    eng.wait_ge(sem, value)


def mm3(nc, out, a, b, start, stop):
    nc.tensor.matmul(out, a[0], b[1], start=start, stop=False)
    nc.tensor.matmul(out, a[0], b[0], start=False, stop=False)
    return nc.tensor.matmul(out, a[1], b[0], start=False, stop=stop)


def as_f32(ap):
    return ap.bitcast(F32)


SEMAPHORES = []


def clear_semaphores(nc):
    with nc.Block() as block:
        @block.gpsimd
        def _(pool):
            nc.clear_and_free_semaphores(list(SEMAPHORES))
    SEMAPHORES.clear()


class Space:

    def __init__(self, nc, ctx, tag):
        self.nc, self.ctx, self.tag = nc, ctx, tag

    def sb(self, name, shape, dt=F32):
        return self.ctx.enter_context(self.nc.sbuf_tensor(f"{self.tag}_{name}", shape, dt))

    def pair(self, name, shape):
        return self.sb(name + "_hi", shape, F32R), self.sb(name + "_lo", shape, F32R)

    def ps(self, name, banks=1):
        return self.ctx.enter_context(self.nc.psum_tensor(f"{self.tag}_{name}", [P, 512 * banks], F32))

    def sem(self, name):
        sem = self.nc.alloc_semaphore(f"{self.tag}_{name}")
        SEMAPHORES.append(sem)
        return sem


class LayerNormT:

    def __init__(self, nc, s, x, ident, xT, banks):
        self.nc, self.x, self.ident, self.xT, self.banks = nc, x, ident, xT, banks
        self.stats = s.sb("ln_stats", [P, TT, 6])
        self.mv = s.sb("ln_mv", [P, TT, 2])
        self.rstd = s.sb("ln_rstd", [P, TT, 3])
        self.xn = s.sb("ln_xn", [P, TT, D])
        self.stats_done = s.sem("ln_stats_done")
        self.mv_done = s.sem("ln_mv_done")
        self.eps_added = s.sem("ln_eps_added")
        self.rstd_done = s.sem("ln_rstd_done")
        self.normed = s.sem("ln_normed")
        self.transposed = s.sem("ln_transposed")
        self.hi_ready = s.sem("ln_hi_ready")
        self.lo_ready = s.sem("ln_lo_ready")

    def vector(self, dve):
        nc = self.nc
        for t in range(TT):
            nc.vector.bn_stats(self.stats[:, t, :], self.x[:, t, :]).then_inc(self.stats_done, 1)
        for t in range(TT):
            dve.wait_ge(self.stats_done, t + 1)
            nc.vector.bn_aggr(self.mv[:, t, :], self.stats[:, t, :]).then_inc(self.mv_done, 1)
        dve.wait_ge(self.rstd_done, 1)
        for t in range(TT):
            nc.vector.tensor_scalar(self.xn[:, t, :], self.x[:, t, :], self.mv[:, t, 0:1],
                                    self.rstd[:, t, 1:2], ALU.subtract, ALU.mult).then_inc(self.normed, 1)
        for t in range(TT):
            dve.wait_ge(self.hi_ready, t + 1)
            nc.vector.tensor_tensor(self.xT[1][:, :, t * P:(t + 1) * P],
                                    self.banks[t][:, :].rearrange("p (c k) -> p c k", c=DC),
                                    as_f32(self.xT[0][:, :, t * P:(t + 1) * P]),
                                    ALU.subtract).then_inc(self.lo_ready, 1)

    def gpsimd(self, pool):
        nc = self.nc
        nc.gpsimd.memset(self.rstd[:, :, 2:3], -0.5).then_inc(self.eps_added, 1)
        pool.wait_ge(self.mv_done, TT)
        nc.gpsimd.tensor_scalar(self.rstd[:, :, 0:1], self.mv[:, :, 1:2], EPS_LN, None,
                                ALU.add).then_inc(self.eps_added, 1)
        pool.wait_ge(self.eps_added, 2)
        nc.gpsimd.tensor_tensor(self.rstd[:, :, 1:2], self.rstd[:, :, 0:1], self.rstd[:, :, 2:3],
                                ALU.pow).then_inc(self.rstd_done, 1)

    def tensor(self, pe):
        for t in range(TT):
            pe.wait_ge(self.normed, t + 1)
            for c in range(DC):
                last = self.nc.tensor.transpose(self.banks[t][:, c * P:(c + 1) * P],
                                                self.xn[:, t, c * P:(c + 1) * P], self.ident[:])
            last.then_inc(self.transposed, 1)

    def scalar(self, act):
        for t in range(TT):
            act.wait_ge(self.transposed, t + 1)
            self.nc.scalar.activation(self.xT[0][:, :, t * P:(t + 1) * P],
                                      self.banks[t][:, :].rearrange("p (c k) -> p c k", c=DC),
                                      ACT.Copy).then_inc(self.hi_ready, 1)

    def wait_ready(self, pe):
        pe.wait_ge(self.lo_ready, TT)


class WeightStream:

    def __init__(self, nc, s, name, width, stage=None, split=None):
        self.nc, self.width = nc, width
        self.stage = stage if stage is not None else s.sb(name + "_stage", [P, 2, width])
        self.split = split if split is not None else s.pair(name, [P, 2, width])
        self.loaded = [s.sem(f"{name}_loaded{i}") for i in range(2)]
        self.hi_ready = s.sem(name + "_hi_ready")
        self.lo_ready = s.sem(name + "_lo_ready")

    def load(self, sp, src, pair, slot):
        need(sp, self.lo_ready, 2 * pair + slot - 1)
        sp.dma_start(self.stage[:, slot, :], src).then_inc(self.loaded[slot], 16)

    def make_hi(self, act, pair, slot, used, per_tile, width=None):
        w = width or self.width
        act.wait_ge(self.loaded[slot], pair * 16 + 16)
        need(act, used, per_tile * (2 * pair + slot - 1))
        self.nc.scalar.activation(self.split[0][:, slot, :w], self.stage[:, slot, :w],
                                  ACT.Copy).then_inc(self.hi_ready, 1)

    def make_lo(self, dve, pair, slot, width=None):
        w = width or self.width
        dve.wait_ge(self.hi_ready, 2 * pair + slot + 1)
        self.nc.vector.tensor_tensor(self.split[1][:, slot, :w], self.stage[:, slot, :w],
                                     as_f32(self.split[0][:, slot, :w]),
                                     ALU.subtract).then_inc(self.lo_ready, 1)

    def wait_tile(self, pe, pair, slot):
        pe.wait_ge(self.lo_ready, 2 * pair + slot + 1)

    def tile(self, slot):
        return self.split[0][:, slot, :], self.split[1][:, slot, :]


def peeled(eng, count, step):
    step(0)
    with eng.Fori(1, count - 1) as i:
        step(i)
    step(count - 1)


def is_at(i, value):
    return isinstance(i, int) and i == value


def cross_attention(nc, tag, g, w, eps, latents_as_keys):
    latents = latents_as_keys
    with ExitStack() as outer:
        so = Space(nc, outer, tag)
        qT = so.sb("qT", [P, B, HEADS, SEQ])
        with ExitStack() as inner:
            si = Space(nc, inner, tag)
            wkv = si.pair("wkv", [P, 4, DC * UW])
            mask = si.sb("mask", [P, CTX]) if w["mask"] is not None else None
            klatT = si.sb("klatT", [P, KVH, TOK]) if latents else None
            vlat = si.sb("vlat", [SEQ, 2, UW]) if latents else None
            queries(nc, tag + "q", g, w, eps, wkv, qT, mask, klatT)
            attend(nc, tag + "a", g, w, eps, wkv, qT, mask, klatT, vlat)
        project_out(nc, tag + "o", g, w, qT)


def queries(nc, tag, g, w, eps, wkv, qT, mask, klatT):
    x, ident = g["x"], g["ident"]
    NQ = HEADS // UNIT_H
    NL = 2 * TT if klatT is not None else 0
    NN = NL + NQ * TT
    SLOTS, LAG = 4, 2
    with ExitStack() as ctx:
        s = Space(nc, ctx, tag)
        xT = s.pair("xT", [P, DC, TOK])
        tbank = [s.ps(f"tbank{i}") for i in range(2)]
        pbank = [s.ps(f"pbank{i}") for i in range(SLOTS)]
        ln = LayerNormT(nc, s, x, ident, xT, tbank)
        stream = WeightStream(nc, s, "w", DC * UW, stage=g["stage"])
        nk = s.sb("norm", [P, 4])
        sq = s.sb("sq", [P, 2, UW])
        ss = s.sb("ss", [P, SLOTS, UNIT_H])
        ms = s.sb("ms", [P, SLOTS, UNIT_H])
        rstd = s.sb("rstd", [P, SLOTS, UNIT_H])
        const = s.sb("const", [P, 2, UNIT_H])
        xn = s.sb("xn", [P, SLOTS, UW])
        vl = s.sb("vl", [P, TT, 2 * UW]) if klatT is not None else None

        small_loaded = s.sem("small_loaded")
        wkv_hi = s.sem("wkv_hi")
        wkv_lo = s.sem("wkv_lo")
        wkv_loaded = [s.sem(f"wkv_loaded{i}") for i in range(2)]
        const_set = s.sem("const_set")
        norm_ready = s.sem("norm_ready")
        projected = s.sem("projected")
        squared = s.sem("squared")
        summed = s.sem("summed")
        meaned = s.sem("meaned")
        rstd_ready = s.sem("rstd_ready")
        normed = s.sem("normed")
        transposed = s.sem("transposed")
        placed = s.sem("placed")
        vl_proj = s.sem("vl_proj")
        vl_ready = s.sem("vl_ready")
        vl_stored = s.sem("vl_stored")

        with nc.Block() as block:
            @block.sync
            def _(sp):
                sp.dma_start(nk[:, 0:2], w["norm"]).then_inc(small_loaded, 16)
                for i in range(4):
                    need(sp, wkv_lo, i - 1)
                    sp.dma_start(g["stage"][:, i % 2, :], w["wkv"][i]).then_inc(wkv_loaded[i % 2], 16)

                def step(i):
                    for slot in range(2):
                        if is_at(i, 0):
                            sp.wait_ge(wkv_lo, 3 + slot)
                        stream.load(sp, w["wq"][bass.ds(2 * i + slot, 1), :, :]
                                    .rearrange("a p n -> p (a n)"), i, slot)
                peeled(sp, NQ // 2, step)
                if vl is not None:
                    sp.wait_ge(vl_ready, 2 * TT)
                    sp.dma_start(g["vlat_dram"].rearrange("(t p) n -> p t n", p=P),
                                 vl[:]).then_inc(vl_stored, 16)
                    sp.wait_ge(vl_stored, 16)

            @block.gpsimd
            def _(pool):
                ln.gpsimd(pool)
                nc.gpsimd.memset(const[:, 0, :], -0.5).then_inc(const_set, 1)
                nc.gpsimd.memset(const[:, 1, :], eps).then_inc(const_set, 1)

                def rstd_of(n, k):
                    pool.wait_ge(const_set, 2)
                    pool.wait_ge(summed, n + 1)
                    nc.gpsimd.tensor_tensor(ms[:, k, :], ss[:, k, :], const[:, 1, :],
                                            ALU.add).then_inc(meaned, 1)
                    pool.wait_ge(meaned, n + 1)
                    nc.gpsimd.tensor_tensor(rstd[:, k, :], ms[:, k, :], const[:, 0, :],
                                            ALU.pow).then_inc(rstd_ready, 1)
                for n in range(NL):
                    rstd_of(n, n)
                peeled(pool, NQ // 2, lambda i: [rstd_of(NL + SLOTS * i + k, k) for k in range(SLOTS)])

            @block.tensor
            def _(pe):
                ln.tensor(pe)
                ln.wait_ready(pe)

                def project(t, wt, bank):
                    for c in range(DC):
                        a = tuple(h[:, c, t * P:(t + 1) * P] for h in xT)
                        last = mm3(nc, bank[:], a, tuple(h[:, c * UW:(c + 1) * UW] for h in wt),
                                   c == 0, c == DC - 1)
                    return last

                def transposes(n, k):
                    if isinstance(n, int) and n < 0:
                        return
                    pe.wait_ge(normed, n + 1)
                    need(pe, placed, n - 1)
                    for h in range(UNIT_H):
                        last = nc.tensor.transpose(tbank[k % 2][:, h * P:(h + 1) * P],
                                                   xn[:, k, h * P:(h + 1) * P], ident[:])
                    last.then_inc(transposed, 1)

                if vl is not None:
                    pe.wait_ge(wkv_lo, 4)
                    for i in range(2 * TT):
                        half, t = divmod(i, TT)
                        project(t, tuple(h[:, 2 + half, :] for h in wkv), pbank[i]).then_inc(vl_proj, 1)
                    for n in range(NL):
                        half, t = divmod(n, TT)
                        pe.wait_ge(vl_ready, n + 1)
                        project(t, tuple(h[:, half, :] for h in wkv), pbank[n]).then_inc(projected, 1)
                        transposes(n - LAG, n - LAG)

                def step(i):
                    for slot in range(2):
                        stream.wait_tile(pe, i, slot)
                        for t in range(TT):
                            k = slot * TT + t
                            n = NL + SLOTS * i + k
                            need(pe, normed, n - SLOTS + 1)
                            project(t, stream.tile(slot), pbank[k]).then_inc(projected, 1)
                            transposes(n - LAG, (k - LAG) % SLOTS)
                peeled(pe, NQ // 2, step)
                for n in range(NN - LAG, NN):
                    transposes(n, n % SLOTS)

            @block.scalar
            def _(act):
                for i in range(4):
                    act.wait_ge(wkv_loaded[i % 2], 16 * (i // 2 + 1))
                    nc.scalar.activation(wkv[0][:, i, :], g["stage"][:, i % 2, :],
                                         ACT.Copy).then_inc(wkv_hi, 1)
                ln.scalar(act)
                stream.make_hi(act, 0, 0, projected, TT)
                if vl is not None:
                    for i in range(2 * TT):
                        half, t = divmod(i, TT)
                        act.wait_ge(vl_proj, i + 1)
                        nc.scalar.activation(vl[:, t, half * UW:(half + 1) * UW], pbank[i][:],
                                             ACT.Copy).then_inc(vl_ready, 1)

                def square(n, k):
                    act.wait_ge(projected, n + 1)
                    need(act, summed, n - 1)
                    nc.scalar.activation(sq[:, k % 2, :], pbank[k][:], ACT.Square, scale=HD ** -0.5).then_inc(squared, 1)

                def place_latents(n):
                    half, t = divmod(n, TT)
                    act.wait_ge(transposed, n + 1)
                    nc.scalar.activation(klatT[:, half * UNIT_H:(half + 1) * UNIT_H, t * P:(t + 1) * P],
                                         tbank[n % 2][:, :].rearrange("p (h k) -> p h k", h=UNIT_H),
                                         ACT.Copy).then_inc(placed, 1)

                def place_queries(i, k):
                    slot, t = divmod(k, TT)
                    act.wait_ge(transposed, NL + SLOTS * i + k + 1)
                    nc.scalar.activation(
                        qT[:, t * BT:(t + 1) * BT, bass.ds((2 * i + slot) * UNIT_H, UNIT_H), :],
                        tbank[k % 2][:, :].rearrange("p (h b q) -> p b h q", h=UNIT_H, b=BT),
                        ACT.Copy, scale=nk[:, 3:4]).then_inc(placed, 1)

                for n in range(NL):
                    square(n, n)
                    if n >= LAG:
                        place_latents(n - LAG)
                act.wait_ge(norm_ready, 2)

                def step(i):
                    for slot in range(2):
                        if slot == 0:
                            stream.make_hi(act, i, 1, projected, TT)
                        elif not is_at(i, NQ // 2 - 1):
                            stream.make_hi(act, i + 1, 0, projected, TT)
                        for t in range(TT):
                            k = slot * TT + t
                            square(NL + SLOTS * i + k, k)
                            if k >= LAG:
                                place_queries(i, k - LAG)
                            elif not is_at(i, 0):
                                place_queries(i - 1, k - LAG + SLOTS)
                            elif NL:
                                place_latents(NL - LAG + k)
                peeled(act, NQ // 2, step)
                for k in range(SLOTS - LAG, SLOTS):
                    place_queries(NQ // 2 - 1, k)

            @block.vector
            def _(dve):
                for i in range(4):
                    dve.wait_ge(wkv_hi, i + 1)
                    nc.vector.tensor_tensor(wkv[1][:, i, :], g["stage"][:, i % 2, :],
                                            as_f32(wkv[0][:, i, :]), ALU.subtract).then_inc(wkv_lo, 1)
                ln.vector(dve)
                dve.wait_ge(small_loaded, 16)
                nc.vector.tensor_tensor(nk[:, 2:3], nk[:, 0:1], nk[:, 1:2], ALU.mult).then_inc(norm_ready, 1)
                dve.wait_ge(norm_ready, 1)
                nc.vector.tensor_scalar(nk[:, 3:4], nk[:, 2:3], HD ** -0.5, None,
                                        ALU.mult).then_inc(norm_ready, 1)
                stream.make_lo(dve, 0, 0)

                def heads(ap):
                    return ap.rearrange("p (h d) -> p h d", h=UNIT_H)

                def sums(n, k):
                    dve.wait_ge(squared, n + 1)
                    need(dve, rstd_ready, n - SLOTS + 1)
                    nc.vector.tensor_reduce(ss[:, k, :], heads(sq[:, k % 2, :]), AX.X,
                                            ALU.add).then_inc(summed, 1)

                def normalise(n, k):
                    if isinstance(n, int) and n < 0:
                        return
                    dve.wait_ge(rstd_ready, n + 1)
                    need(dve, transposed, n - SLOTS + 1)
                    nc.vector.tensor_tensor(heads(xn[:, k, :]), heads(pbank[k][:, :]),
                                            rstd[:, k, :].unsqueeze(2).broadcast_to([P, UNIT_H, HD]),
                                            ALU.mult).then_inc(normed, 1)
                for n in range(NL):
                    sums(n, n)
                    normalise(n - 1, n - 1)

                def step(i):
                    for slot in range(2):
                        if slot == 0:
                            stream.make_lo(dve, i, 1)
                        elif not is_at(i, NQ // 2 - 1):
                            stream.make_lo(dve, i + 1, 0)
                        for t in range(TT):
                            k = slot * TT + t
                            n = NL + SLOTS * i + k
                            sums(n, k)
                            normalise(n - 1, (k - 1) % SLOTS)
                peeled(dve, NQ // 2, step)
                normalise(NN - 1, (NN - 1) % SLOTS)


def attend(nc, tag, g, w, eps, wkv, qT, mask, klatT, vlat):
    ident = g["ident"]
    tail = klatT is not None
    KEYS = CTX + (SEQ if tail else 0)
    with ExitStack() as ctx:
        s = Space(nc, ctx, tag)
        craw = s.sb("craw", [P, CT, DC * P])
        cT = s.pair("cT", [P, CT, DC * P])
        kT = s.sb("kT", [P, 2, UNIT_H, CTX])
        v = s.sb("v", [P, 2, CT, UW])
        q = s.sb("q", [P, 2, UNIT_H, GROUP * SEQ])
        sq = s.sb("sq", [P, UW])
        kn = s.sb("kn", [P, 2, UW])
        ss = s.sb("ss", [P, 2, UNIT_H])
        ms = s.sb("ms", [P, 2, UNIT_H])
        rstd = s.sb("rstd", [P, 2, UNIT_H])
        const = s.sb("const", [P, 2, UNIT_H])
        sm = s.sb("sm", [P, CTX]) if mask is not None else None
        smax = s.sb("smax", [P, CT])
        nmax = s.sb("nmax", [P, CT])
        rsum = s.sb("rsum", [P, CT])
        rinv = s.sb("rinv", [P, CT])
        p = s.sb("p", [P, KEYS])
        pT = s.sb("pT", [P, CT + 1, P])
        on = s.sb("on", [P, HD])

        kbank = [s.ps(f"kbank{i}") for i in range(2)]
        vbank = s.ps("vbank")
        ktbank = s.ps("ktbank")
        sbank = s.ps("sbank", 2)
        ptbank = s.ps("ptbank")
        obank = s.ps("obank")
        TAIL_T = CTX + P
        OT = P

        const_set = s.sem("const_set")
        ctx_loaded = s.sem("ctx_loaded")
        mask_loaded = s.sem("mask_loaded")
        ctx_hi = s.sem("ctx_hi")
        ctx_lo = s.sem("ctx_lo")
        k_proj = s.sem("k_proj")
        k_squared = s.sem("k_squared")
        k_summed = s.sem("k_summed")
        k_mean = s.sem("k_mean")
        k_rstd = s.sem("k_rstd")
        k_normed = s.sem("k_normed")
        kt_done = s.sem("kt_done")
        kt_ready = s.sem("kt_ready")
        v_proj = s.sem("v_proj")
        v_ready = s.sem("v_ready")
        q_staged = s.sem("q_staged")
        vlat_loaded = [s.sem(f"vlat_loaded{i}") for i in range(2)]
        s_done = s.sem("s_done")
        m_raw = s.sem("m_raw")
        m_done = s.sem("m_done")
        p_ready = s.sem("p_ready")
        pt_done = s.sem("pt_done")
        pt_ready = s.sem("pt_ready")
        o_done = s.sem("o_done")
        r_inv = s.sem("r_inv")
        o_normed = s.sem("o_normed")
        ot_done = s.sem("ot_done")
        ot_ready = s.sem("ot_ready")

        def run(eng, slot_step):
            def both(b):
                slot_step(b, 0)
                slot_step(b, 1)
            peeled(eng, B, both)
            slot_step(B, 0)

        def parts(b, hf):
            u = 2 * b + hf
            fixed = isinstance(u, int)
            return (not fixed or u < UNITS), (not fixed or u > 0), (not fixed or u > 1), u

        with nc.Block() as block:
            @block.sync
            def _(sp):
                def load_context(b):
                    need(sp, ctx_lo, CT * b)
                    sp.dma_start(craw[:, :, :].rearrange("p t n -> p (t n)"),
                                 w["ctx"][bass.ds(b, 1), :, :].rearrange("b p n -> p (b n)")
                                 ).then_inc(ctx_loaded, 16)
                load_context(0)
                if mask is not None:
                    for h in range(GROUP):
                        sp.dma_start(mask[h * SEQ:(h + 1) * SEQ, :], w["mask"]).then_inc(mask_loaded, 16)

                def step(b, hf):
                    projects, attends, _, u = parts(b, hf)
                    if projects and hf == 0 and not is_at(b, B - 1):
                        load_context(b + 1)
                    if tail and projects:
                        need(sp, o_done, 4 * (u - 1))
                        sp.dma_start(vlat[:, hf, :],
                                     g["vlat_dram"][bass.ds(b * SEQ, SEQ), hf * UW:(hf + 1) * UW]
                                     ).then_inc(vlat_loaded[hf], 16)
                run(sp, step)

            @block.gpsimd
            def _(pool):
                nc.gpsimd.memset(const[:, 0, :], -0.5).then_inc(const_set, 1)
                nc.gpsimd.memset(const[:, 1, :], eps).then_inc(const_set, 1)

                def step(b, hf):
                    projects, _, _, u = parts(b, hf)
                    if not projects:
                        return
                    need(pool, s_done, 4 * (u - 1))
                    nc.gpsimd.tensor_copy(q[:, hf, :, :].rearrange("p h n -> p (h n)"),
                                          qT[:, bass.ds(b, 1), hf * 16:(hf + 1) * 16, :]
                                          .rearrange("p b h q -> p (b h q)")).then_inc(q_staged, 1)
                    for k in range(CT):
                        n = 4 * u + k
                        pool.wait_ge(const_set, 2)
                        pool.wait_ge(k_summed, n + 1)
                        nc.gpsimd.tensor_tensor(ms[:, k % 2, :], ss[:, k % 2, :], const[:, 1, :],
                                                ALU.add).then_inc(k_mean, 1)
                        pool.wait_ge(k_mean, n + 1)
                        nc.gpsimd.tensor_tensor(rstd[:, k % 2, :], ms[:, k % 2, :], const[:, 0, :],
                                                ALU.pow).then_inc(k_rstd, 1)
                run(pool, step)

            @block.tensor
            def _(pe):
                def project(k, col, bank):
                    for c in range(DC):
                        a = tuple(h[:, k, c * P:(c + 1) * P] for h in cT)
                        last = mm3(nc, bank[:], a, tuple(h[:, col, c * UW:(c + 1) * UW] for h in wkv),
                                   c == 0, c == DC - 1)
                    return last

                def pv(a, ahf, k, b):
                    pe.wait_ge(pt_ready, a + 1)
                    need(pe, ot_ready, a)
                    for t in range(CT):
                        last = nc.tensor.matmul(obank[:, 0:HD], pT[:, t, :], v[:, ahf, t, k * HD:(k + 1) * HD],
                                                start=(t == 0), stop=(t == CT - 1 and not tail))
                    if tail:
                        last = nc.tensor.matmul(obank[:, 0:HD], pT[0:SEQ, CT, :],
                                                vlat[:, ahf, k * HD:(k + 1) * HD], start=False, stop=True)
                    last.then_inc(o_done, 1)

                def o_transpose(a):
                    pe.wait_ge(o_normed, a + 1)
                    nc.tensor.transpose(obank[:, OT:OT + P], on[:], ident[:]).then_inc(ot_done, 1)

                def kt(n, kb):
                    pe.wait_ge(k_normed, n + 1)
                    need(pe, kt_ready, n)
                    for h in range(UNIT_H):
                        last = nc.tensor.transpose(ktbank[:, h * P:(h + 1) * P],
                                                   kn[:, kb, h * P:(h + 1) * P], ident[:])
                    last.then_inc(kt_done, 1)

                def step(b, hf):
                    projects, attends, lags, u = parts(b, hf)
                    ahf = 1 - hf
                    for k in range(CT):
                        n = 4 * u + k
                        a = n - 4
                        lag = attends and (lags or k > 0)
                        if projects:
                            if hf == 0:
                                pe.wait_ge(ctx_lo, CT * b + k + 1)
                            need(pe, k_normed, n - 1)
                            project(k, hf, kbank[k % 2]).then_inc(k_proj, 1)
                        if (projects and k > 0) or (attends and k == 0):
                            kt(n - 1, (k - 1) % 2)
                        if lag:
                            pv(a - 1, ahf if k else hf, (k - 1) % UNIT_H, b)
                        if attends:
                            if k == 0:
                                pe.wait_ge(kt_ready, n)
                                pe.wait_ge(q_staged, u)
                                pe.wait_ge(v_ready, n)
                                if tail:
                                    pe.wait_ge(vlat_loaded[ahf], 16 * (b if hf == 0 else b + 1))
                            need(pe, p_ready, a)
                            need(pe, pt_ready, a)
                            nc_last = nc.tensor.matmul(sbank[:, 0:CTX], q[:, ahf, k, :], kT[:, ahf, k, :],
                                                       start=True, stop=True)
                            if tail:
                                at = (b - 1 if hf == 0 else b) * SEQ
                                nc_last = nc.tensor.matmul(sbank[:, CTX:KEYS], q[:, ahf, k, :],
                                                           klatT[:, ahf * UNIT_H + k, bass.ds(at, SEQ)],
                                                           start=True, stop=True)
                            nc_last.then_inc(s_done, 1)
                        if projects:
                            need(pe, v_ready, n)
                            project(k, 2 + hf, vbank).then_inc(v_proj, 1)
                        if attends:
                            pe.wait_ge(p_ready, a + 1)
                            for t in range(CT):
                                last = nc.tensor.transpose(ptbank[:, t * P:(t + 1) * P],
                                                           p[:, t * P:(t + 1) * P], ident[:])
                            if tail:
                                last = nc.tensor.transpose(sbank[0:SEQ, TAIL_T:TAIL_T + P],
                                                           p[:, CTX:KEYS], ident[:])
                            last.then_inc(pt_done, 1)
                        if lag:
                            o_transpose(a - 1)
                run(pe, step)
                last_a = 4 * UNITS - 1
                pv(last_a, 1, UNIT_H - 1, None)
                o_transpose(last_a)

            @block.scalar
            def _(act):
                def split_hi(k):
                    nc.scalar.activation(cT[0][:, k, :], craw[:, k, :], ACT.Copy).then_inc(ctx_hi, 1)

                act.wait_ge(ctx_loaded, 16)
                for k in range(CT):
                    split_hi(k)

                def step(b, hf):
                    projects, attends, _, u = parts(b, hf)
                    for k in range(CT):
                        n = 4 * u + k
                        a = n - 4
                        if projects:
                            act.wait_ge(k_proj, n + 1)
                            need(act, k_summed, n)
                            nc.scalar.activation(sq[:], kbank[k % 2][:], ACT.Square, scale=HD ** -0.5).then_inc(k_squared, 1)
                        if (projects and k > 0) or (attends and k == 0):
                            act.wait_ge(kt_done, n)
                            need(act, s_done, 4 * (u - 1))
                            kb, kk = (hf, k - 1) if k else (1 - hf, CT - 1)
                            nc.scalar.activation(kT[:, kb, :, kk * P:(kk + 1) * P],
                                                 ktbank[:, :].rearrange("p (h n) -> p h n", h=UNIT_H),
                                                 ACT.Copy).then_inc(kt_ready, 1)
                        if attends:
                            act.wait_ge(m_done, a + 1)
                            need(act, pt_done, a)
                            src = sm[:] if mask is not None else sbank[:, 0:KEYS]
                            nc.scalar.activation(p[:], src, ACT.Exp, bias=nmax[:, k:k + 1],
                                                 accum_out=rsum[:, k:k + 1]).then_inc(p_ready, 1)
                        if projects:
                            act.wait_ge(v_proj, n + 1)
                            need(act, o_done, 4 * (u - 1))
                            nc.scalar.activation(v[:, hf, k, :], vbank[:], ACT.Copy).then_inc(v_ready, 1)
                            if hf == 1 and not is_at(b, B - 1):
                                act.wait_ge(ctx_loaded, b * 16 + 32)
                                split_hi(k)

                run(act, step)

            @block.vector
            def _(dve):
                def split_lo(k, count):
                    dve.wait_ge(ctx_hi, count)
                    nc.vector.tensor_tensor(cT[1][:, k, :], craw[:, k, :], as_f32(cT[0][:, k, :]),
                                            ALU.subtract).then_inc(ctx_lo, 1)

                for k in range(CT):
                    split_lo(k, k + 1)

                def o_norm(a, kk):
                    dve.wait_ge(o_done, a + 1)
                    dve.wait_ge(r_inv, a + 1)
                    need(dve, ot_done, a)
                    nc.vector.tensor_scalar(on[:], obank[:, 0:HD], rinv[:, kk:kk + 1], None,
                                            ALU.mult).then_inc(o_normed, 1)

                def ot_place(a, b, hf, kk):
                    dve.wait_ge(ot_done, a + 1)
                    nc.vector.tensor_copy(
                        qT[:, bass.ds(b, 1), (hf * UNIT_H + kk) * GROUP:(hf * UNIT_H + kk + 1) * GROUP, :]
                        .rearrange("p b h q -> p (b h q)"),
                        obank[:, OT:OT + P]).then_inc(ot_ready, 1)

                def step(b, hf):
                    projects, attends, lags, u = parts(b, hf)
                    for k in range(CT):
                        n = 4 * u + k
                        a = n - 4
                        lag = attends and (lags or k > 0)
                        if k:
                            lb, lhf, lk = (b, 0, k - 1) if hf == 1 else (b - 1, 1, k - 1)
                        else:
                            lb, lhf, lk = b - 1, hf, CT - 1
                        if projects:
                            dve.wait_ge(k_squared, n + 1)
                            nc.vector.tensor_reduce(ss[:, k % 2, :],
                                                    sq[:, :].rearrange("p (h d) -> p h d", h=UNIT_H),
                                                    AX.X, ALU.add).then_inc(k_summed, 1)
                        if attends:
                            if mask is not None:
                                dve.wait_ge(mask_loaded, 16 * GROUP)
                            dve.wait_ge(s_done, a + 1)
                            need(dve, p_ready, a)
                        if lag:
                            nc.vector.reciprocal(rinv[:, lk:lk + 1], rsum[:, lk:lk + 1]).then_inc(r_inv, 1)
                        if attends and mask is None:
                            nc.vector.tensor_reduce(nmax[:, k:k + 1], sbank[:, 0:KEYS], AX.X, ALU.max,
                                                    negate=True).then_inc(m_done, 1)
                        elif attends:
                            nc.vector.tensor_tensor_reduce(
                                out=sm[:], in0=sbank[:, 0:CTX], in1=mask[:], scale=1.0, scalar=-3.4e38,
                                op0=ALU.add, op1=ALU.max, accum_out=smax[:, k:k + 1]).then_inc(m_raw, 1)
                            dve.wait_ge(m_raw, a + 1)
                            nc.vector.tensor_scalar(nmax[:, k:k + 1], smax[:, k:k + 1], -1.0, None,
                                                    ALU.mult).then_inc(m_done, 1)
                        if lag:
                            o_norm(a - 1, lk)
                        if projects:
                            dve.wait_ge(k_rstd, n + 1)
                            need(dve, kt_done, n - 1)
                            nc.vector.tensor_tensor(
                                kn[:, k % 2, :].rearrange("p (h d) -> p h d", h=UNIT_H),
                                kbank[k % 2][:, :].rearrange("p (h d) -> p h d", h=UNIT_H),
                                rstd[:, k % 2, :].unsqueeze(2).broadcast_to([P, UNIT_H, HD]),
                                ALU.mult).then_inc(k_normed, 1)
                        if attends:
                            dve.wait_ge(pt_done, a + 1)
                            need(dve, o_done, a)
                            last = nc.vector.tensor_copy(pT[:, 0:CT, :],
                                                         ptbank[:, :].rearrange("p (t n) -> p t n", t=CT))
                            if tail:
                                last = nc.vector.tensor_copy(pT[0:SEQ, CT, :], sbank[0:SEQ, TAIL_T:TAIL_T + P])
                            last.then_inc(pt_ready, 1)
                        if lag:
                            ot_place(a - 1, lb, lhf, lk)
                        if projects and hf == 1 and not is_at(b, B - 1):
                            dve.wait_ge(v_proj, n + 1)
                            split_lo(k, CT * (b + 1) + k + 1)

                run(dve, step)
                last_a = 4 * UNITS - 1
                nc.vector.reciprocal(rinv[:, 3:4], rsum[:, 3:4]).then_inc(r_inv, 1)
                o_norm(last_a, CT - 1)
                ot_place(last_a, B - 1, 1, CT - 1)
                dve.wait_ge(ot_ready, last_a + 1)


def project_out(nc, tag, g, w, oT):
    x = g["x"]
    NW = HEADS // GROUP
    with ExitStack() as ctx:
        s = Space(nc, ctx, tag)
        stream = WeightStream(nc, s, "w", GROUP * D, stage=g["stage"])
        o = s.pair("o", [P, 2, GROUP, TOK])
        ybank = [s.ps(f"ybank{t}") for t in range(TT)]
        o_hi = s.sem("o_hi")
        o_lo = s.sem("o_lo")
        used = s.sem("used")
        added = s.sem("added")

        def heads_of(i, slot):
            return oT[:, :, bass.ds((2 * i + slot) * GROUP, GROUP), :].rearrange("p b h q -> p h b q")

        def split_of(half, slot):
            return half[:, slot, :, :].rearrange("p h (b q) -> p h b q", b=B)

        with nc.Block() as block:
            @block.sync
            def _(sp):
                def step(i):
                    for slot in range(2):
                        stream.load(sp, w["wo"][bass.ds(2 * i + slot, 1), :, :]
                                    .rearrange("a p n -> p (a n)"), i, slot)
                peeled(sp, NW // 2, step)

            @block.scalar
            def _(act):
                def step(i):
                    for slot in range(2):
                        n = 2 * i + slot
                        need(act, used, n - 1)
                        nc.scalar.activation(split_of(o[0], slot), heads_of(i, slot), ACT.Copy).then_inc(o_hi, 1)
                        stream.make_hi(act, i, slot, used, 1)
                peeled(act, NW // 2, step)

            @block.vector
            def _(dve):
                def step(i):
                    for slot in range(2):
                        n = 2 * i + slot
                        dve.wait_ge(o_hi, n + 1)
                        nc.vector.tensor_tensor(split_of(o[1], slot), heads_of(i, slot),
                                                as_f32(split_of(o[0], slot)), ALU.subtract).then_inc(o_lo, 1)
                        stream.make_lo(dve, i, slot)
                peeled(dve, NW // 2, step)
                dve.wait_ge(used, NW)
                for t in range(TT):
                    nc.vector.tensor_tensor(x[:, t, :], x[:, t, :], ybank[t][:], ALU.add).then_inc(added, 1)
                dve.wait_ge(added, TT)

            @block.tensor
            def _(pe):
                def step(i):
                    for slot in range(2):
                        n = 2 * i + slot
                        pe.wait_ge(o_lo, n + 1)
                        stream.wait_tile(pe, i, slot)
                        wt = stream.tile(slot)
                        for h in range(GROUP):
                            for t in range(TT):
                                last = mm3(nc, ybank[t][:],
                                           tuple(half[:, slot, h, t * P:(t + 1) * P] for half in o),
                                           tuple(half[:, h * D:(h + 1) * D] for half in wt),
                                           is_at(n, 0) and h == 0, is_at(n, NW - 1) and h == GROUP - 1)
                        last.then_inc(used, 1)
                peeled(pe, NW // 2, step)


class GatedTiles:
    RING = 4
    GU = 2 * DC * P
    WIDTH = GU + D

    def __init__(self, nc, s, xT, tiles):
        self.nc, self.xT, self.tiles = nc, xT, tiles
        self.stage = s.sb("stage", [P, self.RING, self.WIDTH])
        self.gu = s.pair("gu", [P, 2, self.GU])
        self.dn = s.pair("dn", [P, 2, D])
        self.sg = s.sb("sg", [P, 2, TOK])
        self.a = s.sb("a", [P, 2, TOK])
        self.raw = s.sb("raw", [P, TOK])
        self.act = s.pair("act", [P, 2, TOK])
        self.gubank = [s.ps(f"gubank{i}") for i in range(2)]
        self.ybank = [s.ps(f"ybank{i}") for i in range(TT)]
        self.loaded = [s.sem(f"loaded{i}") for i in range(self.RING)]
        self.gu_hi_sem = s.sem("gu_hi")
        self.gu_lo_sem = s.sem("gu_lo")
        self.dn_hi_sem = s.sem("dn_hi")
        self.dn_lo_sem = s.sem("dn_lo")
        self.gu_done_sem = s.sem("gu_done")
        self.silu_done_sem = s.sem("silu_done")
        self.a_raw_sem = s.sem("a_raw")
        self.a_done_sem = s.sem("a_done")
        self.act_hi_sem = s.sem("act_hi")
        self.act_lo_sem = s.sem("act_lo")
        self.down_done_sem = s.sem("down_done")

    def load(self, sp, src, f, k):
        need(sp, self.dn_lo_sem, f - self.RING + 1)
        sp.dma_start(self.stage[:, k, :], src).then_inc(self.loaded[k], 16)

    def gu_hi(self, act, f, i, k):
        act.wait_ge(self.loaded[k], i * 16 + 16)
        need(act, self.gu_done_sem, f - 1)
        self.nc.scalar.activation(self.gu[0][:, k % 2, :], self.stage[:, k, :self.GU],
                                  ACT.Copy).then_inc(self.gu_hi_sem, 1)

    def gu_lo(self, dve, f, k):
        dve.wait_ge(self.gu_hi_sem, f + 1)
        self.nc.vector.tensor_tensor(self.gu[1][:, k % 2, :], self.stage[:, k, :self.GU],
                                     as_f32(self.gu[0][:, k % 2, :]), ALU.subtract).then_inc(self.gu_lo_sem, 1)

    def scalar(self, act, f, i, k, last):
        nc, h = self.nc, k % 2
        if not last:
            self.gu_hi(act, f + 1, i + (k + 1) // self.RING, (k + 1) % self.RING)
        act.wait_ge(self.gu_done_sem, f + 1)
        need(act, self.a_done_sem, f - 1)
        nc.scalar.activation(self.sg[:, h, :], self.gubank[h][:, 0:TOK], ACT.Silu).then_inc(self.silu_done_sem, 1)
        need(act, self.down_done_sem, f - 1)
        nc.scalar.activation(self.dn[0][:, h, :], self.stage[:, k, self.GU:], ACT.Copy).then_inc(self.dn_hi_sem, 1)
        act.wait_ge(self.a_done_sem, f + 1)
        nc.scalar.activation(self.act[0][:, h, :], self.a[:, h, :], ACT.Copy).then_inc(self.act_hi_sem, 1)

    def vector(self, dve, f, k, last, combine=None):
        nc, h = self.nc, k % 2
        if not last:
            self.gu_lo(dve, f + 1, (k + 1) % self.RING)
        dve.wait_ge(self.silu_done_sem, f + 1)
        need(dve, self.act_hi_sem, f - 1)
        if combine is None:
            nc.vector.tensor_tensor(self.a[:, h, :], self.sg[:, h, :], self.gubank[h][:, TOK:2 * TOK],
                                    ALU.mult).then_inc(self.a_done_sem, 1)
        else:
            bank, sem, value, before = combine
            nc.vector.tensor_tensor(self.raw[:], self.sg[:, h, :], self.gubank[h][:, TOK:2 * TOK],
                                    ALU.mult).then_inc(self.a_raw_sem, 1)
            dve.wait_ge(sem, value)
            dve.wait_ge(self.a_raw_sem, before + 1)
            nc.vector.tensor_tensor(self.a[:, h, :], self.raw[:], bank, ALU.mult).then_inc(self.a_done_sem, 1)
        dve.wait_ge(self.dn_hi_sem, f + 1)
        nc.vector.tensor_tensor(self.dn[1][:, h, :], self.stage[:, k, self.GU:], as_f32(self.dn[0][:, h, :]),
                                ALU.subtract).then_inc(self.dn_lo_sem, 1)
        dve.wait_ge(self.act_hi_sem, f + 1)
        nc.vector.tensor_tensor(self.act[1][:, h, :], self.a[:, h, :], as_f32(self.act[0][:, h, :]),
                                ALU.subtract).then_inc(self.act_lo_sem, 1)

    def gate_up(self, pe, f, k):
        nc, h = self.nc, k % 2
        pe.wait_ge(self.gu_lo_sem, f + 1)
        need(pe, self.a_done_sem, f - 1)
        for part in range(2):
            for c in range(DC):
                at = (part * DC + c) * P
                last = mm3(nc, self.gubank[h][:, part * TOK:(part + 1) * TOK],
                           tuple(w[:, h, at:at + P] for w in self.gu),
                           tuple(v[:, c, :] for v in self.xT), c == 0, c == DC - 1)
        last.then_inc(self.gu_done_sem, 1)

    def down(self, pe, f, k, start, stop):
        nc, h = self.nc, k % 2
        pe.wait_ge(self.act_lo_sem, f + 1)
        pe.wait_ge(self.dn_lo_sem, f + 1)
        for t in range(TT):
            last = mm3(nc, self.ybank[t][:], tuple(v[:, h, t * P:(t + 1) * P] for v in self.act),
                       tuple(w[:, h, :] for w in self.dn), start, stop)
        last.then_inc(self.down_done_sem, 1)


def split_tile(nc, act=None, dve=None, dst=None, src=None, hi_done=None, lo_done=None):
    if act is not None:
        nc.scalar.activation(dst[0], src, ACT.Copy).then_inc(hi_done, 1)
    else:
        nc.vector.tensor_tensor(dst[1], src, as_f32(dst[0]), ALU.subtract).then_inc(lo_done, 1)


def mixer(nc, tag, g, a):
    x, ident = g["x"], g["ident"]
    NF = a["mix_ffn"].shape[0]
    NT = TAYLOR + 1
    with ExitStack() as ctx:
        s = Space(nc, ctx, tag)
        xT = s.pair("xT", [P, DC, TOK])
        tbank = [s.ps(f"tbank{i}") for i in range(2)]
        ln = LayerNormT(nc, s, x, ident, xT, tbank)
        G = GatedTiles(nc, s, xT, NF)
        praw = s.sb("praw", [P, 2 * DC * P])
        pw = s.pair("pw", [P, 2 * DC * P])
        traw = s.sb("traw", [P, NT, D])
        tw = s.pair("tw", [P, NT, D])
        point = s.sb("point", [P, 1])
        disc = s.sb("disc", [P, TAYLOR])
        factor = s.sb("factor", [P, TAYLOR])
        delta = s.sb("delta", [P, TOK])
        power = s.sb("power", [P, TAYLOR, TOK])
        keep = s.sb("keep", [P, 3, TOK])
        term = s.sb("term", [P, NT, TOK])
        term_s = s.pair("terms", [P, NT, TOK])
        mbank = s.ps("mbank")

        w_loaded = s.sem("w_loaded")
        t_loaded = s.sem("t_loaded")
        pw_hi = s.sem("pw_hi")
        pw_lo = s.sem("pw_lo")
        tw_hi = s.sem("tw_hi")
        tw_lo = s.sem("tw_lo")
        factor_done = s.sem("factor_done")
        m_proj = s.sem("m_proj")
        m_read = s.sem("m_read")
        poly = s.sem("poly")
        terms_done = s.sem("terms_done")
        term_hi = s.sem("term_hi")
        term_lo = s.sem("term_lo")
        t_done = s.sem("t_done")
        added = s.sem("added")

        with nc.Block() as block:
            @block.sync
            def _(sp):
                sp.dma_start(praw[:], a["mix_proj"]).then_inc(w_loaded, 16)
                sp.dma_start(point[:], a["mix_point"]).then_inc(w_loaded, 16)
                sp.dma_start(disc[:], a["mix_disc"].partition_broadcast(P)).then_inc(w_loaded, 16)
                for f in range(NF):
                    G.load(sp, a["mix_ffn"][f], f, f % G.RING)
                    if f == 1:
                        sp.dma_start(traw[:], a["mix_out"]).then_inc(t_loaded, 16)

            @block.gpsimd
            def _(pool):
                ln.gpsimd(pool)
                pool.wait_ge(m_read, 2)
                pool.wait_ge(factor_done, 1)
                count = [0]

                def chain(ins):
                    ins.then_inc(poly, 1)
                    count[0] += 1
                    pool.wait_ge(poly, count[0])
                nc.gpsimd.tensor_scalar(keep[:, 0, :], delta[:], TAYLOR_KEEP, None, ALU.is_le).then_inc(poly, 1)
                count[0] += 1
                chain(nc.gpsimd.tensor_scalar(keep[:, 1, :], delta[:], -TAYLOR_KEEP, None, ALU.is_ge))
                chain(nc.gpsimd.tensor_tensor(keep[:, 2, :], keep[:, 0, :], keep[:, 1, :], ALU.mult))
                before = term[:, 0, :]
                for m in range(1, TAYLOR + 1):
                    chain(nc.gpsimd.tensor_tensor(power[:, m - 1, :], before, delta[:], ALU.mult))
                    before = power[:, m - 1, :]
                    if m > TAYLOR_MIN:
                        chain(nc.gpsimd.tensor_tensor(keep[:, m % 2, :], before, keep[:, 2, :], ALU.mult))
                        before = keep[:, m % 2, :]
                    last = nc.gpsimd.tensor_scalar(term[:, m, :], before, factor[:, m - 1:m], None, ALU.mult)
                last.then_inc(terms_done, 1)

            @block.tensor
            def _(pe):
                ln.tensor(pe)
                ln.wait_ready(pe)
                pe.wait_ge(pw_lo, 1)
                for part in range(2):
                    for c in range(DC):
                        at = (part * DC + c) * P
                        last = mm3(nc, mbank[:, part * TOK:(part + 1) * TOK],
                                   tuple(w[:, at:at + P] for w in pw),
                                   tuple(v[:, c, :] for v in xT), c == 0, c == DC - 1)
                last.then_inc(m_proj, 1)
                for f in range(NF):
                    G.gate_up(pe, f, f % G.RING)
                    if f:
                        G.down(pe, f - 1, (f - 1) % G.RING, f == 1, False)
                G.down(pe, NF - 1, (NF - 1) % G.RING, False, False)
                pe.wait_ge(term_lo, 1)
                pe.wait_ge(tw_lo, 1)
                for t in range(TT):
                    for m in range(NT):
                        last = mm3(nc, G.ybank[t][:], tuple(v[:, m, t * P:(t + 1) * P] for v in term_s),
                                   tuple(w[:, m, :] for w in tw), False, m == NT - 1)
                    last.then_inc(t_done, 1)

            @block.scalar
            def _(act):
                act.wait_ge(w_loaded, 48)
                split_tile(nc, act=act, dst=(pw[0][:], pw[1][:]), src=praw[:], hi_done=pw_hi)
                nc.scalar.activation(factor[:], disc[:], ACT.Exp, scale=-1.0).then_inc(factor_done, 1)
                ln.scalar(act)
                G.gu_hi(act, 0, 0, 0)
                act.wait_ge(m_proj, 1)
                nc.scalar.activation(term[:, 0, :], mbank[:, TOK:2 * TOK], ACT.Copy).then_inc(m_read, 1)
                for f in range(NF):
                    G.scalar(act, f, f // G.RING, f % G.RING, f == NF - 1)
                    if f == 2:
                        act.wait_ge(t_loaded, 16)
                        split_tile(nc, act=act, dst=(tw[0][:], tw[1][:]), src=traw[:], hi_done=tw_hi)
                    if f == NF - 3:
                        act.wait_ge(terms_done, 1)
                        split_tile(nc, act=act, dst=(term_s[0][:], term_s[1][:]), src=term[:], hi_done=term_hi)

            @block.vector
            def _(dve):
                ln.vector(dve)
                dve.wait_ge(pw_hi, 1)
                split_tile(nc, dve=dve, dst=(pw[0][:], pw[1][:]), src=praw[:], lo_done=pw_lo)
                G.gu_lo(dve, 0, 0)
                dve.wait_ge(m_read, 1)
                nc.vector.tensor_scalar(delta[:], mbank[:, 0:TOK], point[:, 0:1], None,
                                        ALU.subtract).then_inc(m_read, 1)
                for f in range(NF):
                    G.vector(dve, f, f % G.RING, f == NF - 1)
                    if f == 2:
                        dve.wait_ge(tw_hi, 1)
                        split_tile(nc, dve=dve, dst=(tw[0][:], tw[1][:]), src=traw[:], lo_done=tw_lo)
                    if f == NF - 3:
                        dve.wait_ge(term_hi, 1)
                        split_tile(nc, dve=dve, dst=(term_s[0][:], term_s[1][:]), src=term[:], lo_done=term_lo)
                for t in range(TT):
                    dve.wait_ge(t_done, t + 1)
                    nc.vector.tensor_tensor(x[:, t, :], x[:, t, :], G.ybank[t][:], ALU.add).then_inc(added, 1)


LORA_H, LORA_R = 1376, 2
LORA_REP = 4
LORA_HQ = LORA_H // LORA_REP
LORA_M = -(-LORA_HQ // P)
LORA_F = LORA_REP * LORA_M


def lora_ffn(nc, tag, g, a):
    x, ident = g["x"], g["ident"]
    with ExitStack() as ctx:
        s = Space(nc, ctx, tag)
        xT = s.pair("xT", [P, DC, TOK])
        tbank = [s.ps(f"tbank{i}") for i in range(2)]
        ln = LayerNormT(nc, s, x, ident, xT, tbank)
        graw = s.sb("graw", [P, 2, LORA_F * P])
        gw = s.pair("gw", [P, 2, LORA_F * P])
        draw = s.sb("draw", [P, LORA_M, D])
        dw = s.pair("dw", [P, LORA_M, D])
        araw = s.sb("araw", [P, DC, P])
        aw = s.pair("aw", [P, DC, P])
        bw = s.sb("bw", [2 * LORA_R, 2, LORA_F * P])
        a2 = s.sb("a2", [P, LORA_F, LORA_R])
        b2 = s.sb("b2", [LORA_R, D])
        la = s.sb("la", [2 * LORA_R, TOK])
        l2 = s.sb("l2", [LORA_R, TOK])
        xs = s.sb("xs", [P, TT, P])
        xsT = s.pair("xsT", [P, TOK])
        sg = s.sb("sg", [P, 2, TOK])
        hid = s.sb("hid", [P, LORA_F, TOK])
        hs = s.sb("hs", [P, LORA_M, TOK])
        hs_s = s.pair("hss", [P, LORA_M, TOK])
        gubank = [s.ps(f"gubank{i}") for i in range(2)]
        lbank = s.ps("lbank")
        ybank = [s.ps(f"ybank{i}") for i in range(TT)]

        g_loaded = s.sem("g_loaded")
        d_loaded = s.sem("d_loaded")
        a_loaded = s.sem("a_loaded")
        small_loaded = s.sem("small_loaded")
        g_hi, g_lo = s.sem("g_hi"), s.sem("g_lo")
        d_hi, d_lo = s.sem("d_hi"), s.sem("d_lo")
        a_hi, a_lo = s.sem("a_hi"), s.sem("a_lo")
        xs_done = s.sem("xs_done")
        xs_tr = s.sem("xs_tr")
        xs_hi, xs_lo = s.sem("xs_hi"), s.sem("xs_lo")
        la_done, la_read = s.sem("la_done"), s.sem("la_read")
        gu_done, silu_done, hid_done = s.sem("gu_done"), s.sem("silu_done"), s.sem("hid_done")
        l2_done, l2_read = s.sem("l2_done"), s.sem("l2_read")
        hs_done, hs_hi, hs_lo = s.sem("hs_done"), s.sem("hs_hi"), s.sem("hs_lo")
        y_done, added = s.sem("y_done"), s.sem("added")

        with nc.Block() as block:
            @block.sync
            def _(sp):
                sp.dma_start(araw[:], a["lora_a"]).then_inc(a_loaded, 16)
                sp.dma_start(graw[:], a["lora_g"]).then_inc(g_loaded, 16)
                sp.dma_start(bw[:], a["lora_b"]).then_inc(small_loaded, 16)
                sp.dma_start(a2[:], a["lora_a2"]).then_inc(small_loaded, 16)
                sp.dma_start(b2[:], a["lora_b2"]).then_inc(small_loaded, 16)
                sp.dma_start(draw[:], a["lora_d"]).then_inc(d_loaded, 16)

            @block.gpsimd
            def _(pool):
                ln.gpsimd(pool)

            @block.tensor
            def _(pe):
                ln.tensor(pe)
                for t in range(TT):
                    pe.wait_ge(xs_done, t + 1)
                    nc.tensor.transpose(lbank[:, t * P:(t + 1) * P], xs[:, t, :], ident[:]).then_inc(xs_tr, 1)
                ln.wait_ready(pe)
                pe.wait_ge(a_lo, 1)
                for c in range(DC):
                    last = mm3(nc, gubank[0][:, 0:TOK], tuple(w[:, c, :] for w in aw),
                               tuple(v[:, c, :] for v in xT), c == 0, c == DC - 1)
                last.then_inc(la_done, 1)
                pe.wait_ge(small_loaded, 48)
                pe.wait_ge(xs_lo, 1)
                pe.wait_ge(la_read, 1)
                for f in range(LORA_F):
                    if f % LORA_REP == 0 and f // LORA_REP < 3:
                        pe.wait_ge(g_lo, f // LORA_REP + 1)
                    need(pe, hid_done, f - 1)
                    for part in range(2):
                        out = gubank[f % 2][:, part * TOK:(part + 1) * TOK]
                        mm3(nc, out, tuple(w[:, part, f * P:(f + 1) * P] for w in gw),
                            tuple(v[:] for v in xsT), True, False)
                        last = nc.tensor.matmul(out, bw[:, part, f * P:(f + 1) * P], la[:], start=False, stop=True)
                    last.then_inc(gu_done, 1)
                pe.wait_ge(xs_hi, 1)
                for f in range(LORA_F):
                    pe.wait_ge(hid_done, f + 1)
                    last = nc.tensor.matmul(lbank[0:LORA_R, 0:TOK], a2[:, f, :], hid[:, f, :],
                                            start=(f == 0), stop=(f == LORA_F - 1))
                last.then_inc(l2_done, 1)
                pe.wait_ge(hs_lo, 1)
                pe.wait_ge(d_lo, 1)
                pe.wait_ge(l2_read, 1)
                for t in range(TT):
                    for m in range(LORA_M):
                        mm3(nc, ybank[t][:], tuple(v[:, m, t * P:(t + 1) * P] for v in hs_s),
                            tuple(w[:, m, :] for w in dw), m == 0, False)
                    nc.tensor.matmul(ybank[t][:], l2[:, t * P:(t + 1) * P], b2[:], start=False,
                                     stop=True).then_inc(y_done, 1)

            def thirds(ap, m):
                n = LORA_REP * P
                return ap[:, :, m * n:(m + 1) * n]

            @block.scalar
            def _(act):
                act.wait_ge(a_loaded, 16)
                nc.scalar.activation(aw[0][:], araw[:], ACT.Copy).then_inc(a_hi, 1)
                ln.scalar(act)
                act.wait_ge(xs_tr, TT)
                nc.scalar.activation(xsT[0][:], lbank[:, 0:TOK], ACT.Copy).then_inc(xs_hi, 1)
                act.wait_ge(g_loaded, 16)
                nc.scalar.activation(thirds(gw[0], 0), thirds(graw, 0), ACT.Copy).then_inc(g_hi, 1)
                act.wait_ge(la_done, 1)
                nc.scalar.activation(la[:], gubank[0][0:2 * LORA_R, 0:TOK], ACT.Copy, scale=0.5).then_inc(la_read, 1)
                for m in range(1, LORA_M):
                    nc.scalar.activation(thirds(gw[0], m), thirds(graw, m), ACT.Copy).then_inc(g_hi, 1)
                for f in range(LORA_F):
                    act.wait_ge(gu_done, f + 1)
                    need(act, hid_done, f - 1)
                    nc.scalar.activation(sg[:, f % 2, :], gubank[f % 2][:, 0:TOK], ACT.Silu).then_inc(silu_done, 1)
                    if f == 2:
                        act.wait_ge(d_loaded, 16)
                        nc.scalar.activation(dw[0][:], draw[:], ACT.Copy).then_inc(d_hi, 1)
                act.wait_ge(hs_done, LORA_M)
                nc.scalar.activation(hs_s[0][:], hs[:], ACT.Copy).then_inc(hs_hi, 1)
                act.wait_ge(l2_done, 1)
                nc.scalar.activation(l2[:], lbank[0:LORA_R, 0:TOK], ACT.Copy, scale=0.5).then_inc(l2_read, 1)

            @block.vector
            def _(dve):
                ln.vector(dve)
                for t in range(TT):
                    dve.wait_ge(ln.normed, t + 1)
                    nc.vector.tensor_reduce(xs[:, t, :], ln.xn[:, t, :].rearrange("p (c k) -> p k c", c=DC),
                                            AX.X, ALU.add).then_inc(xs_done, 1)
                dve.wait_ge(a_hi, 1)
                nc.vector.tensor_tensor(aw[1][:], araw[:], as_f32(aw[0][:]), ALU.subtract).then_inc(a_lo, 1)
                dve.wait_ge(xs_hi, 1)
                nc.vector.tensor_tensor(xsT[1][:], lbank[:, 0:TOK], as_f32(xsT[0][:]), ALU.subtract).then_inc(xs_lo, 1)
                for m in range(LORA_M):
                    dve.wait_ge(g_hi, m + 1)
                    nc.vector.tensor_tensor(thirds(gw[1], m), thirds(graw, m), as_f32(thirds(gw[0], m)),
                                            ALU.subtract).then_inc(g_lo, 1)
                for f in range(LORA_F):
                    dve.wait_ge(silu_done, f + 1)
                    nc.vector.tensor_tensor(hid[:, f, :], sg[:, f % 2, :], gubank[f % 2][:, TOK:2 * TOK],
                                            ALU.mult).then_inc(hid_done, 1)
                    if f == 2:
                        dve.wait_ge(d_hi, 1)
                        nc.vector.tensor_tensor(dw[1][:], draw[:], as_f32(dw[0][:]), ALU.subtract).then_inc(d_lo, 1)
                    if f % LORA_REP == LORA_REP - 1:
                        m = f // LORA_REP
                        dve.wait_ge(hid_done, f + 1)
                        nc.vector.tensor_reduce(hs[:, m, :], hid[:, m * LORA_REP:(m + 1) * LORA_REP, :]
                                                .rearrange("p j k -> p k j"), AX.X, ALU.add).then_inc(hs_done, 1)
                dve.wait_ge(hs_hi, 1)
                nc.vector.tensor_tensor(hs_s[1][:], hs[:], as_f32(hs_s[0][:]), ALU.subtract).then_inc(hs_lo, 1)
                for t in range(TT):
                    dve.wait_ge(y_done, t + 1)
                    nc.vector.tensor_tensor(x[:, t, :], x[:, t, :], ybank[t][:], ALU.add).then_inc(added, 1)


SH, SKV = 32, 8
SD = D // SH
SROWS = P // SD
SKW = SKV * SD


def self_attention(nc, tag, g, a):
    x, ident = g["x"], g["ident"]
    NJ = D // P
    with ExitStack() as ctx:
        s = Space(nc, ctx, tag)
        xT = s.pair("xT", [P, DC, TOK])
        bank = [s.ps(f"bank{i}") for i in range(4)]
        sbank = s.ps("sbank", 2)
        obank = s.ps("obank")
        ybank = s.ps("ybank")
        ln = LayerNormT(nc, s, x, ident, xT, bank[0:2])
        NWR = 3
        wraw = s.sb("wraw", [P, NWR, DC * D])
        ws = s.pair("ws", [P, NWR, DC * D])
        rope = s.sb("rope", [P, 2, SD])
        blocks = s.sb("blocks", [P, SROWS])
        causal = s.sb("causal", [P, SEQ])
        rot = s.sb("rot", [P, TT, SH + SKV, SD])
        q = s.sb("q", [P, TT, SH, SD])
        k = s.sb("k", [P, TT, SKV, SD])
        ko = s.sb("ko", [P, TT, NJ, SROWS, SD])
        v = s.sb("v", [P, TT, SKW])
        qT = s.sb("qT", [P, TT, NJ, P])
        kT = s.sb("kT", [P, NJ, SROWS, P])
        sc = s.sb("sc", [P, SH, SEQ])
        mx = s.sb("mx", [P, SH])
        sm = s.sb("sm", [P, TT, SH])
        pr = s.sb("pr", [P, SH, SEQ])
        prT = s.sb("prT", [P, SH, BT, SEQ])
        on = s.sb("on", [P, D])
        oT = s.pair("oT", [P, DC, P])

        loaded = [s.sem(f"loaded{i}") for i in range(NWR)]
        small_loaded = s.sem("small_loaded")
        w_hi, w_lo = s.sem("w_hi"), s.sem("w_lo")
        proj, roped = s.sem("proj"), s.sem("roped")
        v_read = s.sem("v_read")
        chain = s.sem("chain")
        q_tr, q_read = s.sem("q_tr"), s.sem("q_read")
        k_tr, k_read = s.sem("k_tr"), s.sem("k_read")
        s_done = s.sem("s_done")
        e_in, e_done = s.sem("e_in"), s.sem("e_done")
        zeroed, p_tr = s.sem("zeroed"), s.sem("p_tr")
        o_done, o_normed = s.sem("o_done"), s.sem("o_normed")
        o_tr, o_hi, o_lo = s.sem("o_tr"), s.sem("o_hi"), s.sem("o_lo")
        y_done, added = s.sem("y_done"), s.sem("added")

        with nc.Block() as block:
            @block.sync
            def _(sp):
                sp.dma_start(wraw[:, 0, :], a["s_wq"]).then_inc(loaded[0], 16)
                sp.dma_start(wraw[:, 1, 0:DC * 2 * SKW], a["s_wkv"]).then_inc(loaded[1], 16)
                sp.dma_start(rope[:], a["s_rope"]).then_inc(small_loaded, 16)
                sp.dma_start(blocks[:], a["s_blocks"]).then_inc(small_loaded, 16)
                sp.dma_start(causal[:], a["s_causal"]).then_inc(small_loaded, 16)
                sp.dma_start(wraw[:, 2, :], a["s_wo"]).then_inc(loaded[2], 16)

            @block.gpsimd
            def _(pool):
                nc.gpsimd.memset(prT[:], 0.0).then_inc(zeroed, 1)
                ln.gpsimd(pool)

            WIDTHS = [DC * D, DC * 2 * SKW, DC * D]

            @block.scalar
            def _(act):
                ln.scalar(act)
                for i, n in enumerate(WIDTHS):
                    act.wait_ge(loaded[i], 16)
                    nc.scalar.activation(ws[0][:, i, :n], wraw[:, i, :n], ACT.Copy).then_inc(w_hi, 1)
                for t in range(TT):
                    act.wait_ge(roped, t + 1)
                    nc.scalar.activation(v[:, t, :], bank[2 * t + 1][:, SKW:2 * SKW], ACT.Copy).then_inc(v_read, 1)
                for t in range(TT):
                    act.wait_ge(q_tr, t + 1)
                    nc.scalar.activation(qT[:, t, :, :], bank[2 * t][:, :].rearrange("p (j n) -> p j n", j=NJ),
                                         ACT.Copy).then_inc(q_read, 1)
                for t in range(TT):
                    act.wait_ge(e_in, t + 1)
                    need(act, p_tr, t)
                    nc.scalar.activation(pr[:], sc[:], ACT.Exp).then_inc(e_done, 1)
                    act.wait_ge(o_tr, t + 1)
                    need(act, y_done, t)
                    nc.scalar.activation(oT[0][:], obank[:, :].rearrange("p (c n) -> p c n", c=DC),
                                         ACT.Copy).then_inc(o_hi, 1)

            @block.tensor
            def _(pe):
                ln.tensor(pe)
                ln.wait_ready(pe)
                for t in range(TT):
                    for i, n in enumerate((D, 2 * SKW)):
                        pe.wait_ge(w_lo, i + 1)
                        for c in range(DC):
                            last = mm3(nc, bank[2 * t + i][:, 0:n], tuple(h[:, c, t * P:(t + 1) * P] for h in xT),
                                       tuple(w[:, i, c * n:(c + 1) * n] for w in ws), c == 0, c == DC - 1)
                    last.then_inc(proj, 1)
                for t in range(TT):
                    pe.wait_ge(roped, t + 1)
                    pe.wait_ge(v_read, t + 1)
                    for j in range(NJ):
                        last = nc.tensor.transpose(bank[2 * t][:, j * P:(j + 1) * P],
                                                   q[:, t, j * SROWS:(j + 1) * SROWS, :]
                                                   .rearrange("p h d -> p (h d)"), ident[:])
                    last.then_inc(q_tr, 1)
                    for j in range(NJ):
                        last = nc.tensor.transpose(bank[2 * t + 1][:, j * P:(j + 1) * P],
                                                   ko[:, t, j, :, :].rearrange("p h d -> p (h d)"), ident[:])
                    last.then_inc(k_tr, 1)
                for t in range(TT):
                    pe.wait_ge(q_read, t + 1)
                    pe.wait_ge(k_read, t + 1)
                    need(pe, e_in, t)
                    for j in range(NJ):
                        for b in range(BT):
                            last = nc.tensor.matmul(
                                sbank[b * SEQ:(b + 1) * SEQ, j * SROWS * SEQ:(j + 1) * SROWS * SEQ],
                                qT[:, t, j, b * SEQ:(b + 1) * SEQ], kT[:, j, :, b * SEQ:(b + 1) * SEQ],
                                start=True, stop=True)
                    last.then_inc(s_done, 1)
                    pe.wait_ge(p_tr, t + 1)
                    for h in range(SH):
                        kv = h // (SH // SKV)
                        last = nc.tensor.matmul(obank[:, h * SD:(h + 1) * SD],
                                                prT[:, h, :, :].rearrange("p b q -> p (b q)"),
                                                v[:, t, kv * SD:(kv + 1) * SD], start=True, stop=True)
                    last.then_inc(o_done, 1)
                    pe.wait_ge(o_normed, t + 1)
                    for c in range(DC):
                        last = nc.tensor.transpose(obank[:, c * P:(c + 1) * P], on[:, c * P:(c + 1) * P], ident[:])
                    last.then_inc(o_tr, 1)
                    pe.wait_ge(o_lo, t + 1)
                    pe.wait_ge(w_lo, NWR)
                    need(pe, added, t)
                    for c in range(DC):
                        last = mm3(nc, ybank[:], tuple(h[:, c, :] for h in oT),
                                   tuple(w[:, 2, c * D:(c + 1) * D] for w in ws), c == 0, c == DC - 1)
                    last.then_inc(y_done, 1)

            @block.vector
            def _(dve):
                links = [0]

                def link(ins):
                    ins.then_inc(chain, 1)
                    links[0] += 1
                    dve.wait_ge(chain, links[0])

                ln.vector(dve)
                for i, n in enumerate(WIDTHS):
                    dve.wait_ge(w_hi, i + 1)
                    nc.vector.tensor_tensor(ws[1][:, i, :n], wraw[:, i, :n], as_f32(ws[0][:, i, :n]),
                                            ALU.subtract).then_inc(w_lo, 1)
                dve.wait_ge(small_loaded, 48)
                H2 = SD // 2
                for t in range(TT):
                    dve.wait_ge(proj, t + 1)
                    for src, dst, heads, at in ((bank[2 * t][:, 0:D], q, SH, 0),
                                                (bank[2 * t + 1][:, 0:SKW], k, SKV, SH)):
                        halves = src.rearrange("p (h d) -> p h d", d=SD)

                        def table(i, lo, hi):
                            return rope[:, i, lo:hi].unsqueeze(1).broadcast_to([P, heads, hi - lo])
                        nc.vector.tensor_tensor(rot[:, t, at:at + heads, 0:H2], halves[:, :, H2:SD],
                                                table(1, 0, H2), ALU.mult)
                        nc.vector.tensor_tensor(rot[:, t, at:at + heads, H2:SD], halves[:, :, 0:H2],
                                                table(1, H2, SD), ALU.mult)
                        link(nc.vector.tensor_tensor(dst[:, t, :, :], halves, table(0, 0, SD), ALU.mult))
                        link(nc.vector.tensor_tensor(dst[:, t, :, :], dst[:, t, :, :],
                                                     rot[:, t, at:at + heads, :], ALU.add))
                    rep = SH // SKV
                    nc.vector.tensor_copy(
                        ko[:, t, :, :, :].rearrange("p j (g r) d -> p (j g) r d", r=rep),
                        k[:, t, :, :].unsqueeze(2).broadcast_to([P, SKV, rep, SD])).then_inc(roped, 1)
                for t in range(TT):
                    dve.wait_ge(k_tr, t + 1)
                    need(dve, s_done, t)
                    for j in range(NJ):
                        last = nc.vector.tensor_tensor(
                            kT[:, j, :, :],
                            bank[2 * t + 1][:, j * P:(j + 1) * P].unsqueeze(1).broadcast_to([P, SROWS, P]),
                            blocks[:, :].unsqueeze(2).broadcast_to([P, SROWS, P]), ALU.mult)
                    last.then_inc(k_read, 1)
                    dve.wait_ge(s_done, t + 1)
                    need(dve, e_done, t)
                    link(nc.vector.scalar_tensor_tensor(
                        out=sc[:], in0=sbank[:, :].rearrange("p (h n) -> p h n", h=SH), scalar=SD ** -0.5,
                        in1=causal[:, :].unsqueeze(1).broadcast_to([P, SH, SEQ]), op0=ALU.mult, op1=ALU.add))
                    link(nc.vector.tensor_reduce(mx[:], sc[:], AX.X, ALU.max))
                    nc.vector.tensor_tensor(sc[:], sc[:], mx[:, :].unsqueeze(2).broadcast_to([P, SH, SEQ]),
                                            ALU.subtract).then_inc(e_in, 1)
                    dve.wait_ge(e_done, t + 1)
                    link(nc.vector.tensor_reduce(sm[:, t, :], pr[:], AX.X, ALU.add))
                    link(nc.vector.reciprocal(sm[:, t, :], sm[:, t, :]))
                    dve.wait_ge(zeroed, 1)
                    need(dve, o_done, t)
                    for b in range(BT):
                        rows = slice(b * SEQ, (b + 1) * SEQ)
                        last = nc.vector.transpose(prT[rows, :, b, :], pr[rows, :, :])
                    last.then_inc(p_tr, 1)
                    dve.wait_ge(o_done, t + 1)
                    need(dve, o_tr, t)
                    nc.vector.tensor_tensor(on[:, :].rearrange("p (h d) -> p h d", h=SH),
                                            obank[:, :].rearrange("p (h d) -> p h d", h=SH),
                                            sm[:, t, :].unsqueeze(2).broadcast_to([P, SH, SD]),
                                            ALU.mult).then_inc(o_normed, 1)
                    dve.wait_ge(o_hi, t + 1)
                    nc.vector.tensor_tensor(oT[1][:], obank[:, :].rearrange("p (c n) -> p c n", c=DC),
                                            as_f32(oT[0][:]), ALU.subtract).then_inc(o_lo, 1)
                    dve.wait_ge(y_done, t + 1)
                    nc.vector.tensor_tensor(x[:, t, :], x[:, t, :], ybank[:], ALU.add).then_inc(added, 1)


EXPERTS = 16
SHARED_T = 4


def experts(nc, tag, g, a):
    x, ident = g["x"], g["ident"]
    NF = SHARED_T + EXPERTS
    assert SHARED_T == GatedTiles.RING and NF % GatedTiles.RING == 0
    E = EXPERTS
    with ExitStack() as ctx:
        s = Space(nc, ctx, tag)
        xT = s.pair("xT", [P, DC, TOK])
        tbank = [s.ps(f"tbank{i}") for i in range(2)]
        rbank = s.ps("rbank")
        ln = LayerNormT(nc, s, x, ident, xT, tbank)
        G = GatedTiles(nc, s, xT, NF)
        cbank = tbank
        rraw = s.sb("rraw", [P, DC, E])
        rw = s.pair("rw", [P, DC, E])
        rank = s.sb("rank", [P, E])
        mine = s.sb("mine", [E, E])
        ones = s.sb("ones", [E, P])
        nmx = s.sb("nmx", [P, TT])
        pe_ = s.sb("prob", [P, TT, E])
        tot = s.sb("tot", [P, TT])
        inv = s.sb("inv", [P, TT])
        prob = s.sb("p", [P, TT, E])
        rest = s.sb("rest", [P, TT, E])
        hot = s.sb("hot", [P, 2, TT, E])
        tmp = s.sb("tmp", [P, TT, E])
        best = s.sb("best", [P, 2, TT])
        top = s.sb("top", [P, TT])
        comb = s.sb("comb", [P, TT, E])
        combT = s.sb("combT", [E, TOK])
        diag = s.sb("diag", [E, E, TOK])

        r_loaded = s.sem("r_loaded")
        r_hi, r_lo = s.sem("r_hi"), s.sem("r_lo")
        ones_set = s.sem("ones_set")
        logits, nmx_done, exp_done = s.sem("logits"), s.sem("nmx_done"), s.sem("exp_done")
        chain = s.sem("chain")
        comb_done, comb_tr, comb_read = s.sem("comb_done"), s.sem("comb_tr"), s.sem("comb_read")
        diag_done = s.sem("diag_done")
        cast_done = s.sem("cast_done")
        added = s.sem("added")

        with nc.Block() as block:
            @block.sync
            def _(sp):
                sp.dma_start(rraw[:], a["e_router"]).then_inc(r_loaded, 16)
                sp.dma_start(rank[:], a["e_rank"]).then_inc(r_loaded, 16)
                sp.dma_start(mine[:], a["ident"][0:E, 0:E]).then_inc(r_loaded, 16)

                def step(i):
                    for k in range(G.RING):
                        f = G.RING * i + k
                        G.load(sp, a["e_w"][bass.ds(f, 1), :, :].rearrange("a p n -> p (a n)"), f, k)
                peeled(sp, NF // G.RING, step)

            @block.gpsimd
            def _(pool):
                ln.gpsimd(pool)
                nc.gpsimd.memset(ones[:], 1.0).then_inc(ones_set, 1)

            @block.tensor
            def _(pe):
                ln.tensor(pe)
                ln.wait_ready(pe)
                pe.wait_ge(ones_set, 1)
                pe.wait_ge(r_lo, 1)
                for t in range(TT):
                    for c in range(DC):
                        last = mm3(nc, rbank[:, t * E:(t + 1) * E], tuple(h[:, c, t * P:(t + 1) * P] for h in xT),
                                   tuple(w[:, c, :] for w in rw), c == 0, c == DC - 1)
                last.then_inc(logits, 1)

                def step(i):
                    for k in range(G.RING):
                        f = G.RING * i + k
                        if not is_at(i, 0):
                            e = f - SHARED_T
                            pe.wait_ge(diag_done, 1)
                            pe.wait_ge(G.a_done_sem, f - 1)
                            nc.tensor.matmul(cbank[k % 2][:, 0:TOK], ones[:],
                                             diag[:, bass.ds(e, 1), :].rearrange("p a n -> p (a n)"),
                                             start=True, stop=True).then_inc(cast_done, 1)
                        G.gate_up(pe, f, k)
                        if not is_at(f, 0):
                            G.down(pe, f - 1, (k - 1) % G.RING, is_at(f, 1), False)
                        if is_at(f, G.RING - 1):
                            for t in range(TT):
                                pe.wait_ge(comb_done, 1)
                                last = nc.tensor.transpose(rbank[0:E, t * P:(t + 1) * P], comb[:, t, :], ident[:])
                            last.then_inc(comb_tr, 1)
                peeled(pe, NF // G.RING, step)
                G.down(pe, NF - 1, (NF - 1) % G.RING, False, True)

            @block.scalar
            def _(act):
                act.wait_ge(r_loaded, 48)
                nc.scalar.activation(rw[0][:], rraw[:], ACT.Copy).then_inc(r_hi, 1)
                ln.scalar(act)
                G.gu_hi(act, 0, 0, 0)
                act.wait_ge(nmx_done, 1)
                for t in range(TT):
                    last = nc.scalar.activation(pe_[:, t, :], rbank[:, t * E:(t + 1) * E], ACT.Exp,
                                                bias=nmx[:, t:t + 1], accum_out=tot[:, t:t + 1])
                    last.then_inc(exp_done, 1)

                def step(i):
                    for k in range(G.RING):
                        f = G.RING * i + k
                        G.scalar(act, f, i, k, is_at(f, NF - 1))
                peeled(act, NF // G.RING, step)

            @block.vector
            def _(dve):
                links = [0]

                def link(ins):
                    ins.then_inc(chain, 1)
                    links[0] += 1
                    dve.wait_ge(chain, links[0])

                def wide(ap):
                    return ap.unsqueeze(2).broadcast_to([P, TT, E])

                ranks = rank[:, :].unsqueeze(1).broadcast_to([P, TT, E])
                ln.vector(dve)
                dve.wait_ge(r_hi, 1)
                nc.vector.tensor_tensor(rw[1][:], rraw[:], as_f32(rw[0][:]), ALU.subtract).then_inc(r_lo, 1)
                G.gu_lo(dve, 0, 0)
                dve.wait_ge(logits, 1)
                nc.vector.tensor_reduce(nmx[:], rbank[:, 0:TT * E].rearrange("p (t e) -> p t e", t=TT), AX.X,
                                        ALU.max, negate=True).then_inc(nmx_done, 1)
                dve.wait_ge(exp_done, TT)
                link(nc.vector.reciprocal(inv[:], tot[:]))
                link(nc.vector.tensor_tensor(prob[:], pe_[:], wide(inv[:, :]), ALU.mult))
                left = prob
                for r in range(2):
                    link(nc.vector.tensor_reduce(best[:, r, :], left[:], AX.X, ALU.max))
                    link(nc.vector.tensor_tensor(tmp[:], left[:], wide(best[:, r, :]), ALU.is_equal))
                    link(nc.vector.tensor_tensor(tmp[:], tmp[:], ranks, ALU.mult))
                    link(nc.vector.tensor_reduce(top[:], tmp[:], AX.X, ALU.max))
                    link(nc.vector.tensor_tensor(hot[:, r, :, :], tmp[:], wide(top[:, :]), ALU.is_equal))
                    if r == 0:
                        link(nc.vector.tensor_scalar(tmp[:], hot[:, 0, :, :], -2.0, None, ALU.mult))
                        link(nc.vector.tensor_tensor(rest[:], prob[:], tmp[:], ALU.add))
                        left = rest
                link(nc.vector.tensor_tensor(top[:], best[:, 0, :], best[:, 1, :], ALU.add))
                link(nc.vector.reciprocal(top[:], top[:]))
                link(nc.vector.tensor_tensor(hot[:, 0, :, :], hot[:, 0, :, :], wide(best[:, 0, :]), ALU.mult))
                link(nc.vector.tensor_tensor(hot[:, 1, :, :], hot[:, 1, :, :], wide(best[:, 1, :]), ALU.mult))
                link(nc.vector.tensor_tensor(tmp[:], hot[:, 0, :, :], hot[:, 1, :, :], ALU.add))
                nc.vector.tensor_tensor(comb[:], tmp[:], wide(top[:, :]), ALU.mult).then_inc(comb_done, 1)

                def step(i):
                    for k in range(G.RING):
                        f = G.RING * i + k
                        e = f - SHARED_T
                        combine = None if is_at(i, 0) else (cbank[k % 2][:, 0:TOK], cast_done, e + 1, e)
                        G.vector(dve, f, k, is_at(f, NF - 1), combine)
                        if is_at(f, G.RING - 1):
                            dve.wait_ge(comb_tr, 1)
                            nc.vector.tensor_copy(combT[:], rbank[0:E, 0:TOK]).then_inc(comb_read, 1)
                            dve.wait_ge(comb_read, 1)
                            nc.vector.tensor_tensor(diag[:], combT[:, :].unsqueeze(1).broadcast_to([E, E, TOK]),
                                                    mine[:, :].unsqueeze(2).broadcast_to([E, E, TOK]),
                                                    ALU.mult).then_inc(diag_done, 1)
                peeled(dve, NF // G.RING, step)
                dve.wait_ge(G.down_done_sem, NF)
                for t in range(TT):
                    nc.vector.tensor_tensor(x[:, t, :], x[:, t, :], G.ybank[t][:], ALU.add).then_inc(added, 1)


def build_program(nc, phases=99, **a):
    with ExitStack() as ctx:
        s = Space(nc, ctx, "g")
        x = s.sb("x", [P, TT, D])
        ident = s.sb("ident", [P, P])
        stage = s.sb("stage", [P, 2, DC * UW])
        g = {"x": x, "ident": ident, "stage": stage, "vlat_dram": a["vlat_dram"], "a": a}
        loaded = s.sem("loaded")
        stored = s.sem("stored")
        SEMAPHORES.clear()
        with nc.Block() as block:
            @block.sync
            def _(sp):
                sp.dma_start(x[:], a["x"].rearrange("(t p) d -> p t d", p=P)).then_inc(loaded, 16)
                sp.dma_start(ident[:], a["ident"]).then_inc(loaded, 16)
                sp.wait_ge(loaded, 32)
        L0 = {"wkv": a["l0_wkv"], "wq": a["l0_wq"], "wo": a["l0_wo"], "norm": a["l0_norm"], "ctx": a["ctx"], "mask": None}
        L1 = {"wkv": a["l1_wkv"], "wq": a["l1_wq"], "wo": a["l1_wo"], "norm": a["l1_norm"], "ctx": a["ctx"], "mask": a["mask"]}
        if phases >= 1:
            cross_attention(nc, "c0", g, L0, 1e-6, True)
            clear_semaphores(nc)
        if phases >= 2:
            mixer(nc, "m0", g, a)
            clear_semaphores(nc)
        if phases >= 3:
            lora_ffn(nc, "f0", g, a)
            clear_semaphores(nc)
        if phases >= 4:
            cross_attention(nc, "c1", g, L1, 1e-5, False)
            clear_semaphores(nc)
        if phases >= 5:
            self_attention(nc, "s1", g, a)
            clear_semaphores(nc)
        if phases >= 6:
            experts(nc, "e1", g, a)
        with nc.Block() as block:
            @block.sync
            def _(sp):
                sp.dma_start(a["out"].rearrange("(t p) d -> p t d", p=P), x[:]).then_inc(stored, 16)
                sp.wait_ge(stored, 16)


def lay_out(i):
    def c_major(w_cn):
        n = w_cn.shape[1]
        return w_cn.reshape(DC, P, n).transpose(1, 0, 2).reshape(P, DC * n)

    def halves(w_cn, width):
        return np.stack([c_major(w_cn[:, k:k + width]) for k in range(0, w_cn.shape[1], width)])

    def wkv(wk, wv):
        return np.concatenate([halves(wk, UW), halves(wv, UW)])

    def heads(wo):
        return wo.reshape(HEADS // GROUP, GROUP, HD, D).transpose(0, 2, 1, 3).reshape(HEADS // GROUP, P, GROUP * D)

    o = {"x": i["x"].reshape(TOK, D), "ident": np.eye(P, dtype=np.float32)}
    o["ctx"] = i["ctx_4096"].reshape(B, CT, P, DC, P).transpose(0, 4, 1, 3, 2).reshape(B, P, CT * DC * P)
    o["mask"] = i["mask_1x1xSxS2_ff0"].reshape(SEQ, CTX)
    o["l0_wkv"] = wkv(i["L0_xattn_Wk"], i["L0_xattn_Wv"])
    o["l0_wq"] = halves(i["L0_xattn_Wq"], UW)
    o["l0_wo"] = heads(i["L0_xattn_Wo"])
    o["l0_norm"] = np.stack([i["L0_xattn_q_norm_w"], i["L0_xattn_k_norm_w"]], 1)
    o["l1_wkv"] = wkv(i["L1_xattn_Wk"].T, i["L1_xattn_Wv"].T)
    o["l1_wq"] = halves(i["L1_xattn_Wq"].T, UW)
    o["l1_wo"] = heads(i["L1_xattn_Wo"].T)
    o["l1_norm"] = np.stack([i["L1_xattn_q_norm_w"], i["L1_xattn_k_norm_w"]], 1)
    return lay_out_rest(i, o)


def lay_out_rest(i, o):
    def tile_gud(gate, up, down):
        n = gate.shape[0]
        out = np.zeros((P, GatedTiles.WIDTH), np.float32)
        for part, w in enumerate((gate, up)):
            view = out[:, part * DC * P:(part + 1) * DC * P].reshape(P, DC, P)
            view[:, :, :n] = w.T.reshape(DC, P, n).transpose(1, 0, 2)
        out[:n, GatedTiles.GU:] = down.T
        return out

    def c_major(w_cn):
        n = w_cn.shape[1]
        return w_cn.reshape(DC, P, n).transpose(1, 0, 2).reshape(P, DC * n)

    gw, uw, dw = i["L0_attn_ffn_gate_w"], i["L0_attn_ffn_up_w"], i["L0_attn_ffn_down_w"]
    F = gw.shape[0]
    o["mix_ffn"] = np.stack([tile_gud(gw[k:k + P], uw[k:k + P], dw[:, k:k + P]) for k in range(0, F, P)])
    o["mix_proj"] = np.concatenate([c_major(i["L0_attn_gate_w"].T), c_major(i["L0_attn_up_w"].T)], 1)
    o["mix_point"] = i["L0_attn_local_point"].reshape(P, 1)
    o["mix_disc"] = i["L0_attn_discount_factor"]
    o["mix_out"] = np.concatenate([i["L0_attn_local_approx_output"].T[:, None, :],
                                   i["L0_attn_fuse_weight"].transpose(1, 2, 0)], 1)
    padded = LORA_M * P

    def by_tile(w):
        lead = w.shape[:-1]
        out = np.zeros(lead + (LORA_REP, padded), np.float32)
        out[..., :LORA_HQ] = w.reshape(lead + (LORA_REP, LORA_HQ))
        out = out.reshape(lead + (LORA_REP, LORA_M, P))
        return np.swapaxes(out, -3, -2).reshape(lead + (LORA_F * P,))

    o["lora_g"] = np.stack([by_tile(i["L0_ffn_w1q"].T), by_tile(i["L0_ffn_w3q"].T)], 1)
    d = np.zeros((padded, D), np.float32)
    d[:LORA_HQ] = i["L0_ffn_w2q"].T
    o["lora_d"] = d.reshape(LORA_M, P, D).transpose(1, 0, 2)
    la = np.zeros((D, P), np.float32)
    la[:, 0:LORA_R] = i["L0_ffn_a1"].T
    la[:, LORA_R:2 * LORA_R] = i["L0_ffn_a3"].T
    o["lora_a"] = la.reshape(DC, P, P).transpose(1, 0, 2)
    lb = np.zeros((2 * LORA_R, 2, LORA_F * P), np.float32)
    lb[0:LORA_R, 0] = by_tile(i["L0_ffn_b1"].T)
    lb[LORA_R:, 1] = by_tile(i["L0_ffn_b3"].T)
    o["lora_b"] = lb
    o["lora_a2"] = by_tile(i["L0_ffn_a2"]).reshape(LORA_R, LORA_F, P).transpose(2, 1, 0)
    o["lora_b2"] = i["L0_ffn_b2"].T
    o["s_wq"] = c_major(i["L1_attn_Wq"].T)
    o["s_wkv"] = c_major(np.concatenate([i["L1_attn_Wk"].T, i["L1_attn_Wv"].T], 1))
    o["s_wo"] = c_major(i["L1_attn_Wo"].T)
    o["s_rope"], o["s_blocks"], o["s_causal"] = tables()
    sg, su = np.split(i["L1_ffn_shared_w_gate_up"], 2)
    sd = i["L1_ffn_shared_w_down"]
    tiles = [tile_gud(sg[k:k + P], su[k:k + P], sd[:, k:k + P]) for k in range(0, SHARED_T * P, P)]
    for e in range(EXPERTS):
        eg, eu = np.split(i["L1_ffn_w_gate_up"][e], 2)
        tiles.append(tile_gud(eg, eu, i["L1_ffn_w_down"][e]))
    o["e_w"] = np.stack(tiles)
    o["e_router"] = i["L1_ffn_gate_w"].T.reshape(DC, P, EXPERTS).transpose(1, 0, 2)
    o["e_rank"] = np.tile(np.arange(EXPERTS, 0, -1, dtype=np.float32), (P, 1))
    return o


def tables():
    theta, factor, hi_f, lo_f, orig = 500000.0, 32.0, 4.0, 1.0, 1024
    f32 = np.float32
    inv = (f32(1.0) / f32(theta) ** (np.arange(0, SD, 2, dtype=f32) / f32(SD))).astype(f32)
    wavelen = (f32(2.0 * np.pi) / inv).astype(f32)
    base = np.where(wavelen > orig / lo_f, inv / f32(factor), inv).astype(f32)
    smooth = ((orig / wavelen - lo_f) / (hi_f - lo_f)).astype(f32)
    smoothed = ((1.0 - smooth) * base / f32(factor) + smooth * base).astype(f32)
    medium = ~(wavelen < orig / lo_f) & ~(wavelen > orig / hi_f)
    freqs = np.arange(SEQ, dtype=f32)[:, None] * np.where(medium, smoothed, base).astype(f32)[None, :]
    freqs = freqs.astype(f32)
    cos, sin = np.cos(freqs), np.sin(freqs)
    rope = np.stack([np.concatenate([cos, cos], 1), np.concatenate([-sin, sin], 1)], 1)
    rope = np.tile(rope, (BT, 1, 1)).astype(f32)
    blocks = (np.arange(P)[:, None] // SD == np.arange(SROWS)[None, :]).astype(f32)
    causal = np.where(np.arange(SEQ)[None, :] <= np.arange(SEQ)[:, None], 0.0, -3.0e38)
    return rope, blocks, np.tile(causal, (BT, 1)).astype(f32)


def kernel(**inputs):
    import concourse.bacc as bacc
    from concourse.bass_utils import run_bass_kernel_spmd

    given = {name: np.asarray(v) for name, v in inputs.items()}
    nc = bacc.Bacc("TRN2", target_bir_lowering=False, num_devices=1)
    arrays, aps = {}, {}
    for name, v in lay_out(given).items():
        v = np.ascontiguousarray(v)
        arrays[f"in_{name}"] = v
        aps[name] = nc.dram_tensor(f"in_{name}", v.shape, mybir.dt.from_np(v.dtype), kind="ExternalInput").ap()
    aps["vlat_dram"] = nc.dram_tensor("vlat_dram", (TOK, 2 * UW), F32).ap()
    aps["out"] = nc.dram_tensor("out_dram", (TOK, D), F32, kind="ExternalOutput").ap()
    build_program(nc, **aps)
    r = run_bass_kernel_spmd(nc, [arrays], core_ids=[0])
    return r.results[0]["out_dram"].reshape(B, SEQ, D)
```

```python
from contextlib import ExitStack

import numpy as np

import concourse.bass as bass
from concourse import mybir

ALU = mybir.AluOpType
ACT = mybir.ActivationFunctionType
AX = mybir.AxisListType
F32 = mybir.dt.float32
F32R = mybir.dt.float32r

P = 128
B, SEQ, D = 8, 32, 512
TOK = B * SEQ
TT = TOK // P
BT = P // SEQ
DC = D // P
CTX = 512
CT = CTX // P
HEADS, KVH, HD = 32, 8, 128
GROUP = HEADS // KVH
UNIT_H = 4
UNITS = B * KVH // UNIT_H
UW = UNIT_H * HD
TAYLOR = 6
TAYLOR_MIN, TAYLOR_KEEP = 4, 2.5
EPS_LN = 1e-5


def need(eng, sem, value):
    if isinstance(value, int) and value <= 0:
        return
    eng.wait_ge(sem, value)


def mm3(nc, out, a, b, start, stop):
    nc.tensor.matmul(out, a[0], b[1], start=start, stop=False)
    nc.tensor.matmul(out, a[0], b[0], start=False, stop=False)
    return nc.tensor.matmul(out, a[1], b[0], start=False, stop=stop)


def as_f32(ap):
    return ap.bitcast(F32)


SEMAPHORES = []


def clear_semaphores(nc):
    with nc.Block() as block:
        @block.gpsimd
        def _(pool):
            nc.clear_and_free_semaphores(list(SEMAPHORES))
    SEMAPHORES.clear()


class Space:

    def __init__(self, nc, ctx, tag):
        self.nc, self.ctx, self.tag = nc, ctx, tag

    def sb(self, name, shape, dt=F32):
        return self.ctx.enter_context(self.nc.sbuf_tensor(f"{self.tag}_{name}", shape, dt))

    def pair(self, name, shape):
        return self.sb(name + "_hi", shape, F32R), self.sb(name + "_lo", shape, F32R)

    def twins(self, name, shape):
        at = self.nc.sbuf_base
        raw = self.sb(name, shape)
        assert at % 32 == 0
        return raw, self.nc.alloc_sbuf_tensor_at(f"{self.tag}_{name}_r", shape, F32R, offset=at)

    def ps(self, name, banks=1):
        return self.ctx.enter_context(self.nc.psum_tensor(f"{self.tag}_{name}", [P, 512 * banks], F32))

    def sem(self, name):
        sem = self.nc.alloc_semaphore(f"{self.tag}_{name}")
        SEMAPHORES.append(sem)
        return sem


class LayerNormT:

    def __init__(self, nc, s, x, ident, xT, banks, xn=None):
        self.nc, self.x, self.ident, self.xT, self.banks = nc, x, ident, xT, banks
        self.stats = s.sb("ln_stats", [P, TT, 6])
        self.mv = s.sb("ln_mv", [P, TT, 2])
        self.rstd = s.sb("ln_rstd", [P, TT, 3])
        self.xn = xn if xn is not None else s.sb("ln_xn", [P, TT, D])
        self.stats_done = s.sem("ln_stats_done")
        self.mv_done = s.sem("ln_mv_done")
        self.eps_added = s.sem("ln_eps_added")
        self.rstd_done = s.sem("ln_rstd_done")
        self.normed = s.sem("ln_normed")
        self.transposed = s.sem("ln_transposed")
        self.hi_ready = s.sem("ln_hi_ready")
        self.lo_ready = s.sem("ln_lo_ready")

    def vector(self, dve, between=None):
        nc = self.nc
        for t in range(TT):
            nc.vector.bn_stats(self.stats[:, t, :], self.x[:, t, :]).then_inc(self.stats_done, 1)
        for t in range(TT):
            dve.wait_ge(self.stats_done, t + 1)
            nc.vector.bn_aggr(self.mv[:, t, :], self.stats[:, t, :]).then_inc(self.mv_done, 1)
        dve.wait_ge(self.rstd_done, 1)
        for t in range(TT):
            nc.vector.tensor_scalar(self.xn[:, t, :], self.x[:, t, :], self.mv[:, t, 0:1],
                                    self.rstd[:, t, 1:2], ALU.subtract, ALU.mult).then_inc(self.normed, 1)
        if between is not None:
            between()
        for t in range(TT):
            dve.wait_ge(self.hi_ready, t + 1)
            nc.vector.tensor_tensor(self.xT[1][:, :, t * P:(t + 1) * P],
                                    self.banks[t][:, :].rearrange("p (c k) -> p c k", c=DC),
                                    as_f32(self.xT[0][:, :, t * P:(t + 1) * P]),
                                    ALU.subtract).then_inc(self.lo_ready, 1)

    def gpsimd(self, pool):
        nc = self.nc
        nc.gpsimd.memset(self.rstd[:, :, 2:3], -0.5).then_inc(self.eps_added, 1)
        pool.wait_ge(self.mv_done, TT)
        nc.gpsimd.tensor_scalar(self.rstd[:, :, 0:1], self.mv[:, :, 1:2], EPS_LN, None,
                                ALU.add).then_inc(self.eps_added, 1)
        pool.wait_ge(self.eps_added, 2)
        nc.gpsimd.tensor_tensor(self.rstd[:, :, 1:2], self.rstd[:, :, 0:1], self.rstd[:, :, 2:3],
                                ALU.pow).then_inc(self.rstd_done, 1)

    def tensor(self, pe):
        for t in range(TT):
            pe.wait_ge(self.normed, t + 1)
            for c in range(DC):
                last = self.nc.tensor.transpose(self.banks[t][:, c * P:(c + 1) * P],
                                                self.xn[:, t, c * P:(c + 1) * P], self.ident[:])
            last.then_inc(self.transposed, 1)

    def scalar(self, act):
        for t in range(TT):
            act.wait_ge(self.transposed, t + 1)
            self.nc.scalar.activation(self.xT[0][:, :, t * P:(t + 1) * P],
                                      self.banks[t][:, :].rearrange("p (c k) -> p c k", c=DC),
                                      ACT.Copy).then_inc(self.hi_ready, 1)

    def wait_ready(self, pe):
        pe.wait_ge(self.lo_ready, TT)


class WeightStream:

    def __init__(self, nc, s, name, width, stage=None, split=None):
        self.nc, self.width = nc, width
        self.stage = stage if stage is not None else s.sb(name + "_stage", [P, 2, width])
        self.split = split if split is not None else s.pair(name, [P, 2, width])
        self.loaded = [s.sem(f"{name}_loaded{i}") for i in range(2)]
        self.hi_ready = s.sem(name + "_hi_ready")
        self.lo_ready = s.sem(name + "_lo_ready")

    def load(self, sp, src, pair, slot):
        need(sp, self.lo_ready, 2 * pair + slot - 1)
        sp.dma_start(self.stage[:, slot, :], src).then_inc(self.loaded[slot], 16)

    def make_hi(self, act, pair, slot, used, per_tile, width=None):
        w = width or self.width
        act.wait_ge(self.loaded[slot], pair * 16 + 16)
        need(act, used, per_tile * (2 * pair + slot - 1))
        self.nc.scalar.activation(self.split[0][:, slot, :w], self.stage[:, slot, :w],
                                  ACT.Copy).then_inc(self.hi_ready, 1)

    def make_lo(self, dve, pair, slot, width=None):
        w = width or self.width
        dve.wait_ge(self.hi_ready, 2 * pair + slot + 1)
        self.nc.vector.tensor_tensor(self.split[1][:, slot, :w], self.stage[:, slot, :w],
                                     as_f32(self.split[0][:, slot, :w]),
                                     ALU.subtract).then_inc(self.lo_ready, 1)

    def wait_tile(self, pe, pair, slot):
        pe.wait_ge(self.lo_ready, 2 * pair + slot + 1)

    def tile(self, slot):
        return self.split[0][:, slot, :], self.split[1][:, slot, :]


def peeled(eng, count, step):
    step(0)
    with eng.Fori(1, count - 1) as i:
        step(i)
    step(count - 1)


def is_at(i, value):
    return isinstance(i, int) and i == value


def cross_attention(nc, tag, g, w, eps, latents_as_keys):
    latents = latents_as_keys
    with ExitStack() as outer:
        so = Space(nc, outer, tag)
        qT = so.sb("qT", [P, B, HEADS, SEQ])
        with ExitStack() as inner:
            si = Space(nc, inner, tag)
            wkv_raw, wkv_lo = si.twins("wkv_lo", [P, 4, DC * UW])
            wkv = si.sb("wkv_hi", [P, 4, DC * UW], F32R), wkv_lo
            mask = si.sb("mask", [P, CTX]) if w["mask"] is not None else None
            klatT = si.sb("klatT", [P, KVH, TOK]) if latents else None
            vlat = si.sb("vlat", [SEQ, 2, UW]) if latents else None
            context = Context(nc, si, w["ctx"])
            wo = OutputWeights(nc, si, w["wo"], wkv, wkv_raw)
            queries(nc, tag + "q", g, w, eps, wkv, wkv_raw, qT, mask, klatT, context)
            attend(nc, tag + "a", g, w, eps, wkv, qT, mask, klatT, vlat, context, wo)
            project_out(nc, tag + "o", g, w, qT, wo)


class Context:

    def __init__(self, nc, s, src):
        self.nc, self.src = nc, src
        self.raw, lo = s.twins("cT_lo", [P, CT, DC * P])
        self.split = s.sb("cT_hi", [P, CT, DC * P], F32R), lo
        self.loaded = [s.sem(f"ctx_loaded{k}") for k in range(CT)]
        self.hi_ready = s.sem("ctx_hi")
        self.lo_ready = s.sem("ctx_lo")

    def load(self, sp, b, k):
        sp.dma_start(self.raw[:, k, :],
                     self.src[bass.ds(b, 1), :, k * DC * P:(k + 1) * DC * P].rearrange("b p n -> p (b n)")
                     ).then_inc(self.loaded[k], 16)

    def make_hi(self, act, b, k):
        act.wait_ge(self.loaded[k], 16 * b + 16)
        self.nc.scalar.activation(self.split[0][:, k, :], self.raw[:, k, :],
                                  ACT.Copy).then_inc(self.hi_ready, 1)

    def make_lo(self, dve, b, k):
        dve.wait_ge(self.hi_ready, CT * b + k + 1)
        self.nc.vector.tensor_tensor(self.split[1][:, k, :], self.raw[:, k, :],
                                     as_f32(self.split[0][:, k, :]), ALU.subtract).then_inc(self.lo_ready, 1)

    def wait_tile(self, pe, b, k):
        pe.wait_ge(self.lo_ready, CT * b + k + 1)


class OutputWeights:
    RING = 4
    PLACES = (0, 2, 1, 3)

    def __init__(self, nc, s, src, wkv, wkv_raw):
        self.nc, self.src, self.wkv, self.wkv_raw = nc, src, wkv, wkv_raw
        self.loaded = [s.sem(f"wo_loaded{i}") for i in range(self.RING)]
        self.hi_ready = s.sem("wo_hi")
        self.lo_ready = s.sem("wo_lo")

    def tile(self, n):
        return tuple(h[:, self.PLACES[n % self.RING], :] for h in self.wkv)

    def raw(self, n):
        return self.wkv_raw[:, self.PLACES[n % self.RING], :]

    def load(self, sp, n):
        sp.dma_start(self.raw(n), self.src[n]).then_inc(self.loaded[n % self.RING], 16)

    def make_hi(self, act, n):
        act.wait_ge(self.loaded[n % self.RING], 16 * (n // self.RING) + 16)
        self.nc.scalar.activation(self.tile(n)[0], self.raw(n), ACT.Copy).then_inc(self.hi_ready, 1)

    def make_lo(self, eng, n, subtract):
        eng.wait_ge(self.hi_ready, n + 1)
        hi, lo = self.tile(n)
        subtract(lo, self.raw(n), as_f32(hi), ALU.subtract).then_inc(self.lo_ready, 1)


def queries(nc, tag, g, w, eps, wkv, wkv_raw, qT, mask, klatT, context):
    x, ident = g["x"], g["ident"]
    NQ = HEADS // UNIT_H
    NL = 2 * TT if klatT is not None else 0
    N0 = NQ * TT
    NN = N0 + NL
    assert NQ // 2 == 4
    SLOTS, LAG = 4, 2
    with ExitStack() as ctx:
        s = Space(nc, ctx, tag)
        xT = s.pair("xT", [P, DC, TOK])
        tbank = [s.ps(f"tbank{i}") for i in range(2)]
        pbank = [s.ps(f"pbank{i}") for i in range(SLOTS)]
        xn = s.sb("xn", [P, SLOTS, UW])
        ln = LayerNormT(nc, s, x, ident, xT, tbank, xn[:, 0:TT, :])
        stream = WeightStream(nc, s, "w", DC * UW, stage=g["stage"])
        nk = s.sb("norm", [P, 4])
        sq = s.sb("sq", [P, 2, UW])
        ss = s.sb("ss", [P, SLOTS, UNIT_H])
        ms = s.sb("ms", [P, SLOTS, UNIT_H])
        rstd = s.sb("rstd", [P, SLOTS, UNIT_H])
        const = s.sb("const", [P, 2, UNIT_H])
        vl = s.sb("vl", [P, TT, 2 * UW]) if klatT is not None else None

        small_loaded = s.sem("small_loaded")
        wkv_hi = s.sem("wkv_hi")
        wkv_lo = s.sem("wkv_lo")
        wkv_loaded = s.sem("wkv_loaded")
        const_set = s.sem("const_set")
        norm_ready = s.sem("norm_ready")
        projected = s.sem("projected")
        squared = s.sem("squared")
        summed = s.sem("summed")
        meaned = s.sem("meaned")
        rstd_ready = s.sem("rstd_ready")
        normed = s.sem("normed")
        transposed = s.sem("transposed")
        placed = s.sem("placed")
        vl_proj = s.sem("vl_proj")
        vl_ready = s.sem("vl_ready")
        vl_stored = s.sem("vl_stored")

        WKH = DC * UW // 2

        def wkv_half(part, i, slot):
            return (*wkv, wkv_raw)[part][:, bass.ds(i, 1), slot * WKH:(slot + 1) * WKH]

        with nc.Block() as block:
            @block.sync
            def _(sp):
                sp.dma_start(nk[:, 0:2], w["norm"]).then_inc(small_loaded, 16)

                def step(i):
                    for slot in range(2):
                        stream.load(sp, w["wq"][bass.ds(2 * i + slot, 1), :, :]
                                    .rearrange("a p n -> p (a n)"), i, slot)
                        need(sp, wkv_loaded, 16 * (2 * i + slot))
                        sp.dma_start(wkv_half(2, i, slot).rearrange("p a n -> p (a n)"),
                                     w["wkv"][bass.ds(i, 1), :, slot * WKH:(slot + 1) * WKH]
                                     .rearrange("a p n -> p (a n)")).then_inc(wkv_loaded, 16)
                peeled(sp, NQ // 2, step)
                for k in range(CT):
                    context.load(sp, 0, k)
                if vl is not None:
                    sp.wait_ge(vl_ready, 2 * TT)
                    sp.dma_start(g["vlat_dram"].rearrange("(t p) n -> p t n", p=P),
                                 vl[:]).then_inc(vl_stored, 16)
                    sp.wait_ge(vl_stored, 16)

            @block.gpsimd
            def _(pool):
                ln.gpsimd(pool)
                nc.gpsimd.memset(const[:, 0, :], -0.5).then_inc(const_set, 1)
                nc.gpsimd.memset(const[:, 1, :], eps).then_inc(const_set, 1)

                def rstd_of(n, k):
                    pool.wait_ge(const_set, 2)
                    pool.wait_ge(summed, n + 1)
                    nc.gpsimd.tensor_tensor(ms[:, k, :], ss[:, k, :], const[:, 1, :],
                                            ALU.add).then_inc(meaned, 1)
                    pool.wait_ge(meaned, n + 1)
                    nc.gpsimd.tensor_tensor(rstd[:, k, :], ms[:, k, :], const[:, 0, :],
                                            ALU.pow).then_inc(rstd_ready, 1)
                peeled(pool, NQ // 2, lambda i: [rstd_of(SLOTS * i + k, k) for k in range(SLOTS)])
                for j in range(NL):
                    rstd_of(N0 + j, j)

            @block.tensor
            def _(pe):
                ln.tensor(pe)
                ln.wait_ready(pe)

                def project(t, wt, bank):
                    for c in range(DC):
                        a = tuple(h[:, c, t * P:(t + 1) * P] for h in xT)
                        last = mm3(nc, bank[:], a, tuple(h[:, c * UW:(c + 1) * UW] for h in wt),
                                   c == 0, c == DC - 1)
                    return last

                def transposes(n, k):
                    if isinstance(n, int) and n < 0:
                        return
                    pe.wait_ge(normed, n + 1)
                    need(pe, placed, n - 1)
                    for h in range(UNIT_H):
                        last = nc.tensor.transpose(tbank[k % 2][:, h * P:(h + 1) * P],
                                                   xn[:, k, h * P:(h + 1) * P], ident[:])
                    last.then_inc(transposed, 1)

                def step(i):
                    for slot in range(2):
                        stream.wait_tile(pe, i, slot)
                        for t in range(TT):
                            k = slot * TT + t
                            n = SLOTS * i + k
                            need(pe, normed, n - SLOTS + 1)
                            project(t, stream.tile(slot), pbank[k]).then_inc(projected, 1)
                            transposes(n - LAG, (k - LAG) % SLOTS)
                peeled(pe, NQ // 2, step)
                if vl is not None:
                    pe.wait_ge(wkv_lo, 8)
                    for j in range(NL):
                        half, t = divmod(j, TT)
                        pe.wait_ge(normed, N0 + j - SLOTS + 1)
                        project(t, tuple(h[:, half, :] for h in wkv), pbank[j]).then_inc(projected, 1)
                        transposes(N0 + j - LAG, (j - LAG) % SLOTS)
                    for j in range(2 * TT):
                        half, t = divmod(j, TT)
                        pe.wait_ge(normed, N0 + j + 1)
                        project(t, tuple(h[:, 2 + half, :] for h in wkv), pbank[j]).then_inc(vl_proj, 1)
                        if j < LAG:
                            transposes(NN - LAG + j, (NN - LAG + j) % SLOTS)
                    return
                for n in range(NN - LAG, NN):
                    transposes(n, n % SLOTS)

            @block.scalar
            def _(act):
                stream.make_hi(act, 0, 0, projected, TT)
                ln.scalar(act)

                def square(n, k):
                    act.wait_ge(projected, n + 1)
                    need(act, summed, n - 1)
                    nc.scalar.activation(sq[:, k % 2, :], pbank[k][:], ACT.Square, scale=HD ** -0.5).then_inc(squared, 1)

                def place_latents(j):
                    half, t = divmod(j, TT)
                    act.wait_ge(transposed, N0 + j + 1)
                    nc.scalar.activation(klatT[:, half * UNIT_H:(half + 1) * UNIT_H, t * P:(t + 1) * P],
                                         tbank[j % 2][:, :].rearrange("p (h k) -> p h k", h=UNIT_H),
                                         ACT.Copy).then_inc(placed, 1)

                def place_queries(i, k):
                    slot, t = divmod(k, TT)
                    act.wait_ge(transposed, SLOTS * i + k + 1)
                    nc.scalar.activation(
                        qT[:, t * BT:(t + 1) * BT, bass.ds((2 * i + slot) * UNIT_H, UNIT_H), :],
                        tbank[k % 2][:, :].rearrange("p (h b q) -> p b h q", h=UNIT_H, b=BT),
                        ACT.Copy, scale=nk[:, 3:4]).then_inc(placed, 1)

                act.wait_ge(norm_ready, 2)

                def step(i):
                    for slot in range(2):
                        if slot == 0:
                            stream.make_hi(act, i, 1, projected, TT)
                        elif not is_at(i, NQ // 2 - 1):
                            stream.make_hi(act, i + 1, 0, projected, TT)
                        for t in range(TT):
                            k = slot * TT + t
                            square(SLOTS * i + k, k)
                            if k >= LAG:
                                place_queries(i, k - LAG)
                            elif not is_at(i, 0):
                                place_queries(i - 1, k - LAG + SLOTS)
                        act.wait_ge(wkv_loaded, 16 * (2 * i + slot) + 16)
                        nc.scalar.activation(wkv_half(0, i, slot), wkv_half(2, i, slot),
                                             ACT.Copy).then_inc(wkv_hi, 1)
                peeled(act, NQ // 2, step)
                for j in range(max(NL, LAG)):
                    if NL:
                        square(N0 + j, j)
                        context.make_hi(act, 0, j)
                    if j < LAG:
                        place_queries(NQ // 2 - 1, SLOTS - LAG + j)
                    else:
                        place_latents(j - LAG)
                if NL:
                    for j in range(2 * TT):
                        half, t = divmod(j, TT)
                        act.wait_ge(vl_proj, j + 1)
                        nc.scalar.activation(vl[:, t, half * UW:(half + 1) * UW], pbank[j][:],
                                             ACT.Copy).then_inc(vl_ready, 1)
                        if j < LAG:
                            place_latents(NL - LAG + j)
                if not NL:
                    for k in range(CT):
                        context.make_hi(act, 0, k)

            @block.vector
            def _(dve):
                ln.vector(dve, lambda: stream.make_lo(dve, 0, 0))
                dve.wait_ge(small_loaded, 16)
                nc.vector.tensor_tensor(nk[:, 2:3], nk[:, 0:1], nk[:, 1:2], ALU.mult).then_inc(norm_ready, 1)
                dve.wait_ge(norm_ready, 1)
                nc.vector.tensor_scalar(nk[:, 3:4], nk[:, 2:3], HD ** -0.5, None,
                                        ALU.mult).then_inc(norm_ready, 1)

                def heads(ap):
                    return ap.rearrange("p (h d) -> p h d", h=UNIT_H)

                def sums(n, k):
                    dve.wait_ge(squared, n + 1)
                    need(dve, rstd_ready, n - SLOTS + 1)
                    nc.vector.tensor_reduce(ss[:, k, :], heads(sq[:, k % 2, :]), AX.X,
                                            ALU.add).then_inc(summed, 1)

                def normalise(n, k):
                    if isinstance(n, int) and n < 0:
                        return
                    dve.wait_ge(rstd_ready, n + 1)
                    need(dve, transposed, n - SLOTS + 1)
                    nc.vector.tensor_tensor(heads(xn[:, k, :]), heads(pbank[k][:, :]),
                                            rstd[:, k, :].unsqueeze(2).broadcast_to([P, UNIT_H, HD]),
                                            ALU.mult).then_inc(normed, 1)
                def step(i):
                    for slot in range(2):
                        if slot == 0:
                            stream.make_lo(dve, i, 1)
                        elif not is_at(i, NQ // 2 - 1):
                            stream.make_lo(dve, i + 1, 0)
                        for t in range(TT):
                            k = slot * TT + t
                            n = SLOTS * i + k
                            sums(n, k)
                            normalise(n - 1, (k - 1) % SLOTS)
                        dve.wait_ge(wkv_hi, 2 * i + slot + 1)
                        nc.vector.tensor_tensor(wkv_half(1, i, slot), wkv_half(2, i, slot),
                                                as_f32(wkv_half(0, i, slot)), ALU.subtract).then_inc(wkv_lo, 1)
                peeled(dve, NQ // 2, step)
                for n in range(N0, NN):
                    sums(n, n % SLOTS)
                    normalise(n - 1, (n - 1) % SLOTS)
                    context.make_lo(dve, 0, n - N0)
                normalise(NN - 1, (NN - 1) % SLOTS)
                if not NL:
                    for k in range(CT):
                        context.make_lo(dve, 0, k)


def attend(nc, tag, g, w, eps, wkv, qT, mask, klatT, vlat, context, wo):
    ident = g["ident"]
    tail = klatT is not None
    KEYS = CTX + (SEQ if tail else 0)
    with ExitStack() as ctx:
        s = Space(nc, ctx, tag)
        kT = (s.sb("kT_hi", [P, 2, UNIT_H, CTX], F32R),
              g["stage_r"][:, :, :].rearrange("p a (h n) -> p a h n", h=UNIT_H))
        v = s.sb("v", [P, 2, CT, UW])
        q = s.pair("q", [P, 2, UNIT_H, GROUP * SEQ])
        q_whole = s.sb("q_whole", [P, 2, UNIT_H, GROUP * SEQ]) if tail else None
        sq = s.sb("sq", [P, UW])
        kn = s.sb("kn", [P, 2, UW])
        ss = s.sb("ss", [P, 2, UNIT_H])
        ms = s.sb("ms", [P, 2, UNIT_H])
        rstd = s.sb("rstd", [P, 2, UNIT_H])
        const = s.sb("const", [P, 2, UNIT_H])
        sm = s.sb("sm", [P, 2, CTX]) if mask is not None else None
        smax = s.sb("smax", [P, CT])
        nmax = s.sb("nmax", [P, CT])
        rsum = s.sb("rsum", [P, CT])
        rinv = s.sb("rinv", [P, CT])
        p = s.sb("p", [P, 2, KEYS])
        pT = s.sb("pT", [P, 2, CT + 1, P])
        on = s.sb("on", [P, 2, HD])

        kbanks = s.ps("kbanks", 2)
        kbank = [kbanks[:, i * 512:(i + 1) * 512] for i in range(2)]
        vbank = s.ps("vbank")
        ktbank = s.ps("ktbank")
        sbank = s.ps("sbank", 2)
        ptbank = s.ps("ptbank")
        obank = s.ps("obank")
        TAIL_T = CTX + P
        OT = P

        const_set = s.sem("const_set")
        mask_loaded = s.sem("mask_loaded")
        k_proj = s.sem("k_proj")
        k_squared = s.sem("k_squared")
        k_summed = s.sem("k_summed")
        k_mean = s.sem("k_mean")
        k_rstd = s.sem("k_rstd")
        k_normed = s.sem("k_normed")
        kt_done = s.sem("kt_done")
        kt_hi = s.sem("kt_hi")
        kt_lo = s.sem("kt_lo")
        v_proj = s.sem("v_proj")
        v_ready = s.sem("v_ready")
        q_hi = s.sem("q_hi")
        q_lo = s.sem("q_lo")
        vlat_loaded = [s.sem(f"vlat_loaded{i}") for i in range(2)]
        s_done = s.sem("s_done")
        m_raw = s.sem("m_raw")
        m_done = s.sem("m_done")
        p_ready = s.sem("p_ready")
        pt_done = s.sem("pt_done")
        pt_ready = s.sem("pt_ready")
        o_done = s.sem("o_done")
        r_inv = s.sem("r_inv")
        o_normed = s.sem("o_normed")
        ot_done = s.sem("ot_done")
        ot_ready = s.sem("ot_ready")

        scores = [sbank, kbanks]
        ptbanks = [ptbank, vbank]
        obanks = [obank, ktbank]
        LAST = UNIT_H * (UNITS - 1)

        def run(eng, slot_step, finish):
            def both(b):
                slot_step(b, 0)
                slot_step(b, 1)
            peeled(eng, B, both)
            finish()

        def parts(b, hf):
            u = 2 * b + hf
            fixed = isinstance(u, int)
            return (not fixed or u > 0), (not fixed or u > 1), u

        with nc.Block() as block:
            @block.sync
            def _(sp):
                if mask is not None:
                    for h in range(GROUP):
                        sp.dma_start(mask[h * SEQ:(h + 1) * SEQ, :], w["mask"]).then_inc(mask_loaded, 16)

                def step(b, hf):
                    _, _, u = parts(b, hf)
                    if tail:
                        need(sp, o_done, UNIT_H * (u - 1))
                        sp.dma_start(vlat[:, hf, :],
                                     g["vlat_dram"][bass.ds(b * SEQ, SEQ), hf * UW:(hf + 1) * UW]
                                     ).then_inc(vlat_loaded[hf], 16)
                    if is_at(b, B - 1) and hf == 1:
                        sp.wait_ge(v_proj, CT * u)
                        for n in range(2):
                            wo.load(sp, n)
                    if hf == 1 and not is_at(b, B - 1):
                        for k in range(CT):
                            sp.wait_ge(v_proj, CT * u + k + 1)
                            context.load(sp, b + 1, k)

                def finish():
                    sp.wait_ge(v_proj, CT * UNITS)
                    for n in range(2, wo.RING):
                        wo.load(sp, n)
                run(sp, step, finish)

            @block.gpsimd
            def _(pool):
                nc.gpsimd.memset(const[:, 0, :], -0.5).then_inc(const_set, 1)
                nc.gpsimd.memset(const[:, 1, :], eps).then_inc(const_set, 1)

                def step(b, hf):
                    _, _, u = parts(b, hf)
                    mine = qT[:, bass.ds(b, 1), hf * 16:(hf + 1) * 16, :].rearrange("p b h q -> p (b h q)")

                    def flat(ap):
                        return ap[:, hf, :, :].rearrange("p h n -> p (h n)")
                    need(pool, s_done, UNIT_H * (u - 1))
                    if tail:
                        nc.gpsimd.tensor_copy(flat(q_whole), mine)
                    nc.gpsimd.tensor_copy(flat(q[0]), mine).then_inc(q_hi, 1)
                    for k in range(CT):
                        n = CT * u + k
                        pool.wait_ge(const_set, 2)
                        if k == 0:
                            pool.wait_ge(q_hi, u + 1)
                        pool.wait_ge(k_summed, n + 1)
                        nc.gpsimd.tensor_tensor(ms[:, k % 2, :], ss[:, k % 2, :], const[:, 1, :],
                                                ALU.add).then_inc(k_mean, 1)
                        pool.wait_ge(k_mean, n + 1)
                        nc.gpsimd.tensor_tensor(rstd[:, k % 2, :], ms[:, k % 2, :], const[:, 0, :],
                                                ALU.pow).then_inc(k_rstd, 1)
                        if k == 0:
                            nc.gpsimd.tensor_tensor(flat(q[1]), mine, as_f32(flat(q[0])),
                                                    ALU.subtract).then_inc(q_lo, 1)

                def finish():
                    for n in range(2):
                        wo.make_lo(pool, n, nc.gpsimd.tensor_tensor)
                run(pool, step, finish)

            @block.tensor
            def _(pe):
                def project(k, col, bank):
                    for c in range(DC):
                        a = tuple(h[:, k, c * P:(c + 1) * P] for h in context.split)
                        last = mm3(nc, bank[:, :], a, tuple(h[:, col, c * UW:(c + 1) * UW] for h in wkv),
                                   c == 0, c == DC - 1)
                    return last

                def score(a, bank, ahf, k, at):
                    last = mm3(nc, bank[:, 0:CTX], tuple(h[:, ahf, k, :] for h in q),
                               tuple(h[:, ahf, k, :] for h in kT), True, True)
                    if tail:
                        last = nc.tensor.matmul(bank[:, CTX:KEYS], q_whole[:, ahf, k, :],
                                                klatT[:, ahf * UNIT_H + k, bass.ds(at, SEQ)],
                                                start=True, stop=True)
                    last.then_inc(s_done, 1)

                def p_transpose(k, bank, tail_bank):
                    for t in range(CT):
                        last = nc.tensor.transpose(bank[:, t * P:(t + 1) * P],
                                                   p[:, k % 2, t * P:(t + 1) * P], ident[:])
                    if tail:
                        last = nc.tensor.transpose(tail_bank[0:SEQ, TAIL_T:TAIL_T + P],
                                                   p[:, k % 2, CTX:KEYS], ident[:])
                    last.then_inc(pt_done, 1)

                def pv(a, ahf, k, bank):
                    pe.wait_ge(pt_ready, a + 1)
                    for t in range(CT):
                        last = nc.tensor.matmul(bank[:, 0:HD], pT[:, k % 2, t, :],
                                                v[:, ahf, t, k * HD:(k + 1) * HD],
                                                start=(t == 0), stop=(t == CT - 1 and not tail))
                    if tail:
                        last = nc.tensor.matmul(bank[:, 0:HD], pT[0:SEQ, k % 2, CT, :],
                                                vlat[:, ahf, k * HD:(k + 1) * HD], start=False, stop=True)
                    last.then_inc(o_done, 1)

                def o_transpose(a, k, bank):
                    pe.wait_ge(o_normed, a + 1)
                    nc.tensor.transpose(bank[:, OT:OT + P], on[:, k % 2, :], ident[:]).then_inc(ot_done, 1)

                def kt(n, kb):
                    pe.wait_ge(k_normed, n + 1)
                    need(pe, kt_lo, n)
                    for h in range(UNIT_H):
                        last = nc.tensor.transpose(ktbank[:, h * P:(h + 1) * P],
                                                   kn[:, kb, h * P:(h + 1) * P], ident[:])
                    last.then_inc(kt_done, 1)

                def wait_unit(u, ahf, b_loads):
                    pe.wait_ge(kt_lo, CT * u)
                    pe.wait_ge(q_lo, u)
                    pe.wait_ge(v_ready, CT * u)
                    if tail:
                        pe.wait_ge(vlat_loaded[ahf], 16 * b_loads)

                def step(b, hf):
                    attends, lags, u = parts(b, hf)
                    ahf = 1 - hf
                    for k in range(CT):
                        n = CT * u + k
                        a = n - UNIT_H
                        lag = attends and (lags or k > 0)
                        if hf == 0:
                            context.wait_tile(pe, b, k)
                        need(pe, k_normed, n - 1)
                        project(k, hf, kbank[k % 2]).then_inc(k_proj, 1)
                        if lag:
                            need(pe, ot_ready, a - 1)
                            pv(a - 1, ahf if k else hf, (k - 1) % UNIT_H, obank)
                        if attends:
                            if k == 0:
                                wait_unit(u, ahf, b if hf == 0 else b + 1)
                            need(pe, p_ready, a)
                            need(pe, pt_ready, a)
                            score(a, sbank, ahf, k, (b - 1 if hf == 0 else b) * SEQ)
                        need(pe, v_ready, n)
                        project(k, 2 + hf, vbank).then_inc(v_proj, 1)
                        if attends:
                            pe.wait_ge(p_ready, a + 1)
                            p_transpose(k, ptbank, sbank)
                        kt(n, k % 2)
                        if lag:
                            o_transpose(a - 1, (k - 1) % 2, obank)

                def finish():
                    at = (B - 1) * SEQ
                    pe.wait_ge(ot_ready, LAST - 1)
                    pv(LAST - 1, 0, UNIT_H - 1, obank)
                    wait_unit(UNITS, 1, B)
                    pe.wait_ge(p_ready, LAST)
                    pe.wait_ge(pt_ready, LAST)
                    for k in range(2):
                        score(LAST + k, scores[k], 1, k, at)
                    o_transpose(LAST - 1, 1, obank)
                    for pair in range(0, UNIT_H, 2):
                        for k in (pair, pair + 1):
                            pe.wait_ge(p_ready, LAST + k + 1)
                            p_transpose(k, ptbanks[k % 2], scores[k % 2])
                        for k in (pair, pair + 1):
                            pe.wait_ge(ot_ready, LAST + max(0, k - 1))
                            pv(LAST + k, 1, k, obanks[k % 2])
                            if k + 2 < UNIT_H:
                                score(LAST + k + 2, scores[k % 2], 1, k + 2, at)
                        for k in (pair, pair + 1):
                            o_transpose(LAST + k, k, obanks[k % 2])
                run(pe, step, finish)

            @block.scalar
            def _(act):
                def place_k(n, kb, kk, u):
                    act.wait_ge(kt_done, n + 1)
                    need(act, s_done, UNIT_H * (u - 1))
                    nc.scalar.activation(kT[0][:, kb, :, kk * P:(kk + 1) * P],
                                         ktbank[:, :].rearrange("p (h n) -> p h n", h=UNIT_H),
                                         ACT.Copy).then_inc(kt_hi, 1)

                def exponential(a, k, bank):
                    act.wait_ge(m_done, a + 1)
                    need(act, pt_done, a - 1)
                    src = sm[:, k % 2, :] if mask is not None else bank[:, 0:KEYS]
                    nc.scalar.activation(p[:, k % 2, :], src, ACT.Exp, bias=nmax[:, k:k + 1],
                                         accum_out=rsum[:, k:k + 1]).then_inc(p_ready, 1)

                def step(b, hf):
                    attends, _, u = parts(b, hf)
                    for k in range(CT):
                        n = CT * u + k
                        act.wait_ge(k_proj, n + 1)
                        need(act, k_summed, n)
                        nc.scalar.activation(sq[:], kbank[k % 2], ACT.Square, scale=HD ** -0.5).then_inc(k_squared, 1)
                        if attends:
                            exponential(n - UNIT_H, k, sbank)
                        act.wait_ge(v_proj, n + 1)
                        need(act, o_done, UNIT_H * (u - 1))
                        nc.scalar.activation(v[:, hf, k, :], vbank[:], ACT.Copy).then_inc(v_ready, 1)
                        place_k(n, hf, k, u)
                        if hf == 1 and k > 0 and not is_at(b, B - 1):
                            context.make_hi(act, b + 1, k - 1)
                        if hf == 0 and k == 0 and not is_at(b, 0):
                            context.make_hi(act, b, CT - 1)

                def finish():
                    for k in range(UNIT_H):
                        exponential(LAST + k, k, scores[k % 2])
                        if k % 2:
                            wo.make_hi(act, k // 2)
                run(act, step, finish)

            @block.vector
            def _(dve):
                def lo_of_k(n, kb, kk):
                    dve.wait_ge(kt_hi, n + 1)
                    nc.vector.tensor_tensor(kT[1][:, kb, :, kk * P:(kk + 1) * P],
                                            ktbank[:, :].rearrange("p (h n) -> p h n", h=UNIT_H),
                                            as_f32(kT[0][:, kb, :, kk * P:(kk + 1) * P]),
                                            ALU.subtract).then_inc(kt_lo, 1)

                def inverse_sum(k):
                    nc.vector.reciprocal(rinv[:, k:k + 1], rsum[:, k:k + 1]).then_inc(r_inv, 1)

                def maximum(a, k, bank):
                    if mask is None:
                        nc.vector.tensor_reduce(nmax[:, k:k + 1], bank[:, 0:KEYS], AX.X, ALU.max,
                                                negate=True).then_inc(m_done, 1)
                    else:
                        nc.vector.tensor_tensor_reduce(
                            out=sm[:, k % 2, :], in0=bank[:, 0:CTX], in1=mask[:], scale=1.0, scalar=-3.4e38,
                            op0=ALU.add, op1=ALU.max, accum_out=smax[:, k:k + 1]).then_inc(m_raw, 1)
                        dve.wait_ge(m_raw, a + 1)
                        nc.vector.tensor_scalar(nmax[:, k:k + 1], smax[:, k:k + 1], -1.0, None,
                                                ALU.mult).then_inc(m_done, 1)

                def o_norm(a, kk, bank):
                    dve.wait_ge(o_done, a + 1)
                    dve.wait_ge(r_inv, a + 1)
                    need(dve, ot_done, a - 1)
                    nc.vector.tensor_scalar(on[:, kk % 2, :], bank[:, 0:HD], rinv[:, kk:kk + 1], None,
                                            ALU.mult).then_inc(o_normed, 1)

                def pt_copy(a, k, bank, tail_bank):
                    dve.wait_ge(pt_done, a + 1)
                    need(dve, o_done, a - 1)
                    last = nc.vector.tensor_copy(pT[:, k % 2, 0:CT, :],
                                                 bank[:, :].rearrange("p (t n) -> p t n", t=CT))
                    if tail:
                        last = nc.vector.tensor_copy(pT[0:SEQ, k % 2, CT, :], tail_bank[0:SEQ, TAIL_T:TAIL_T + P])
                    last.then_inc(pt_ready, 1)

                def ot_place(a, b, hf, kk, bank):
                    dve.wait_ge(ot_done, a + 1)
                    nc.vector.tensor_copy(
                        qT[:, bass.ds(b, 1), (hf * UNIT_H + kk) * GROUP:(hf * UNIT_H + kk + 1) * GROUP, :]
                        .rearrange("p b h q -> p (b h q)"),
                        bank[:, OT:OT + P]).then_inc(ot_ready, 1)

                def step(b, hf):
                    attends, lags, u = parts(b, hf)
                    for k in range(CT):
                        n = CT * u + k
                        a = n - UNIT_H
                        lag = attends and (lags or k > 0)
                        if k:
                            lb, lhf, lk = (b, 0, k - 1) if hf == 1 else (b - 1, 1, k - 1)
                        else:
                            lb, lhf, lk = b - 1, hf, CT - 1
                        dve.wait_ge(k_squared, n + 1)
                        nc.vector.tensor_reduce(ss[:, k % 2, :],
                                                sq[:, :].rearrange("p (h d) -> p h d", h=UNIT_H),
                                                AX.X, ALU.add).then_inc(k_summed, 1)
                        if attends:
                            if mask is not None:
                                dve.wait_ge(mask_loaded, 16 * GROUP)
                            dve.wait_ge(s_done, a + 1)
                            need(dve, p_ready, a)
                        if lag:
                            inverse_sum(lk)
                        if attends:
                            maximum(a, k, sbank)
                        if lag:
                            o_norm(a - 1, lk, obank)
                        dve.wait_ge(k_rstd, n + 1)
                        need(dve, kt_done, n - 1)
                        nc.vector.tensor_tensor(
                            kn[:, k % 2, :].rearrange("p (h d) -> p h d", h=UNIT_H),
                            kbank[k % 2].rearrange("p (h d) -> p h d", h=UNIT_H),
                            rstd[:, k % 2, :].unsqueeze(2).broadcast_to([P, UNIT_H, HD]),
                            ALU.mult).then_inc(k_normed, 1)
                        if attends:
                            pt_copy(a, k, ptbank, sbank)
                        lo_of_k(n, hf, k)
                        if lag:
                            ot_place(a - 1, lb, lhf, lk, obank)
                        if hf == 1 and k > 0 and not is_at(b, B - 1):
                            context.make_lo(dve, b + 1, k - 1)
                        if hf == 0 and k == 0 and not is_at(b, 0):
                            context.make_lo(dve, b, CT - 1)

                def finish():
                    dve.wait_ge(p_ready, LAST)
                    inverse_sum(UNIT_H - 1)
                    o_norm(LAST - 1, UNIT_H - 1, obank)
                    for k in range(2):
                        dve.wait_ge(s_done, LAST + k + 1)
                        maximum(LAST + k, k, scores[k])
                    ot_place(LAST - 1, B - 1, 0, UNIT_H - 1, obank)
                    for pair in range(0, UNIT_H, 2):
                        for k in (pair, pair + 1):
                            pt_copy(LAST + k, k, ptbanks[k % 2], scores[k % 2])
                        for k in (pair, pair + 1):
                            dve.wait_ge(p_ready, LAST + k + 1)
                            inverse_sum(k)
                            if k + 2 < UNIT_H:
                                dve.wait_ge(s_done, LAST + k + 3)
                                maximum(LAST + k + 2, k + 2, scores[k % 2])
                            o_norm(LAST + k, k, obanks[k % 2])
                        for k in (pair, pair + 1):
                            ot_place(LAST + k, B - 1, 1, k, obanks[k % 2])
                    dve.wait_ge(ot_ready, LAST + UNIT_H)
                run(dve, step, finish)


def project_out(nc, tag, g, w, oT, wo):
    x = g["x"]
    NW = HEADS // GROUP
    SPLIT = 2
    with ExitStack() as ctx:
        s = Space(nc, ctx, tag)
        o = s.pair("o", [P, 2, GROUP, TOK])
        ybank = [s.ps(f"ybank{t}") for t in range(TT)]
        o_hi = s.sem("o_hi")
        o_lo = s.sem("o_lo")
        used = s.sem("used")
        added = s.sem("added")

        def heads_of(n):
            return oT[:, :, n * GROUP:(n + 1) * GROUP, :].rearrange("p b h q -> p h b q")

        def split_of(half, n):
            return half[:, n % 2, :, :].rearrange("p h (b q) -> p h b q", b=B)

        with nc.Block() as block:
            @block.sync
            def _(sp):
                for n in range(wo.RING, NW):
                    sp.wait_ge(used, n - wo.RING + 1)
                    wo.load(sp, n)

            @block.scalar
            def _(act):
                for n in range(NW):
                    need(act, used, n - 1)
                    nc.scalar.activation(split_of(o[0], n), heads_of(n), ACT.Copy).then_inc(o_hi, 1)
                    if n >= SPLIT:
                        wo.make_hi(act, n)

            @block.vector
            def _(dve):
                for n in range(NW):
                    dve.wait_ge(o_hi, n + 1)
                    nc.vector.tensor_tensor(split_of(o[1], n), heads_of(n), as_f32(split_of(o[0], n)),
                                            ALU.subtract).then_inc(o_lo, 1)
                    if n >= SPLIT:
                        wo.make_lo(dve, n, nc.vector.tensor_tensor)
                dve.wait_ge(used, NW)
                for t in range(TT):
                    nc.vector.tensor_tensor(x[:, t, :], x[:, t, :], ybank[t][:], ALU.add).then_inc(added, 1)
                dve.wait_ge(added, TT)

            @block.tensor
            def _(pe):
                for n in range(NW):
                    pe.wait_ge(o_lo, n + 1)
                    pe.wait_ge(wo.lo_ready, n + 1)
                    wt = wo.tile(n)
                    for h in range(GROUP):
                        for t in range(TT):
                            last = mm3(nc, ybank[t][:],
                                       tuple(half[:, n % 2, h, t * P:(t + 1) * P] for half in o),
                                       tuple(half[:, h * D:(h + 1) * D] for half in wt),
                                       n == 0 and h == 0, n == NW - 1 and h == GROUP - 1)
                    last.then_inc(used, 1)


class GatedTiles:
    RING = 4
    GU = 2 * DC * P
    WIDTH = GU + D

    def __init__(self, nc, s, xT, tiles):
        self.nc, self.xT, self.tiles = nc, xT, tiles
        self.stage = s.sb("stage", [P, self.RING, self.WIDTH])
        self.gu = s.pair("gu", [P, 2, self.GU])
        self.dn = s.pair("dn", [P, 2, D])
        self.sg = s.sb("sg", [P, 2, TOK])
        self.a = s.sb("a", [P, 2, TOK])
        self.raw = s.sb("raw", [P, TOK])
        self.act = s.pair("act", [P, 2, TOK])
        self.gubank = [s.ps(f"gubank{i}") for i in range(2)]
        self.ybank = [s.ps(f"ybank{i}") for i in range(TT)]
        self.loaded = [s.sem(f"loaded{i}") for i in range(self.RING)]
        self.gu_hi_sem = s.sem("gu_hi")
        self.gu_lo_sem = s.sem("gu_lo")
        self.dn_hi_sem = s.sem("dn_hi")
        self.dn_lo_sem = s.sem("dn_lo")
        self.gu_done_sem = s.sem("gu_done")
        self.silu_done_sem = s.sem("silu_done")
        self.a_raw_sem = s.sem("a_raw")
        self.a_done_sem = s.sem("a_done")
        self.act_hi_sem = s.sem("act_hi")
        self.act_lo_sem = s.sem("act_lo")
        self.down_done_sem = s.sem("down_done")

    def load(self, sp, src, f, k):
        need(sp, self.dn_lo_sem, f - self.RING + 1)
        sp.dma_start(self.stage[:, k, :], src).then_inc(self.loaded[k], 16)

    def gu_hi(self, act, f, i, k):
        act.wait_ge(self.loaded[k], i * 16 + 16)
        need(act, self.gu_done_sem, f - 1)
        self.nc.scalar.activation(self.gu[0][:, k % 2, :], self.stage[:, k, :self.GU],
                                  ACT.Copy).then_inc(self.gu_hi_sem, 1)

    def gu_lo(self, dve, f, k):
        dve.wait_ge(self.gu_hi_sem, f + 1)
        self.nc.vector.tensor_tensor(self.gu[1][:, k % 2, :], self.stage[:, k, :self.GU],
                                     as_f32(self.gu[0][:, k % 2, :]), ALU.subtract).then_inc(self.gu_lo_sem, 1)

    def scalar(self, act, f, i, k, last):
        nc, h = self.nc, k % 2
        if not last:
            self.gu_hi(act, f + 1, i + (k + 1) // self.RING, (k + 1) % self.RING)
        act.wait_ge(self.gu_done_sem, f + 1)
        need(act, self.a_done_sem, f - 1)
        nc.scalar.activation(self.sg[:, h, :], self.gubank[h][:, 0:TOK], ACT.Silu).then_inc(self.silu_done_sem, 1)
        need(act, self.down_done_sem, f - 1)
        nc.scalar.activation(self.dn[0][:, h, :], self.stage[:, k, self.GU:], ACT.Copy).then_inc(self.dn_hi_sem, 1)
        act.wait_ge(self.a_done_sem, f + 1)
        nc.scalar.activation(self.act[0][:, h, :], self.a[:, h, :], ACT.Copy).then_inc(self.act_hi_sem, 1)

    def vector(self, dve, f, k, last, combine=None):
        nc, h = self.nc, k % 2
        if not last:
            self.gu_lo(dve, f + 1, (k + 1) % self.RING)
        dve.wait_ge(self.silu_done_sem, f + 1)
        need(dve, self.act_hi_sem, f - 1)
        if combine is None:
            nc.vector.tensor_tensor(self.a[:, h, :], self.sg[:, h, :], self.gubank[h][:, TOK:2 * TOK],
                                    ALU.mult).then_inc(self.a_done_sem, 1)
        else:
            bank, sem, value, before = combine
            nc.vector.tensor_tensor(self.raw[:], self.sg[:, h, :], self.gubank[h][:, TOK:2 * TOK],
                                    ALU.mult).then_inc(self.a_raw_sem, 1)
            dve.wait_ge(sem, value)
            dve.wait_ge(self.a_raw_sem, before + 1)
            nc.vector.tensor_tensor(self.a[:, h, :], self.raw[:], bank, ALU.mult).then_inc(self.a_done_sem, 1)
        dve.wait_ge(self.dn_hi_sem, f + 1)
        nc.vector.tensor_tensor(self.dn[1][:, h, :], self.stage[:, k, self.GU:], as_f32(self.dn[0][:, h, :]),
                                ALU.subtract).then_inc(self.dn_lo_sem, 1)
        dve.wait_ge(self.act_hi_sem, f + 1)
        nc.vector.tensor_tensor(self.act[1][:, h, :], self.a[:, h, :], as_f32(self.act[0][:, h, :]),
                                ALU.subtract).then_inc(self.act_lo_sem, 1)

    def gate_up(self, pe, f, k):
        nc, h = self.nc, k % 2
        pe.wait_ge(self.gu_lo_sem, f + 1)
        need(pe, self.a_done_sem, f - 1)
        for part in range(2):
            for c in range(DC):
                at = (part * DC + c) * P
                last = mm3(nc, self.gubank[h][:, part * TOK:(part + 1) * TOK],
                           tuple(w[:, h, at:at + P] for w in self.gu),
                           tuple(v[:, c, :] for v in self.xT), c == 0, c == DC - 1)
        last.then_inc(self.gu_done_sem, 1)

    def down(self, pe, f, k, start, stop):
        nc, h = self.nc, k % 2
        pe.wait_ge(self.act_lo_sem, f + 1)
        pe.wait_ge(self.dn_lo_sem, f + 1)
        for t in range(TT):
            last = mm3(nc, self.ybank[t][:], tuple(v[:, h, t * P:(t + 1) * P] for v in self.act),
                       tuple(w[:, h, :] for w in self.dn), start, stop)
        last.then_inc(self.down_done_sem, 1)


def split_tile(nc, act=None, dve=None, dst=None, src=None, hi_done=None, lo_done=None):
    if act is not None:
        nc.scalar.activation(dst[0], src, ACT.Copy).then_inc(hi_done, 1)
    else:
        nc.vector.tensor_tensor(dst[1], src, as_f32(dst[0]), ALU.subtract).then_inc(lo_done, 1)


def mixer(nc, tag, g, a):
    x, ident = g["x"], g["ident"]
    NF = a["mix_ffn"].shape[0]
    NT = TAYLOR + 1
    with ExitStack() as ctx:
        s = Space(nc, ctx, tag)
        xT = s.pair("xT", [P, DC, TOK])
        tbank = [s.ps(f"tbank{i}") for i in range(2)]
        ln = LayerNormT(nc, s, x, ident, xT, tbank)
        G = GatedTiles(nc, s, xT, NF)
        praw = s.sb("praw", [P, 2 * DC * P])
        pw = s.pair("pw", [P, 2 * DC * P])
        traw = s.sb("traw", [P, NT, D])
        tw = s.pair("tw", [P, NT, D])
        point = s.sb("point", [P, 1])
        disc = s.sb("disc", [P, TAYLOR])
        factor = s.sb("factor", [P, TAYLOR])
        delta = s.sb("delta", [P, TOK])
        power = s.sb("power", [P, TAYLOR, TOK])
        keep = s.sb("keep", [P, 3, TOK])
        term = s.sb("term", [P, NT, TOK])
        term_s = s.pair("terms", [P, NT, TOK])
        mbank = s.ps("mbank")

        w_loaded = s.sem("w_loaded")
        t_loaded = s.sem("t_loaded")
        pw_hi = s.sem("pw_hi")
        pw_lo = s.sem("pw_lo")
        tw_hi = s.sem("tw_hi")
        tw_lo = s.sem("tw_lo")
        factor_done = s.sem("factor_done")
        m_proj = s.sem("m_proj")
        m_read = s.sem("m_read")
        poly = s.sem("poly")
        terms_done = s.sem("terms_done")
        term_hi = s.sem("term_hi")
        term_lo = s.sem("term_lo")
        t_done = s.sem("t_done")
        added = s.sem("added")

        with nc.Block() as block:
            @block.sync
            def _(sp):
                sp.dma_start(praw[:], a["mix_proj"]).then_inc(w_loaded, 16)
                sp.dma_start(point[:], a["mix_point"]).then_inc(w_loaded, 16)
                sp.dma_start(disc[:], a["mix_disc"].partition_broadcast(P)).then_inc(w_loaded, 16)
                for f in range(NF):
                    G.load(sp, a["mix_ffn"][f], f, f % G.RING)
                    if f == 1:
                        sp.dma_start(traw[:], a["mix_out"]).then_inc(t_loaded, 16)

            @block.gpsimd
            def _(pool):
                ln.gpsimd(pool)
                pool.wait_ge(m_read, 2)
                pool.wait_ge(factor_done, 1)
                count = [0]

                def chain(ins):
                    ins.then_inc(poly, 1)
                    count[0] += 1
                    pool.wait_ge(poly, count[0])
                nc.gpsimd.tensor_scalar(keep[:, 0, :], delta[:], TAYLOR_KEEP, None, ALU.is_le).then_inc(poly, 1)
                count[0] += 1
                chain(nc.gpsimd.tensor_scalar(keep[:, 1, :], delta[:], -TAYLOR_KEEP, None, ALU.is_ge))
                chain(nc.gpsimd.tensor_tensor(keep[:, 2, :], keep[:, 0, :], keep[:, 1, :], ALU.mult))
                before = term[:, 0, :]
                for m in range(1, TAYLOR + 1):
                    chain(nc.gpsimd.tensor_tensor(power[:, m - 1, :], before, delta[:], ALU.mult))
                    before = power[:, m - 1, :]
                    if m > TAYLOR_MIN:
                        chain(nc.gpsimd.tensor_tensor(keep[:, m % 2, :], before, keep[:, 2, :], ALU.mult))
                        before = keep[:, m % 2, :]
                    last = nc.gpsimd.tensor_scalar(term[:, m, :], before, factor[:, m - 1:m], None, ALU.mult)
                last.then_inc(terms_done, 1)

            @block.tensor
            def _(pe):
                ln.tensor(pe)
                ln.wait_ready(pe)
                pe.wait_ge(pw_lo, 1)
                for part in range(2):
                    for c in range(DC):
                        at = (part * DC + c) * P
                        last = mm3(nc, mbank[:, part * TOK:(part + 1) * TOK],
                                   tuple(w[:, at:at + P] for w in pw),
                                   tuple(v[:, c, :] for v in xT), c == 0, c == DC - 1)
                last.then_inc(m_proj, 1)
                for f in range(NF):
                    G.gate_up(pe, f, f % G.RING)
                    if f:
                        G.down(pe, f - 1, (f - 1) % G.RING, f == 1, False)
                G.down(pe, NF - 1, (NF - 1) % G.RING, False, False)
                pe.wait_ge(term_lo, 1)
                pe.wait_ge(tw_lo, 1)
                for t in range(TT):
                    for m in range(NT):
                        last = mm3(nc, G.ybank[t][:], tuple(v[:, m, t * P:(t + 1) * P] for v in term_s),
                                   tuple(w[:, m, :] for w in tw), False, m == NT - 1)
                    last.then_inc(t_done, 1)

            @block.scalar
            def _(act):
                act.wait_ge(w_loaded, 48)
                split_tile(nc, act=act, dst=(pw[0][:], pw[1][:]), src=praw[:], hi_done=pw_hi)
                nc.scalar.activation(factor[:], disc[:], ACT.Exp, scale=-1.0).then_inc(factor_done, 1)
                ln.scalar(act)
                G.gu_hi(act, 0, 0, 0)
                act.wait_ge(m_proj, 1)
                nc.scalar.activation(term[:, 0, :], mbank[:, TOK:2 * TOK], ACT.Copy).then_inc(m_read, 1)
                for f in range(NF):
                    G.scalar(act, f, f // G.RING, f % G.RING, f == NF - 1)
                    if f == 2:
                        act.wait_ge(t_loaded, 16)
                        split_tile(nc, act=act, dst=(tw[0][:], tw[1][:]), src=traw[:], hi_done=tw_hi)
                    if f == NF - 3:
                        act.wait_ge(terms_done, 1)
                        split_tile(nc, act=act, dst=(term_s[0][:], term_s[1][:]), src=term[:], hi_done=term_hi)

            @block.vector
            def _(dve):
                ln.vector(dve)
                dve.wait_ge(pw_hi, 1)
                split_tile(nc, dve=dve, dst=(pw[0][:], pw[1][:]), src=praw[:], lo_done=pw_lo)
                G.gu_lo(dve, 0, 0)
                dve.wait_ge(m_read, 1)
                nc.vector.tensor_scalar(delta[:], mbank[:, 0:TOK], point[:, 0:1], None,
                                        ALU.subtract).then_inc(m_read, 1)
                for f in range(NF):
                    G.vector(dve, f, f % G.RING, f == NF - 1)
                    if f == 2:
                        dve.wait_ge(tw_hi, 1)
                        split_tile(nc, dve=dve, dst=(tw[0][:], tw[1][:]), src=traw[:], lo_done=tw_lo)
                    if f == NF - 3:
                        dve.wait_ge(term_hi, 1)
                        split_tile(nc, dve=dve, dst=(term_s[0][:], term_s[1][:]), src=term[:], lo_done=term_lo)
                for t in range(TT):
                    dve.wait_ge(t_done, t + 1)
                    nc.vector.tensor_tensor(x[:, t, :], x[:, t, :], G.ybank[t][:], ALU.add).then_inc(added, 1)


LORA_H, LORA_R = 1376, 2
LORA_REP = 4
LORA_HQ = LORA_H // LORA_REP
LORA_M = -(-LORA_HQ // P)
LORA_F = LORA_REP * LORA_M


def lora_ffn(nc, tag, g, a):
    x, ident = g["x"], g["ident"]
    with ExitStack() as ctx:
        s = Space(nc, ctx, tag)
        xT = s.pair("xT", [P, DC, TOK])
        tbank = [s.ps(f"tbank{i}") for i in range(2)]
        ln = LayerNormT(nc, s, x, ident, xT, tbank)
        graw = s.sb("graw", [P, 2, LORA_F * P])
        gw = s.pair("gw", [P, 2, LORA_F * P])
        draw = s.sb("draw", [P, LORA_M, D])
        dw = s.pair("dw", [P, LORA_M, D])
        araw = s.sb("araw", [P, DC, P])
        aw = s.pair("aw", [P, DC, P])
        bw = s.sb("bw", [2 * LORA_R, 2, LORA_F * P])
        a2 = s.sb("a2", [P, LORA_F, LORA_R])
        b2 = s.sb("b2", [LORA_R, D])
        la = s.sb("la", [2 * LORA_R, TOK])
        l2 = s.sb("l2", [LORA_R, TOK])
        xs = s.sb("xs", [P, TT, P])
        xsT = s.pair("xsT", [P, TOK])
        sg = s.sb("sg", [P, 2, TOK])
        hid = s.sb("hid", [P, LORA_F, TOK])
        hs = s.sb("hs", [P, LORA_M, TOK])
        hs_s = s.pair("hss", [P, LORA_M, TOK])
        gubank = [s.ps(f"gubank{i}") for i in range(2)]
        lbank = s.ps("lbank")
        ybank = [s.ps(f"ybank{i}") for i in range(TT)]

        g_loaded = s.sem("g_loaded")
        d_loaded = s.sem("d_loaded")
        a_loaded = s.sem("a_loaded")
        small_loaded = s.sem("small_loaded")
        g_hi, g_lo = s.sem("g_hi"), s.sem("g_lo")
        d_hi, d_lo = s.sem("d_hi"), s.sem("d_lo")
        a_hi, a_lo = s.sem("a_hi"), s.sem("a_lo")
        xs_done = s.sem("xs_done")
        xs_tr = s.sem("xs_tr")
        xs_hi, xs_lo = s.sem("xs_hi"), s.sem("xs_lo")
        la_done, la_read = s.sem("la_done"), s.sem("la_read")
        gu_done, silu_done, hid_done = s.sem("gu_done"), s.sem("silu_done"), s.sem("hid_done")
        l2_done, l2_read = s.sem("l2_done"), s.sem("l2_read")
        hs_done, hs_hi, hs_lo = s.sem("hs_done"), s.sem("hs_hi"), s.sem("hs_lo")
        y_done, added = s.sem("y_done"), s.sem("added")

        with nc.Block() as block:
            @block.sync
            def _(sp):
                sp.dma_start(araw[:], a["lora_a"]).then_inc(a_loaded, 16)
                sp.dma_start(graw[:], a["lora_g"]).then_inc(g_loaded, 16)
                sp.dma_start(bw[:], a["lora_b"]).then_inc(small_loaded, 16)
                sp.dma_start(a2[:], a["lora_a2"]).then_inc(small_loaded, 16)
                sp.dma_start(b2[:], a["lora_b2"]).then_inc(small_loaded, 16)
                sp.dma_start(draw[:], a["lora_d"]).then_inc(d_loaded, 16)

            @block.gpsimd
            def _(pool):
                ln.gpsimd(pool)

            @block.tensor
            def _(pe):
                ln.tensor(pe)
                for t in range(TT):
                    pe.wait_ge(xs_done, t + 1)
                    nc.tensor.transpose(lbank[:, t * P:(t + 1) * P], xs[:, t, :], ident[:]).then_inc(xs_tr, 1)
                ln.wait_ready(pe)
                pe.wait_ge(a_lo, 1)
                for c in range(DC):
                    last = mm3(nc, gubank[0][:, 0:TOK], tuple(w[:, c, :] for w in aw),
                               tuple(v[:, c, :] for v in xT), c == 0, c == DC - 1)
                last.then_inc(la_done, 1)
                pe.wait_ge(small_loaded, 48)
                pe.wait_ge(xs_lo, 1)
                pe.wait_ge(la_read, 1)
                for f in range(LORA_F):
                    if f % LORA_REP == 0 and f // LORA_REP < 3:
                        pe.wait_ge(g_lo, f // LORA_REP + 1)
                    need(pe, hid_done, f - 1)
                    for part in range(2):
                        out = gubank[f % 2][:, part * TOK:(part + 1) * TOK]
                        mm3(nc, out, tuple(w[:, part, f * P:(f + 1) * P] for w in gw),
                            tuple(v[:] for v in xsT), True, False)
                        last = nc.tensor.matmul(out, bw[:, part, f * P:(f + 1) * P], la[:], start=False, stop=True)
                    last.then_inc(gu_done, 1)
                pe.wait_ge(xs_hi, 1)
                for f in range(LORA_F):
                    pe.wait_ge(hid_done, f + 1)
                    last = nc.tensor.matmul(lbank[0:LORA_R, 0:TOK], a2[:, f, :], hid[:, f, :],
                                            start=(f == 0), stop=(f == LORA_F - 1))
                last.then_inc(l2_done, 1)
                pe.wait_ge(hs_lo, 1)
                pe.wait_ge(d_lo, 1)
                pe.wait_ge(l2_read, 1)
                for t in range(TT):
                    for m in range(LORA_M):
                        mm3(nc, ybank[t][:], tuple(v[:, m, t * P:(t + 1) * P] for v in hs_s),
                            tuple(w[:, m, :] for w in dw), m == 0, False)
                    nc.tensor.matmul(ybank[t][:], l2[:, t * P:(t + 1) * P], b2[:], start=False,
                                     stop=True).then_inc(y_done, 1)

            def thirds(ap, m):
                n = LORA_REP * P
                return ap[:, :, m * n:(m + 1) * n]

            @block.scalar
            def _(act):
                act.wait_ge(a_loaded, 16)
                nc.scalar.activation(aw[0][:], araw[:], ACT.Copy).then_inc(a_hi, 1)
                ln.scalar(act)
                act.wait_ge(xs_tr, TT)
                nc.scalar.activation(xsT[0][:], lbank[:, 0:TOK], ACT.Copy).then_inc(xs_hi, 1)
                act.wait_ge(g_loaded, 16)
                nc.scalar.activation(thirds(gw[0], 0), thirds(graw, 0), ACT.Copy).then_inc(g_hi, 1)
                act.wait_ge(la_done, 1)
                nc.scalar.activation(la[:], gubank[0][0:2 * LORA_R, 0:TOK], ACT.Copy, scale=0.5).then_inc(la_read, 1)
                for m in range(1, LORA_M):
                    nc.scalar.activation(thirds(gw[0], m), thirds(graw, m), ACT.Copy).then_inc(g_hi, 1)
                for f in range(LORA_F):
                    act.wait_ge(gu_done, f + 1)
                    need(act, hid_done, f - 1)
                    nc.scalar.activation(sg[:, f % 2, :], gubank[f % 2][:, 0:TOK], ACT.Silu).then_inc(silu_done, 1)
                    if f == 2:
                        act.wait_ge(d_loaded, 16)
                        nc.scalar.activation(dw[0][:], draw[:], ACT.Copy).then_inc(d_hi, 1)
                act.wait_ge(hs_done, LORA_M)
                nc.scalar.activation(hs_s[0][:], hs[:], ACT.Copy).then_inc(hs_hi, 1)
                act.wait_ge(l2_done, 1)
                nc.scalar.activation(l2[:], lbank[0:LORA_R, 0:TOK], ACT.Copy, scale=0.5).then_inc(l2_read, 1)

            @block.vector
            def _(dve):
                ln.vector(dve)
                for t in range(TT):
                    dve.wait_ge(ln.normed, t + 1)
                    nc.vector.tensor_reduce(xs[:, t, :], ln.xn[:, t, :].rearrange("p (c k) -> p k c", c=DC),
                                            AX.X, ALU.add).then_inc(xs_done, 1)
                dve.wait_ge(a_hi, 1)
                nc.vector.tensor_tensor(aw[1][:], araw[:], as_f32(aw[0][:]), ALU.subtract).then_inc(a_lo, 1)
                dve.wait_ge(xs_hi, 1)
                nc.vector.tensor_tensor(xsT[1][:], lbank[:, 0:TOK], as_f32(xsT[0][:]), ALU.subtract).then_inc(xs_lo, 1)
                for m in range(LORA_M):
                    dve.wait_ge(g_hi, m + 1)
                    nc.vector.tensor_tensor(thirds(gw[1], m), thirds(graw, m), as_f32(thirds(gw[0], m)),
                                            ALU.subtract).then_inc(g_lo, 1)
                for f in range(LORA_F):
                    dve.wait_ge(silu_done, f + 1)
                    nc.vector.tensor_tensor(hid[:, f, :], sg[:, f % 2, :], gubank[f % 2][:, TOK:2 * TOK],
                                            ALU.mult).then_inc(hid_done, 1)
                    if f == 2:
                        dve.wait_ge(d_hi, 1)
                        nc.vector.tensor_tensor(dw[1][:], draw[:], as_f32(dw[0][:]), ALU.subtract).then_inc(d_lo, 1)
                    if f % LORA_REP == LORA_REP - 1:
                        m = f // LORA_REP
                        dve.wait_ge(hid_done, f + 1)
                        nc.vector.tensor_reduce(hs[:, m, :], hid[:, m * LORA_REP:(m + 1) * LORA_REP, :]
                                                .rearrange("p j k -> p k j"), AX.X, ALU.add).then_inc(hs_done, 1)
                dve.wait_ge(hs_hi, 1)
                nc.vector.tensor_tensor(hs_s[1][:], hs[:], as_f32(hs_s[0][:]), ALU.subtract).then_inc(hs_lo, 1)
                for t in range(TT):
                    dve.wait_ge(y_done, t + 1)
                    nc.vector.tensor_tensor(x[:, t, :], x[:, t, :], ybank[t][:], ALU.add).then_inc(added, 1)


SH, SKV = 32, 8
SD = D // SH
SROWS = P // SD
SKW = SKV * SD


def self_attention(nc, tag, g, a):
    x, ident = g["x"], g["ident"]
    NJ = D // P
    with ExitStack() as ctx:
        s = Space(nc, ctx, tag)
        xT = s.pair("xT", [P, DC, TOK])
        bank = [s.ps(f"bank{i}") for i in range(4)]
        sbank = s.ps("sbank", 2)
        obank = s.ps("obank")
        ybank = s.ps("ybank")
        ln = LayerNormT(nc, s, x, ident, xT, bank[0:2])
        NWR = 3
        wraw = s.sb("wraw", [P, NWR, DC * D])
        ws = s.pair("ws", [P, NWR, DC * D])
        rope = s.sb("rope", [P, 2, SD])
        blocks = s.sb("blocks", [P, SROWS])
        causal = s.sb("causal", [P, SEQ])
        rot = s.sb("rot", [P, TT, SH + SKV, SD])
        q = s.sb("q", [P, TT, SH, SD])
        k = s.sb("k", [P, TT, SKV, SD])
        ko = s.sb("ko", [P, TT, NJ, SROWS, SD])
        v = s.sb("v", [P, TT, SKW])
        qT = s.sb("qT", [P, TT, NJ, P])
        kT = s.sb("kT", [P, NJ, SROWS, P])
        sc = s.sb("sc", [P, SH, SEQ])
        mx = s.sb("mx", [P, SH])
        sm = s.sb("sm", [P, TT, SH])
        pr = s.sb("pr", [P, SH, SEQ])
        prT = s.sb("prT", [P, SH, BT, SEQ])
        on = s.sb("on", [P, D])
        oT = s.pair("oT", [P, DC, P])

        loaded = [s.sem(f"loaded{i}") for i in range(NWR)]
        small_loaded = s.sem("small_loaded")
        w_hi, w_lo = s.sem("w_hi"), s.sem("w_lo")
        proj, roped = s.sem("proj"), s.sem("roped")
        v_read = s.sem("v_read")
        chain = s.sem("chain")
        q_tr, q_read = s.sem("q_tr"), s.sem("q_read")
        k_tr, k_read = s.sem("k_tr"), s.sem("k_read")
        s_done = s.sem("s_done")
        e_in, e_done = s.sem("e_in"), s.sem("e_done")
        zeroed, p_tr = s.sem("zeroed"), s.sem("p_tr")
        o_done, o_normed = s.sem("o_done"), s.sem("o_normed")
        o_tr, o_hi, o_lo = s.sem("o_tr"), s.sem("o_hi"), s.sem("o_lo")
        y_done, added = s.sem("y_done"), s.sem("added")

        with nc.Block() as block:
            @block.sync
            def _(sp):
                sp.dma_start(wraw[:, 0, :], a["s_wq"]).then_inc(loaded[0], 16)
                sp.dma_start(wraw[:, 1, 0:DC * 2 * SKW], a["s_wkv"]).then_inc(loaded[1], 16)
                sp.dma_start(rope[:], a["s_rope"]).then_inc(small_loaded, 16)
                sp.dma_start(blocks[:], a["s_blocks"]).then_inc(small_loaded, 16)
                sp.dma_start(causal[:], a["s_causal"]).then_inc(small_loaded, 16)
                sp.dma_start(wraw[:, 2, :], a["s_wo"]).then_inc(loaded[2], 16)

            @block.gpsimd
            def _(pool):
                nc.gpsimd.memset(prT[:], 0.0).then_inc(zeroed, 1)
                ln.gpsimd(pool)

            WIDTHS = [DC * D, DC * 2 * SKW, DC * D]

            @block.scalar
            def _(act):
                ln.scalar(act)
                for i, n in enumerate(WIDTHS):
                    act.wait_ge(loaded[i], 16)
                    nc.scalar.activation(ws[0][:, i, :n], wraw[:, i, :n], ACT.Copy).then_inc(w_hi, 1)
                for t in range(TT):
                    act.wait_ge(roped, t + 1)
                    nc.scalar.activation(v[:, t, :], bank[2 * t + 1][:, SKW:2 * SKW], ACT.Copy).then_inc(v_read, 1)
                for t in range(TT):
                    act.wait_ge(q_tr, t + 1)
                    nc.scalar.activation(qT[:, t, :, :], bank[2 * t][:, :].rearrange("p (j n) -> p j n", j=NJ),
                                         ACT.Copy).then_inc(q_read, 1)
                for t in range(TT):
                    act.wait_ge(e_in, t + 1)
                    need(act, p_tr, t)
                    nc.scalar.activation(pr[:], sc[:], ACT.Exp).then_inc(e_done, 1)
                    act.wait_ge(o_tr, t + 1)
                    need(act, y_done, t)
                    nc.scalar.activation(oT[0][:], obank[:, :].rearrange("p (c n) -> p c n", c=DC),
                                         ACT.Copy).then_inc(o_hi, 1)

            @block.tensor
            def _(pe):
                ln.tensor(pe)
                ln.wait_ready(pe)
                for t in range(TT):
                    for i, n in enumerate((D, 2 * SKW)):
                        pe.wait_ge(w_lo, i + 1)
                        for c in range(DC):
                            last = mm3(nc, bank[2 * t + i][:, 0:n], tuple(h[:, c, t * P:(t + 1) * P] for h in xT),
                                       tuple(w[:, i, c * n:(c + 1) * n] for w in ws), c == 0, c == DC - 1)
                    last.then_inc(proj, 1)
                for t in range(TT):
                    pe.wait_ge(roped, t + 1)
                    pe.wait_ge(v_read, t + 1)
                    for j in range(NJ):
                        last = nc.tensor.transpose(bank[2 * t][:, j * P:(j + 1) * P],
                                                   q[:, t, j * SROWS:(j + 1) * SROWS, :]
                                                   .rearrange("p h d -> p (h d)"), ident[:])
                    last.then_inc(q_tr, 1)
                    for j in range(NJ):
                        last = nc.tensor.transpose(bank[2 * t + 1][:, j * P:(j + 1) * P],
                                                   ko[:, t, j, :, :].rearrange("p h d -> p (h d)"), ident[:])
                    last.then_inc(k_tr, 1)
                for t in range(TT):
                    pe.wait_ge(q_read, t + 1)
                    pe.wait_ge(k_read, t + 1)
                    need(pe, e_in, t)
                    for j in range(NJ):
                        for b in range(BT):
                            last = nc.tensor.matmul(
                                sbank[b * SEQ:(b + 1) * SEQ, j * SROWS * SEQ:(j + 1) * SROWS * SEQ],
                                qT[:, t, j, b * SEQ:(b + 1) * SEQ], kT[:, j, :, b * SEQ:(b + 1) * SEQ],
                                start=True, stop=True)
                    last.then_inc(s_done, 1)
                    pe.wait_ge(p_tr, t + 1)
                    for h in range(SH):
                        kv = h // (SH // SKV)
                        last = nc.tensor.matmul(obank[:, h * SD:(h + 1) * SD],
                                                prT[:, h, :, :].rearrange("p b q -> p (b q)"),
                                                v[:, t, kv * SD:(kv + 1) * SD], start=True, stop=True)
                    last.then_inc(o_done, 1)
                    pe.wait_ge(o_normed, t + 1)
                    for c in range(DC):
                        last = nc.tensor.transpose(obank[:, c * P:(c + 1) * P], on[:, c * P:(c + 1) * P], ident[:])
                    last.then_inc(o_tr, 1)
                    pe.wait_ge(o_lo, t + 1)
                    pe.wait_ge(w_lo, NWR)
                    need(pe, added, t)
                    for c in range(DC):
                        last = mm3(nc, ybank[:], tuple(h[:, c, :] for h in oT),
                                   tuple(w[:, 2, c * D:(c + 1) * D] for w in ws), c == 0, c == DC - 1)
                    last.then_inc(y_done, 1)

            @block.vector
            def _(dve):
                links = [0]

                def link(ins):
                    ins.then_inc(chain, 1)
                    links[0] += 1
                    dve.wait_ge(chain, links[0])

                ln.vector(dve)
                for i, n in enumerate(WIDTHS):
                    dve.wait_ge(w_hi, i + 1)
                    nc.vector.tensor_tensor(ws[1][:, i, :n], wraw[:, i, :n], as_f32(ws[0][:, i, :n]),
                                            ALU.subtract).then_inc(w_lo, 1)
                dve.wait_ge(small_loaded, 48)
                H2 = SD // 2
                for t in range(TT):
                    dve.wait_ge(proj, t + 1)
                    for src, dst, heads, at in ((bank[2 * t][:, 0:D], q, SH, 0),
                                                (bank[2 * t + 1][:, 0:SKW], k, SKV, SH)):
                        halves = src.rearrange("p (h d) -> p h d", d=SD)

                        def table(i, lo, hi):
                            return rope[:, i, lo:hi].unsqueeze(1).broadcast_to([P, heads, hi - lo])
                        nc.vector.tensor_tensor(rot[:, t, at:at + heads, 0:H2], halves[:, :, H2:SD],
                                                table(1, 0, H2), ALU.mult)
                        nc.vector.tensor_tensor(rot[:, t, at:at + heads, H2:SD], halves[:, :, 0:H2],
                                                table(1, H2, SD), ALU.mult)
                        link(nc.vector.tensor_tensor(dst[:, t, :, :], halves, table(0, 0, SD), ALU.mult))
                        link(nc.vector.tensor_tensor(dst[:, t, :, :], dst[:, t, :, :],
                                                     rot[:, t, at:at + heads, :], ALU.add))
                    rep = SH // SKV
                    nc.vector.tensor_copy(
                        ko[:, t, :, :, :].rearrange("p j (g r) d -> p (j g) r d", r=rep),
                        k[:, t, :, :].unsqueeze(2).broadcast_to([P, SKV, rep, SD])).then_inc(roped, 1)
                for t in range(TT):
                    dve.wait_ge(k_tr, t + 1)
                    need(dve, s_done, t)
                    for j in range(NJ):
                        last = nc.vector.tensor_tensor(
                            kT[:, j, :, :],
                            bank[2 * t + 1][:, j * P:(j + 1) * P].unsqueeze(1).broadcast_to([P, SROWS, P]),
                            blocks[:, :].unsqueeze(2).broadcast_to([P, SROWS, P]), ALU.mult)
                    last.then_inc(k_read, 1)
                    dve.wait_ge(s_done, t + 1)
                    need(dve, e_done, t)
                    link(nc.vector.scalar_tensor_tensor(
                        out=sc[:], in0=sbank[:, :].rearrange("p (h n) -> p h n", h=SH), scalar=SD ** -0.5,
                        in1=causal[:, :].unsqueeze(1).broadcast_to([P, SH, SEQ]), op0=ALU.mult, op1=ALU.add))
                    link(nc.vector.tensor_reduce(mx[:], sc[:], AX.X, ALU.max))
                    nc.vector.tensor_tensor(sc[:], sc[:], mx[:, :].unsqueeze(2).broadcast_to([P, SH, SEQ]),
                                            ALU.subtract).then_inc(e_in, 1)
                    dve.wait_ge(e_done, t + 1)
                    link(nc.vector.tensor_reduce(sm[:, t, :], pr[:], AX.X, ALU.add))
                    link(nc.vector.reciprocal(sm[:, t, :], sm[:, t, :]))
                    dve.wait_ge(zeroed, 1)
                    need(dve, o_done, t)
                    for b in range(BT):
                        rows = slice(b * SEQ, (b + 1) * SEQ)
                        last = nc.vector.transpose(prT[rows, :, b, :], pr[rows, :, :])
                    last.then_inc(p_tr, 1)
                    dve.wait_ge(o_done, t + 1)
                    need(dve, o_tr, t)
                    nc.vector.tensor_tensor(on[:, :].rearrange("p (h d) -> p h d", h=SH),
                                            obank[:, :].rearrange("p (h d) -> p h d", h=SH),
                                            sm[:, t, :].unsqueeze(2).broadcast_to([P, SH, SD]),
                                            ALU.mult).then_inc(o_normed, 1)
                    dve.wait_ge(o_hi, t + 1)
                    nc.vector.tensor_tensor(oT[1][:], obank[:, :].rearrange("p (c n) -> p c n", c=DC),
                                            as_f32(oT[0][:]), ALU.subtract).then_inc(o_lo, 1)
                    dve.wait_ge(y_done, t + 1)
                    nc.vector.tensor_tensor(x[:, t, :], x[:, t, :], ybank[:], ALU.add).then_inc(added, 1)


EXPERTS = 16
SHARED_T = 4


def experts(nc, tag, g, a):
    x, ident = g["x"], g["ident"]
    NF = SHARED_T + EXPERTS
    assert SHARED_T == GatedTiles.RING and NF % GatedTiles.RING == 0
    E = EXPERTS
    with ExitStack() as ctx:
        s = Space(nc, ctx, tag)
        xT = s.pair("xT", [P, DC, TOK])
        tbank = [s.ps(f"tbank{i}") for i in range(2)]
        rbank = s.ps("rbank")
        ln = LayerNormT(nc, s, x, ident, xT, tbank)
        G = GatedTiles(nc, s, xT, NF)
        cbank = tbank
        rraw = s.sb("rraw", [P, DC, E])
        rw = s.pair("rw", [P, DC, E])
        rank = s.sb("rank", [P, E])
        mine = s.sb("mine", [E, E])
        ones = s.sb("ones", [E, P])
        nmx = s.sb("nmx", [P, TT])
        pe_ = s.sb("prob", [P, TT, E])
        tot = s.sb("tot", [P, TT])
        inv = s.sb("inv", [P, TT])
        prob = s.sb("p", [P, TT, E])
        rest = s.sb("rest", [P, TT, E])
        hot = s.sb("hot", [P, 2, TT, E])
        tmp = s.sb("tmp", [P, TT, E])
        best = s.sb("best", [P, 2, TT])
        top = s.sb("top", [P, TT])
        comb = s.sb("comb", [P, TT, E])
        combT = s.sb("combT", [E, TOK])
        diag = s.sb("diag", [E, E, TOK])

        r_loaded = s.sem("r_loaded")
        r_hi, r_lo = s.sem("r_hi"), s.sem("r_lo")
        ones_set = s.sem("ones_set")
        logits, nmx_done, exp_done = s.sem("logits"), s.sem("nmx_done"), s.sem("exp_done")
        chain = s.sem("chain")
        comb_done, comb_tr, comb_read = s.sem("comb_done"), s.sem("comb_tr"), s.sem("comb_read")
        diag_done = s.sem("diag_done")
        cast_done = s.sem("cast_done")
        added = s.sem("added")

        with nc.Block() as block:
            @block.sync
            def _(sp):
                sp.dma_start(rraw[:], a["e_router"]).then_inc(r_loaded, 16)
                sp.dma_start(rank[:], a["e_rank"]).then_inc(r_loaded, 16)
                sp.dma_start(mine[:], a["ident"][0:E, 0:E]).then_inc(r_loaded, 16)

                def step(i):
                    for k in range(G.RING):
                        f = G.RING * i + k
                        G.load(sp, a["e_w"][bass.ds(f, 1), :, :].rearrange("a p n -> p (a n)"), f, k)
                peeled(sp, NF // G.RING, step)

            @block.gpsimd
            def _(pool):
                ln.gpsimd(pool)
                nc.gpsimd.memset(ones[:], 1.0).then_inc(ones_set, 1)

            @block.tensor
            def _(pe):
                ln.tensor(pe)
                ln.wait_ready(pe)
                pe.wait_ge(ones_set, 1)
                pe.wait_ge(r_lo, 1)
                for t in range(TT):
                    for c in range(DC):
                        last = mm3(nc, rbank[:, t * E:(t + 1) * E], tuple(h[:, c, t * P:(t + 1) * P] for h in xT),
                                   tuple(w[:, c, :] for w in rw), c == 0, c == DC - 1)
                last.then_inc(logits, 1)

                def step(i):
                    for k in range(G.RING):
                        f = G.RING * i + k
                        if not is_at(i, 0):
                            e = f - SHARED_T
                            pe.wait_ge(diag_done, 1)
                            pe.wait_ge(G.a_done_sem, f - 1)
                            nc.tensor.matmul(cbank[k % 2][:, 0:TOK], ones[:],
                                             diag[:, bass.ds(e, 1), :].rearrange("p a n -> p (a n)"),
                                             start=True, stop=True).then_inc(cast_done, 1)
                        G.gate_up(pe, f, k)
                        if not is_at(f, 0):
                            G.down(pe, f - 1, (k - 1) % G.RING, is_at(f, 1), False)
                        if is_at(f, G.RING - 1):
                            for t in range(TT):
                                pe.wait_ge(comb_done, 1)
                                last = nc.tensor.transpose(rbank[0:E, t * P:(t + 1) * P], comb[:, t, :], ident[:])
                            last.then_inc(comb_tr, 1)
                peeled(pe, NF // G.RING, step)
                G.down(pe, NF - 1, (NF - 1) % G.RING, False, True)

            @block.scalar
            def _(act):
                act.wait_ge(r_loaded, 48)
                nc.scalar.activation(rw[0][:], rraw[:], ACT.Copy).then_inc(r_hi, 1)
                ln.scalar(act)
                G.gu_hi(act, 0, 0, 0)
                act.wait_ge(nmx_done, 1)
                for t in range(TT):
                    last = nc.scalar.activation(pe_[:, t, :], rbank[:, t * E:(t + 1) * E], ACT.Exp,
                                                bias=nmx[:, t:t + 1], accum_out=tot[:, t:t + 1])
                    last.then_inc(exp_done, 1)

                def step(i):
                    for k in range(G.RING):
                        f = G.RING * i + k
                        G.scalar(act, f, i, k, is_at(f, NF - 1))
                peeled(act, NF // G.RING, step)

            @block.vector
            def _(dve):
                links = [0]

                def link(ins):
                    ins.then_inc(chain, 1)
                    links[0] += 1
                    dve.wait_ge(chain, links[0])

                def wide(ap):
                    return ap.unsqueeze(2).broadcast_to([P, TT, E])

                ranks = rank[:, :].unsqueeze(1).broadcast_to([P, TT, E])
                ln.vector(dve)
                dve.wait_ge(r_hi, 1)
                nc.vector.tensor_tensor(rw[1][:], rraw[:], as_f32(rw[0][:]), ALU.subtract).then_inc(r_lo, 1)
                G.gu_lo(dve, 0, 0)
                dve.wait_ge(logits, 1)
                nc.vector.tensor_reduce(nmx[:], rbank[:, 0:TT * E].rearrange("p (t e) -> p t e", t=TT), AX.X,
                                        ALU.max, negate=True).then_inc(nmx_done, 1)
                dve.wait_ge(exp_done, TT)
                link(nc.vector.reciprocal(inv[:], tot[:]))
                link(nc.vector.tensor_tensor(prob[:], pe_[:], wide(inv[:, :]), ALU.mult))
                left = prob
                for r in range(2):
                    link(nc.vector.tensor_reduce(best[:, r, :], left[:], AX.X, ALU.max))
                    link(nc.vector.tensor_tensor(tmp[:], left[:], wide(best[:, r, :]), ALU.is_equal))
                    link(nc.vector.tensor_tensor(tmp[:], tmp[:], ranks, ALU.mult))
                    link(nc.vector.tensor_reduce(top[:], tmp[:], AX.X, ALU.max))
                    link(nc.vector.tensor_tensor(hot[:, r, :, :], tmp[:], wide(top[:, :]), ALU.is_equal))
                    if r == 0:
                        link(nc.vector.tensor_scalar(tmp[:], hot[:, 0, :, :], -2.0, None, ALU.mult))
                        link(nc.vector.tensor_tensor(rest[:], prob[:], tmp[:], ALU.add))
                        left = rest
                link(nc.vector.tensor_tensor(top[:], best[:, 0, :], best[:, 1, :], ALU.add))
                link(nc.vector.reciprocal(top[:], top[:]))
                link(nc.vector.tensor_tensor(hot[:, 0, :, :], hot[:, 0, :, :], wide(best[:, 0, :]), ALU.mult))
                link(nc.vector.tensor_tensor(hot[:, 1, :, :], hot[:, 1, :, :], wide(best[:, 1, :]), ALU.mult))
                link(nc.vector.tensor_tensor(tmp[:], hot[:, 0, :, :], hot[:, 1, :, :], ALU.add))
                nc.vector.tensor_tensor(comb[:], tmp[:], wide(top[:, :]), ALU.mult).then_inc(comb_done, 1)

                def step(i):
                    for k in range(G.RING):
                        f = G.RING * i + k
                        e = f - SHARED_T
                        combine = None if is_at(i, 0) else (cbank[k % 2][:, 0:TOK], cast_done, e + 1, e)
                        G.vector(dve, f, k, is_at(f, NF - 1), combine)
                        if is_at(f, G.RING - 1):
                            dve.wait_ge(comb_tr, 1)
                            nc.vector.tensor_copy(combT[:], rbank[0:E, 0:TOK]).then_inc(comb_read, 1)
                            dve.wait_ge(comb_read, 1)
                            nc.vector.tensor_tensor(diag[:], combT[:, :].unsqueeze(1).broadcast_to([E, E, TOK]),
                                                    mine[:, :].unsqueeze(2).broadcast_to([E, E, TOK]),
                                                    ALU.mult).then_inc(diag_done, 1)
                peeled(dve, NF // G.RING, step)
                dve.wait_ge(G.down_done_sem, NF)
                for t in range(TT):
                    nc.vector.tensor_tensor(x[:, t, :], x[:, t, :], G.ybank[t][:], ALU.add).then_inc(added, 1)


def build_program(nc, phases=99, **a):
    with ExitStack() as ctx:
        s = Space(nc, ctx, "g")
        x = s.sb("x", [P, TT, D])
        ident = s.sb("ident", [P, P])
        stage, stage_r = s.twins("stage", [P, 2, DC * UW])
        g = {"x": x, "ident": ident, "stage": stage, "stage_r": stage_r, "vlat_dram": a["vlat_dram"], "a": a}
        loaded = s.sem("loaded")
        stored = s.sem("stored")
        SEMAPHORES.clear()
        with nc.Block() as block:
            @block.sync
            def _(sp):
                sp.dma_start(x[:], a["x"].rearrange("(t p) d -> p t d", p=P)).then_inc(loaded, 16)
                sp.dma_start(ident[:], a["ident"]).then_inc(loaded, 16)
                sp.wait_ge(loaded, 32)
        L0 = {"wkv": a["l0_wkv"], "wq": a["l0_wq"], "wo": a["l0_wo"], "norm": a["l0_norm"], "ctx": a["ctx"], "mask": None}
        L1 = {"wkv": a["l1_wkv"], "wq": a["l1_wq"], "wo": a["l1_wo"], "norm": a["l1_norm"], "ctx": a["ctx"], "mask": a["mask"]}
        if phases >= 1:
            cross_attention(nc, "c0", g, L0, 1e-6, True)
            clear_semaphores(nc)
        if phases >= 2:
            mixer(nc, "m0", g, a)
            clear_semaphores(nc)
        if phases >= 3:
            lora_ffn(nc, "f0", g, a)
            clear_semaphores(nc)
        if phases >= 4:
            cross_attention(nc, "c1", g, L1, 1e-5, False)
            clear_semaphores(nc)
        if phases >= 5:
            self_attention(nc, "s1", g, a)
            clear_semaphores(nc)
        if phases >= 6:
            experts(nc, "e1", g, a)
        with nc.Block() as block:
            @block.sync
            def _(sp):
                sp.dma_start(a["out"].rearrange("(t p) d -> p t d", p=P), x[:]).then_inc(stored, 16)
                sp.wait_ge(stored, 16)


def lay_out(i):
    def c_major(w_cn):
        n = w_cn.shape[1]
        return w_cn.reshape(DC, P, n).transpose(1, 0, 2).reshape(P, DC * n)

    def halves(w_cn, width):
        return np.stack([c_major(w_cn[:, k:k + width]) for k in range(0, w_cn.shape[1], width)])

    def wkv(wk, wv):
        return np.concatenate([halves(wk, UW), halves(wv, UW)])

    def heads(wo):
        return wo.reshape(HEADS // GROUP, GROUP, HD, D).transpose(0, 2, 1, 3).reshape(HEADS // GROUP, P, GROUP * D)

    o = {"x": i["x"].reshape(TOK, D), "ident": np.eye(P, dtype=np.float32)}
    o["ctx"] = i["ctx_4096"].reshape(B, CT, P, DC, P).transpose(0, 4, 1, 3, 2).reshape(B, P, CT * DC * P)
    o["mask"] = i["mask_1x1xSxS2_ff0"].reshape(SEQ, CTX)
    o["l0_wkv"] = wkv(i["L0_xattn_Wk"], i["L0_xattn_Wv"])
    o["l0_wq"] = halves(i["L0_xattn_Wq"], UW)
    o["l0_wo"] = heads(i["L0_xattn_Wo"])
    o["l0_norm"] = np.stack([i["L0_xattn_q_norm_w"], i["L0_xattn_k_norm_w"]], 1)
    o["l1_wkv"] = wkv(i["L1_xattn_Wk"].T, i["L1_xattn_Wv"].T)
    o["l1_wq"] = halves(i["L1_xattn_Wq"].T, UW)
    o["l1_wo"] = heads(i["L1_xattn_Wo"].T)
    o["l1_norm"] = np.stack([i["L1_xattn_q_norm_w"], i["L1_xattn_k_norm_w"]], 1)
    return lay_out_rest(i, o)


def lay_out_rest(i, o):
    def tile_gud(gate, up, down):
        n = gate.shape[0]
        out = np.zeros((P, GatedTiles.WIDTH), np.float32)
        for part, w in enumerate((gate, up)):
            view = out[:, part * DC * P:(part + 1) * DC * P].reshape(P, DC, P)
            view[:, :, :n] = w.T.reshape(DC, P, n).transpose(1, 0, 2)
        out[:n, GatedTiles.GU:] = down.T
        return out

    def c_major(w_cn):
        n = w_cn.shape[1]
        return w_cn.reshape(DC, P, n).transpose(1, 0, 2).reshape(P, DC * n)

    gw, uw, dw = i["L0_attn_ffn_gate_w"], i["L0_attn_ffn_up_w"], i["L0_attn_ffn_down_w"]
    F = gw.shape[0]
    o["mix_ffn"] = np.stack([tile_gud(gw[k:k + P], uw[k:k + P], dw[:, k:k + P]) for k in range(0, F, P)])
    o["mix_proj"] = np.concatenate([c_major(i["L0_attn_gate_w"].T), c_major(i["L0_attn_up_w"].T)], 1)
    o["mix_point"] = i["L0_attn_local_point"].reshape(P, 1)
    o["mix_disc"] = i["L0_attn_discount_factor"]
    o["mix_out"] = np.concatenate([i["L0_attn_local_approx_output"].T[:, None, :],
                                   i["L0_attn_fuse_weight"].transpose(1, 2, 0)], 1)
    padded = LORA_M * P

    def by_tile(w):
        lead = w.shape[:-1]
        out = np.zeros(lead + (LORA_REP, padded), np.float32)
        out[..., :LORA_HQ] = w.reshape(lead + (LORA_REP, LORA_HQ))
        out = out.reshape(lead + (LORA_REP, LORA_M, P))
        return np.swapaxes(out, -3, -2).reshape(lead + (LORA_F * P,))

    o["lora_g"] = np.stack([by_tile(i["L0_ffn_w1q"].T), by_tile(i["L0_ffn_w3q"].T)], 1)
    d = np.zeros((padded, D), np.float32)
    d[:LORA_HQ] = i["L0_ffn_w2q"].T
    o["lora_d"] = d.reshape(LORA_M, P, D).transpose(1, 0, 2)
    la = np.zeros((D, P), np.float32)
    la[:, 0:LORA_R] = i["L0_ffn_a1"].T
    la[:, LORA_R:2 * LORA_R] = i["L0_ffn_a3"].T
    o["lora_a"] = la.reshape(DC, P, P).transpose(1, 0, 2)
    lb = np.zeros((2 * LORA_R, 2, LORA_F * P), np.float32)
    lb[0:LORA_R, 0] = by_tile(i["L0_ffn_b1"].T)
    lb[LORA_R:, 1] = by_tile(i["L0_ffn_b3"].T)
    o["lora_b"] = lb
    o["lora_a2"] = by_tile(i["L0_ffn_a2"]).reshape(LORA_R, LORA_F, P).transpose(2, 1, 0)
    o["lora_b2"] = i["L0_ffn_b2"].T
    o["s_wq"] = c_major(i["L1_attn_Wq"].T)
    o["s_wkv"] = c_major(np.concatenate([i["L1_attn_Wk"].T, i["L1_attn_Wv"].T], 1))
    o["s_wo"] = c_major(i["L1_attn_Wo"].T)
    o["s_rope"], o["s_blocks"], o["s_causal"] = tables()
    sg, su = np.split(i["L1_ffn_shared_w_gate_up"], 2)
    sd = i["L1_ffn_shared_w_down"]
    tiles = [tile_gud(sg[k:k + P], su[k:k + P], sd[:, k:k + P]) for k in range(0, SHARED_T * P, P)]
    for e in range(EXPERTS):
        eg, eu = np.split(i["L1_ffn_w_gate_up"][e], 2)
        tiles.append(tile_gud(eg, eu, i["L1_ffn_w_down"][e]))
    o["e_w"] = np.stack(tiles)
    o["e_router"] = i["L1_ffn_gate_w"].T.reshape(DC, P, EXPERTS).transpose(1, 0, 2)
    o["e_rank"] = np.tile(np.arange(EXPERTS, 0, -1, dtype=np.float32), (P, 1))
    return o


def tables():
    theta, factor, hi_f, lo_f, orig = 500000.0, 32.0, 4.0, 1.0, 1024
    f32 = np.float32
    inv = (f32(1.0) / f32(theta) ** (np.arange(0, SD, 2, dtype=f32) / f32(SD))).astype(f32)
    wavelen = (f32(2.0 * np.pi) / inv).astype(f32)
    base = np.where(wavelen > orig / lo_f, inv / f32(factor), inv).astype(f32)
    smooth = ((orig / wavelen - lo_f) / (hi_f - lo_f)).astype(f32)
    smoothed = ((1.0 - smooth) * base / f32(factor) + smooth * base).astype(f32)
    medium = ~(wavelen < orig / lo_f) & ~(wavelen > orig / hi_f)
    freqs = np.arange(SEQ, dtype=f32)[:, None] * np.where(medium, smoothed, base).astype(f32)[None, :]
    freqs = freqs.astype(f32)
    cos, sin = np.cos(freqs), np.sin(freqs)
    rope = np.stack([np.concatenate([cos, cos], 1), np.concatenate([-sin, sin], 1)], 1)
    rope = np.tile(rope, (BT, 1, 1)).astype(f32)
    blocks = (np.arange(P)[:, None] // SD == np.arange(SROWS)[None, :]).astype(f32)
    causal = np.where(np.arange(SEQ)[None, :] <= np.arange(SEQ)[:, None], 0.0, -3.0e38)
    return rope, blocks, np.tile(causal, (BT, 1)).astype(f32)


def kernel(**inputs):
    import concourse.bacc as bacc
    from concourse.bass_utils import run_bass_kernel_spmd

    given = {name: np.asarray(v) for name, v in inputs.items()}
    nc = bacc.Bacc("TRN2", target_bir_lowering=False, num_devices=1)
    arrays, aps = {}, {}
    for name, v in lay_out(given).items():
        v = np.ascontiguousarray(v)
        arrays[f"in_{name}"] = v
        aps[name] = nc.dram_tensor(f"in_{name}", v.shape, mybir.dt.from_np(v.dtype), kind="ExternalInput").ap()
    aps["vlat_dram"] = nc.dram_tensor("vlat_dram", (TOK, 2 * UW), F32).ap()
    aps["out"] = nc.dram_tensor("out_dram", (TOK, D), F32, kind="ExternalOutput").ap()
    build_program(nc, **aps)
    r = run_bass_kernel_spmd(nc, [arrays], core_ids=[0])
    return r.results[0]["out_dram"].reshape(B, SEQ, D)
```

```python
from contextlib import ExitStack

import numpy as np

import concourse.bass as bass
from concourse import mybir

ALU = mybir.AluOpType
ACT = mybir.ActivationFunctionType
AX = mybir.AxisListType
F32 = mybir.dt.float32
F32R = mybir.dt.float32r

P = 128
B, SEQ, D = 8, 32, 512
TOK = B * SEQ
TT = TOK // P
BT = P // SEQ
DC = D // P
CTX = 512
CT = CTX // P
HEADS, KVH, HD = 32, 8, 128
GROUP = HEADS // KVH
UNIT_H = 4
UNITS = B * KVH // UNIT_H
UW = UNIT_H * HD
TAYLOR = 6
TAYLOR_MIN, TAYLOR_KEEP = 4, 2.5
EPS_LN = 1e-5


def need(eng, sem, value):
    if isinstance(value, int) and value <= 0:
        return
    eng.wait_ge(sem, value)


def mm3(nc, out, a, b, start, stop):
    nc.tensor.matmul(out, a[0], b[1], start=start, stop=False)
    nc.tensor.matmul(out, a[0], b[0], start=False, stop=False)
    return nc.tensor.matmul(out, a[1], b[0], start=False, stop=stop)


def as_f32(ap):
    return ap.bitcast(F32)


SEMAPHORES = []


def clear_semaphores(nc):
    with nc.Block() as block:
        @block.gpsimd
        def _(pool):
            nc.clear_and_free_semaphores(list(SEMAPHORES))
    SEMAPHORES.clear()


class Space:

    def __init__(self, nc, ctx, tag):
        self.nc, self.ctx, self.tag = nc, ctx, tag

    def sb(self, name, shape, dt=F32):
        return self.ctx.enter_context(self.nc.sbuf_tensor(f"{self.tag}_{name}", shape, dt))

    def pair(self, name, shape):
        return self.sb(name + "_hi", shape, F32R), self.sb(name + "_lo", shape, F32R)

    def twins(self, name, shape):
        at = self.nc.sbuf_base
        raw = self.sb(name, shape)
        assert at % 32 == 0
        return raw, self.nc.alloc_sbuf_tensor_at(f"{self.tag}_{name}_r", shape, F32R, offset=at)

    def ps(self, name, banks=1):
        return self.ctx.enter_context(self.nc.psum_tensor(f"{self.tag}_{name}", [P, 512 * banks], F32))

    def sem(self, name):
        sem = self.nc.alloc_semaphore(f"{self.tag}_{name}")
        SEMAPHORES.append(sem)
        return sem


class LayerNormT:

    def __init__(self, nc, s, x, ident, xT, banks, xn=None):
        self.nc, self.x, self.ident, self.xT, self.banks = nc, x, ident, xT, banks
        self.stats = s.sb("ln_stats", [P, TT, 6])
        self.mv = s.sb("ln_mv", [P, TT, 2])
        self.rstd = s.sb("ln_rstd", [P, TT, 3])
        self.xn = xn if xn is not None else s.sb("ln_xn", [P, TT, D])
        self.stats_done = s.sem("ln_stats_done")
        self.mv_done = s.sem("ln_mv_done")
        self.eps_added = s.sem("ln_eps_added")
        self.rstd_done = s.sem("ln_rstd_done")
        self.normed = s.sem("ln_normed")
        self.transposed = s.sem("ln_transposed")
        self.hi_ready = s.sem("ln_hi_ready")
        self.lo_ready = s.sem("ln_lo_ready")

    def vector(self, dve, between=None):
        nc = self.nc
        for t in range(TT):
            nc.vector.bn_stats(self.stats[:, t, :], self.x[:, t, :]).then_inc(self.stats_done, 1)
        for t in range(TT):
            dve.wait_ge(self.stats_done, t + 1)
            nc.vector.bn_aggr(self.mv[:, t, :], self.stats[:, t, :]).then_inc(self.mv_done, 1)
        dve.wait_ge(self.rstd_done, 1)
        for t in range(TT):
            nc.vector.tensor_scalar(self.xn[:, t, :], self.x[:, t, :], self.mv[:, t, 0:1],
                                    self.rstd[:, t, 1:2], ALU.subtract, ALU.mult).then_inc(self.normed, 1)
        if between is not None:
            between()
        for t in range(TT):
            dve.wait_ge(self.hi_ready, t + 1)
            nc.vector.tensor_tensor(self.xT[1][:, :, t * P:(t + 1) * P],
                                    self.banks[t][:, :].rearrange("p (c k) -> p c k", c=DC),
                                    as_f32(self.xT[0][:, :, t * P:(t + 1) * P]),
                                    ALU.subtract).then_inc(self.lo_ready, 1)

    def gpsimd(self, pool):
        nc = self.nc
        nc.gpsimd.memset(self.rstd[:, :, 2:3], -0.5).then_inc(self.eps_added, 1)
        pool.wait_ge(self.mv_done, TT)
        nc.gpsimd.tensor_scalar(self.rstd[:, :, 0:1], self.mv[:, :, 1:2], EPS_LN, None,
                                ALU.add).then_inc(self.eps_added, 1)
        pool.wait_ge(self.eps_added, 2)
        nc.gpsimd.tensor_tensor(self.rstd[:, :, 1:2], self.rstd[:, :, 0:1], self.rstd[:, :, 2:3],
                                ALU.pow).then_inc(self.rstd_done, 1)

    def tensor(self, pe):
        for t in range(TT):
            pe.wait_ge(self.normed, t + 1)
            for c in range(DC):
                last = self.nc.tensor.transpose(self.banks[t][:, c * P:(c + 1) * P],
                                                self.xn[:, t, c * P:(c + 1) * P], self.ident[:])
            last.then_inc(self.transposed, 1)

    def scalar(self, act):
        for t in range(TT):
            act.wait_ge(self.transposed, t + 1)
            self.nc.scalar.activation(self.xT[0][:, :, t * P:(t + 1) * P],
                                      self.banks[t][:, :].rearrange("p (c k) -> p c k", c=DC),
                                      ACT.Copy).then_inc(self.hi_ready, 1)

    def wait_ready(self, pe):
        pe.wait_ge(self.lo_ready, TT)


class WeightStream:

    def __init__(self, nc, s, name, width, stage=None, split=None, preloaded=False):
        self.nc, self.width, self.ahead = nc, width, int(preloaded)
        self.stage = stage if stage is not None else s.sb(name + "_stage", [P, 2, width])
        self.split = split if split is not None else s.pair(name, [P, 2, width])
        self.loaded = [s.sem(f"{name}_loaded{i}") for i in range(2)]
        self.hi_ready = s.sem(name + "_hi_ready")
        self.lo_ready = s.sem(name + "_lo_ready")

    def load(self, sp, src, pair, slot):
        need(sp, self.lo_ready, 2 * pair + slot - 1)
        sp.dma_start(self.stage[:, slot, :], src).then_inc(self.loaded[slot], 16)

    def make_hi(self, act, pair, slot, used, per_tile, width=None):
        w = width or self.width
        need(act, self.loaded[slot], (pair + 1 - self.ahead) * 16)
        need(act, used, per_tile * (2 * pair + slot - 1))
        self.nc.scalar.activation(self.split[0][:, slot, :w], self.stage[:, slot, :w],
                                  ACT.Copy).then_inc(self.hi_ready, 1)

    def make_lo(self, dve, pair, slot, width=None):
        w = width or self.width
        dve.wait_ge(self.hi_ready, 2 * pair + slot + 1)
        self.nc.vector.tensor_tensor(self.split[1][:, slot, :w], self.stage[:, slot, :w],
                                     as_f32(self.split[0][:, slot, :w]),
                                     ALU.subtract).then_inc(self.lo_ready, 1)

    def wait_tile(self, pe, pair, slot):
        pe.wait_ge(self.lo_ready, 2 * pair + slot + 1)

    def tile(self, slot):
        return self.split[0][:, slot, :], self.split[1][:, slot, :]


def peeled(eng, count, step):
    step(0)
    with eng.Fori(1, count - 1) as i:
        step(i)
    step(count - 1)


def is_at(i, value):
    return isinstance(i, int) and i == value


def cross_attention(nc, tag, g, w, eps, latents_as_keys):
    latents = latents_as_keys
    with ExitStack() as outer:
        so = Space(nc, outer, tag)
        qT = so.sb("qT", [P, B, HEADS, SEQ])
        with ExitStack() as inner:
            si = Space(nc, inner, tag)
            wkv_raw, wkv_lo = si.twins("wkv_lo", [P, 4, DC * UW])
            wkv = si.sb("wkv_hi", [P, 4, DC * UW], F32R), wkv_lo
            mask = si.sb("mask", [P, CTX]) if w["mask"] is not None else None
            klatT = si.sb("klatT", [P, KVH, TOK]) if latents else None
            vlat = si.sb("vlat", [SEQ, 2, UW]) if latents else None
            vl_stored = si.sem("vl_stored")
            context = Context(nc, si, w["ctx"])
            wo = OutputWeights(nc, si, w["wo"], wkv, wkv_raw)
            queries(nc, tag + "q", g, w, eps, wkv, wkv_raw, qT, mask, klatT, context, vl_stored)
            attend(nc, tag + "a", g, w, eps, wkv, qT, mask, klatT, vlat, context, wo, vl_stored)
            project_out(nc, tag + "o", g, w, qT, wo)


class Context:

    def __init__(self, nc, s, src):
        self.nc, self.src = nc, src
        self.raw, lo = s.twins("cT_lo", [P, CT, DC * P])
        self.split = s.sb("cT_hi", [P, CT, DC * P], F32R), lo
        self.loaded = [s.sem(f"ctx_loaded{k}") for k in range(CT)]
        self.hi_ready = s.sem("ctx_hi")
        self.lo_ready = s.sem("ctx_lo")

    def load(self, sp, b, k):
        sp.dma_start(self.raw[:, k, :],
                     self.src[bass.ds(b, 1), :, k * DC * P:(k + 1) * DC * P].rearrange("b p n -> p (b n)")
                     ).then_inc(self.loaded[k], 16)

    def make_hi(self, act, b, k):
        act.wait_ge(self.loaded[k], 16 * b + 16)
        self.nc.scalar.activation(self.split[0][:, k, :], self.raw[:, k, :],
                                  ACT.Copy).then_inc(self.hi_ready, 1)

    def make_lo(self, dve, b, k):
        dve.wait_ge(self.hi_ready, CT * b + k + 1)
        self.nc.vector.tensor_tensor(self.split[1][:, k, :], self.raw[:, k, :],
                                     as_f32(self.split[0][:, k, :]), ALU.subtract).then_inc(self.lo_ready, 1)

    def wait_tile(self, pe, b, k):
        pe.wait_ge(self.lo_ready, CT * b + k + 1)


class OutputWeights:
    RING = 4
    PLACES = (0, 2, 1, 3)

    def __init__(self, nc, s, src, wkv, wkv_raw):
        self.nc, self.src, self.wkv, self.wkv_raw = nc, src, wkv, wkv_raw
        self.loaded = [s.sem(f"wo_loaded{i}") for i in range(self.RING)]
        self.hi_ready = s.sem("wo_hi")
        self.lo_ready = s.sem("wo_lo")

    def tile(self, n):
        return tuple(h[:, self.PLACES[n % self.RING], :] for h in self.wkv)

    def raw(self, n):
        return self.wkv_raw[:, self.PLACES[n % self.RING], :]

    def load(self, sp, n):
        sp.dma_start(self.raw(n), self.src[n]).then_inc(self.loaded[n % self.RING], 16)

    def make_hi(self, act, n):
        act.wait_ge(self.loaded[n % self.RING], 16 * (n // self.RING) + 16)
        self.nc.scalar.activation(self.tile(n)[0], self.raw(n), ACT.Copy).then_inc(self.hi_ready, 1)

    def make_lo(self, eng, n, subtract):
        eng.wait_ge(self.hi_ready, n + 1)
        hi, lo = self.tile(n)
        subtract(lo, self.raw(n), as_f32(hi), ALU.subtract).then_inc(self.lo_ready, 1)


def queries(nc, tag, g, w, eps, wkv, wkv_raw, qT, mask, klatT, context, vl_stored):
    x, ident = g["x"], g["ident"]
    NQ = HEADS // UNIT_H
    NL = 2 * TT if klatT is not None else 0
    N0 = NQ * TT
    NN = N0 + NL
    assert NQ // 2 == 4
    SLOTS, LAG = 4, 2
    with ExitStack() as ctx:
        s = Space(nc, ctx, tag)
        xT = s.pair("xT", [P, DC, TOK])
        tbank = [s.ps(f"tbank{i}") for i in range(2)]
        pbank = [s.ps(f"pbank{i}") for i in range(SLOTS)]
        xn = s.sb("xn", [P, SLOTS, UW])
        ln = LayerNormT(nc, s, x, ident, xT, tbank, xn[:, 0:TT, :])
        stream = WeightStream(nc, s, "w", DC * UW, stage=g["stage"], preloaded=w["preloaded"])
        nk = s.sb("norm", [P, 4])
        sq = s.sb("sq", [P, 2, UW])
        ss = s.sb("ss", [P, SLOTS, UNIT_H])
        ms = s.sb("ms", [P, SLOTS, UNIT_H])
        rstd = s.sb("rstd", [P, SLOTS, UNIT_H])
        const = s.sb("const", [P, 2, UNIT_H])
        vl = g["stage"][:, 0, :].rearrange("p (t n) -> p t n", t=TT) if klatT is not None else None

        small_loaded = s.sem("small_loaded")
        wkv_hi = s.sem("wkv_hi")
        wkv_lo = s.sem("wkv_lo")
        wkv_loaded = s.sem("wkv_loaded")
        const_set = s.sem("const_set")
        norm_ready = s.sem("norm_ready")
        projected = s.sem("projected")
        squared = s.sem("squared")
        summed = s.sem("summed")
        meaned = s.sem("meaned")
        rstd_ready = s.sem("rstd_ready")
        normed = s.sem("normed")
        transposed = s.sem("transposed")
        placed = s.sem("placed")
        vl_proj = s.sem("vl_proj")
        vl_ready = s.sem("vl_ready")

        WKH = DC * UW // 2

        def wkv_half(part, i, slot):
            return (*wkv, wkv_raw)[part][:, bass.ds(i, 1), slot * WKH:(slot + 1) * WKH]

        with nc.Block() as block:
            @block.sync
            def _(sp):
                sp.dma_start(nk[:, 0:2], w["norm"]).then_inc(small_loaded, 16)

                def step(i):
                    for slot in range(2):
                        if not (w["preloaded"] and is_at(i, 0)):
                            stream.load(sp, w["wq"][bass.ds(2 * i + slot, 1), :, :]
                                        .rearrange("a p n -> p (a n)"), i, slot)
                        need(sp, wkv_loaded, 16 * (2 * i + slot))
                        sp.dma_start(wkv_half(2, i, slot).rearrange("p a n -> p (a n)"),
                                     w["wkv"][bass.ds(i, 1), :, slot * WKH:(slot + 1) * WKH]
                                     .rearrange("a p n -> p (a n)")).then_inc(wkv_loaded, 16)
                    if is_at(i, 0):
                        for k in range(CT):
                            context.load(sp, 0, k)
                peeled(sp, NQ // 2, step)
                if vl is not None:
                    sp.wait_ge(vl_ready, 2 * TT)
                    sp.dma_start(g["vlat_dram"].rearrange("(t p) n -> p t n", p=P), vl).then_inc(vl_stored, 16)

            @block.gpsimd
            def _(pool):
                ln.gpsimd(pool)
                nc.gpsimd.memset(const[:, 0, :], -0.5).then_inc(const_set, 1)
                nc.gpsimd.memset(const[:, 1, :], eps).then_inc(const_set, 1)

                def rstd_of(n, k):
                    pool.wait_ge(const_set, 2)
                    pool.wait_ge(summed, n + 1)
                    nc.gpsimd.tensor_tensor(ms[:, k, :], ss[:, k, :], const[:, 1, :],
                                            ALU.add).then_inc(meaned, 1)
                    pool.wait_ge(meaned, n + 1)
                    nc.gpsimd.tensor_tensor(rstd[:, k, :], ms[:, k, :], const[:, 0, :],
                                            ALU.pow).then_inc(rstd_ready, 1)

                def wkv_lo_of(i, slot):
                    nc.gpsimd.tensor_tensor(wkv_half(1, i, slot), wkv_half(2, i, slot),
                                            as_f32(wkv_half(0, i, slot)), ALU.subtract).then_inc(wkv_lo, 1)

                def step(i):
                    for slot in range(2):
                        need(pool, wkv_hi, 2 * i + slot)
                        for t in range(TT):
                            rstd_of(SLOTS * i + slot * TT + t, slot * TT + t)
                        if slot == 1:
                            wkv_lo_of(i, 0)
                        elif not is_at(i, 0):
                            wkv_lo_of(i - 1, 1)
                peeled(pool, NQ // 2, step)
                pool.wait_ge(wkv_hi, NQ)
                wkv_lo_of(NQ // 2 - 1, 1)
                for j in range(NL):
                    rstd_of(N0 + j, j)

            @block.tensor
            def _(pe):
                ln.tensor(pe)
                ln.wait_ready(pe)

                def project(t, wt, bank):
                    for c in range(DC):
                        a = tuple(h[:, c, t * P:(t + 1) * P] for h in xT)
                        last = mm3(nc, bank[:], a, tuple(h[:, c * UW:(c + 1) * UW] for h in wt),
                                   c == 0, c == DC - 1)
                    return last

                def transposes(n, k):
                    if isinstance(n, int) and n < 0:
                        return
                    pe.wait_ge(normed, n + 1)
                    need(pe, placed, n - 1)
                    for h in range(UNIT_H):
                        last = nc.tensor.transpose(tbank[k % 2][:, h * P:(h + 1) * P],
                                                   xn[:, k, h * P:(h + 1) * P], ident[:])
                    last.then_inc(transposed, 1)

                def step(i):
                    for slot in range(2):
                        stream.wait_tile(pe, i, slot)
                        for t in range(TT):
                            k = slot * TT + t
                            n = SLOTS * i + k
                            need(pe, normed, n - SLOTS + 1)
                            project(t, stream.tile(slot), pbank[k]).then_inc(projected, 1)
                            transposes(n - LAG, (k - LAG) % SLOTS)
                peeled(pe, NQ // 2, step)
                if vl is not None:
                    for j in range(NL):
                        half, t = divmod(j, TT)
                        pe.wait_ge(wkv_lo, 2 * half + 2)
                        pe.wait_ge(normed, N0 + j - SLOTS + 1)
                        project(t, tuple(h[:, half, :] for h in wkv), pbank[j]).then_inc(projected, 1)
                        transposes(N0 + j - LAG, (j - LAG) % SLOTS)
                    for j in range(2 * TT):
                        half, t = divmod(j, TT)
                        pe.wait_ge(wkv_lo, 2 * half + 6)
                        pe.wait_ge(normed, N0 + j + 1)
                        project(t, tuple(h[:, 2 + half, :] for h in wkv), pbank[j]).then_inc(vl_proj, 1)
                        if j < LAG:
                            transposes(NN - LAG + j, (NN - LAG + j) % SLOTS)
                    return
                for n in range(NN - LAG, NN):
                    transposes(n, n % SLOTS)

            @block.scalar
            def _(act):
                stream.make_hi(act, 0, 0, projected, TT)
                ln.scalar(act)

                def square(n, k):
                    act.wait_ge(projected, n + 1)
                    need(act, summed, n - 1)
                    nc.scalar.activation(sq[:, k % 2, :], pbank[k][:], ACT.Square, scale=HD ** -0.5).then_inc(squared, 1)

                def place_latents(j):
                    half, t = divmod(j, TT)
                    act.wait_ge(transposed, N0 + j + 1)
                    nc.scalar.activation(klatT[:, half * UNIT_H:(half + 1) * UNIT_H, t * P:(t + 1) * P],
                                         tbank[j % 2][:, :].rearrange("p (h k) -> p h k", h=UNIT_H),
                                         ACT.Copy).then_inc(placed, 1)

                def place_queries(i, k):
                    slot, t = divmod(k, TT)
                    act.wait_ge(transposed, SLOTS * i + k + 1)
                    nc.scalar.activation(
                        qT[:, t * BT:(t + 1) * BT, bass.ds((2 * i + slot) * UNIT_H, UNIT_H), :],
                        tbank[k % 2][:, :].rearrange("p (h b q) -> p b h q", h=UNIT_H, b=BT),
                        ACT.Copy, scale=nk[:, 3:4]).then_inc(placed, 1)

                act.wait_ge(norm_ready, 2)

                def step(i):
                    for slot in range(2):
                        if slot == 0:
                            stream.make_hi(act, i, 1, projected, TT)
                        elif not is_at(i, NQ // 2 - 1):
                            stream.make_hi(act, i + 1, 0, projected, TT)
                        else:
                            for k in range(CT):
                                context.make_hi(act, 0, k)
                        act.wait_ge(wkv_loaded, 16 * (2 * i + slot) + 16)
                        nc.scalar.activation(wkv_half(0, i, slot), wkv_half(2, i, slot),
                                             ACT.Copy).then_inc(wkv_hi, 1)
                        for t in range(TT):
                            k = slot * TT + t
                            square(SLOTS * i + k, k)
                            if k >= LAG:
                                place_queries(i, k - LAG)
                            elif not is_at(i, 0):
                                place_queries(i - 1, k - LAG + SLOTS)
                peeled(act, NQ // 2, step)
                for j in range(max(NL, LAG)):
                    if NL:
                        square(N0 + j, j)
                    if j < LAG:
                        place_queries(NQ // 2 - 1, SLOTS - LAG + j)
                    else:
                        place_latents(j - LAG)
                if NL:
                    for j in range(2 * TT):
                        half, t = divmod(j, TT)
                        act.wait_ge(vl_proj, j + 1)
                        if j == 0:
                            act.wait_ge(stream.lo_ready, NQ)
                        nc.scalar.activation(vl[:, t, half * UW:(half + 1) * UW], pbank[j][:],
                                             ACT.Copy).then_inc(vl_ready, 1)
                        if j < LAG:
                            place_latents(NL - LAG + j)

            @block.vector
            def _(dve):
                def between():
                    dve.wait_ge(small_loaded, 16)
                    nc.vector.tensor_tensor(nk[:, 2:3], nk[:, 0:1], nk[:, 1:2], ALU.mult).then_inc(norm_ready, 1)
                    dve.wait_ge(norm_ready, 1)
                    nc.vector.tensor_scalar(nk[:, 3:4], nk[:, 2:3], HD ** -0.5, None,
                                            ALU.mult).then_inc(norm_ready, 1)
                    stream.make_lo(dve, 0, 0)
                ln.vector(dve, between)

                def heads(ap):
                    return ap.rearrange("p (h d) -> p h d", h=UNIT_H)

                def sums(n, k):
                    dve.wait_ge(squared, n + 1)
                    need(dve, rstd_ready, n - SLOTS + 1)
                    nc.vector.tensor_reduce(ss[:, k, :], heads(sq[:, k % 2, :]), AX.X,
                                            ALU.add).then_inc(summed, 1)

                def normalise(n, k):
                    if isinstance(n, int) and n < 0:
                        return
                    dve.wait_ge(rstd_ready, n + 1)
                    need(dve, transposed, n - SLOTS + 1)
                    nc.vector.tensor_tensor(heads(xn[:, k, :]), heads(pbank[k][:, :]),
                                            rstd[:, k, :].unsqueeze(2).broadcast_to([P, UNIT_H, HD]),
                                            ALU.mult).then_inc(normed, 1)
                def step(i):
                    for slot in range(2):
                        if slot == 0:
                            stream.make_lo(dve, i, 1)
                        elif not is_at(i, NQ // 2 - 1):
                            stream.make_lo(dve, i + 1, 0)
                        else:
                            for k in range(CT):
                                context.make_lo(dve, 0, k)
                        for t in range(TT):
                            k = slot * TT + t
                            n = SLOTS * i + k
                            sums(n, k)
                            normalise(n - 1, (k - 1) % SLOTS)
                peeled(dve, NQ // 2, step)
                for n in range(N0, NN):
                    sums(n, n % SLOTS)
                    normalise(n - 1, (n - 1) % SLOTS)
                normalise(NN - 1, (NN - 1) % SLOTS)


def attend(nc, tag, g, w, eps, wkv, qT, mask, klatT, vlat, context, wo, vl_stored):
    ident = g["ident"]
    tail = klatT is not None
    KEYS = CTX + (SEQ if tail else 0)
    with ExitStack() as ctx:
        s = Space(nc, ctx, tag)
        kT = (s.sb("kT_hi", [P, 2, UNIT_H, CTX], F32R),
              g["stage_r"][:, :, :].rearrange("p a (h n) -> p a h n", h=UNIT_H))
        v = s.sb("v", [P, 2, CT, UW])
        q = s.pair("q", [P, 2, UNIT_H, GROUP * SEQ])
        q_whole = s.sb("q_whole", [P, 2, UNIT_H, GROUP * SEQ]) if tail else None
        sq = s.sb("sq", [P, UW])
        kn = s.sb("kn", [P, 2, UW])
        ss = s.sb("ss", [P, 2, UNIT_H])
        ms = s.sb("ms", [P, 2, UNIT_H])
        rstd = s.sb("rstd", [P, 2, UNIT_H])
        const = s.sb("const", [P, 2, UNIT_H])
        sm = s.sb("sm", [P, 2, CTX]) if mask is not None else None
        smax = s.sb("smax", [P, CT])
        nmax = s.sb("nmax", [P, CT])
        rsum = s.sb("rsum", [P, CT])
        rinv = s.sb("rinv", [P, CT])
        p = s.sb("p", [P, 2, KEYS])
        pT = s.sb("pT", [P, 2, CT + 1, P])
        on = s.sb("on", [P, 2, HD])

        kbanks = s.ps("kbanks", 2)
        kbank = [kbanks[:, i * 512:(i + 1) * 512] for i in range(2)]
        vbank = s.ps("vbank")
        ktbank = s.ps("ktbank")
        sbank = s.ps("sbank", 2)
        ptbank = s.ps("ptbank")
        obank = s.ps("obank")
        TAIL_T = CTX + P
        OT = P

        const_set = s.sem("const_set")
        mask_loaded = s.sem("mask_loaded")
        k_proj = s.sem("k_proj")
        k_squared = s.sem("k_squared")
        k_summed = s.sem("k_summed")
        k_mean = s.sem("k_mean")
        k_rstd = s.sem("k_rstd")
        k_normed = s.sem("k_normed")
        kt_done = s.sem("kt_done")
        kt_hi = s.sem("kt_hi")
        kt_lo = s.sem("kt_lo")
        v_proj = s.sem("v_proj")
        v_ready = s.sem("v_ready")
        q_hi = s.sem("q_hi")
        q_lo = s.sem("q_lo")
        vlat_loaded = [s.sem(f"vlat_loaded{i}") for i in range(2)]
        s_done = s.sem("s_done")
        m_raw = s.sem("m_raw")
        m_done = s.sem("m_done")
        p_ready = s.sem("p_ready")
        pt_done = s.sem("pt_done")
        pt_ready = s.sem("pt_ready")
        o_done = s.sem("o_done")
        r_inv = s.sem("r_inv")
        o_normed = s.sem("o_normed")
        ot_done = s.sem("ot_done")
        ot_ready = s.sem("ot_ready")

        scores = [sbank, kbanks]
        ptbanks = [ptbank, vbank]
        obanks = [obank, ktbank]
        LAST = UNIT_H * (UNITS - 1)

        def run(eng, slot_step, finish):
            def both(b):
                slot_step(b, 0)
                slot_step(b, 1)
            peeled(eng, B, both)
            finish()

        def parts(b, hf):
            u = 2 * b + hf
            fixed = isinstance(u, int)
            return (not fixed or u > 0), (not fixed or u > 1), u

        with nc.Block() as block:
            @block.sync
            def _(sp):
                if mask is not None:
                    for h in range(GROUP):
                        sp.dma_start(mask[h * SEQ:(h + 1) * SEQ, :], w["mask"]).then_inc(mask_loaded, 16)

                def step(b, hf):
                    _, _, u = parts(b, hf)
                    if tail:
                        need(sp, o_done, UNIT_H * (u - 1))
                        if is_at(b, 0) and hf == 0:
                            sp.wait_ge(vl_stored, 16)
                        sp.dma_start(vlat[:, hf, :],
                                     g["vlat_dram"][bass.ds(b * SEQ, SEQ), hf * UW:(hf + 1) * UW]
                                     ).then_inc(vlat_loaded[hf], 16)
                    if is_at(b, B - 1) and hf == 1:
                        sp.wait_ge(v_proj, CT * u)
                        for n in range(2):
                            wo.load(sp, n)
                    if hf == 1 and not is_at(b, B - 1):
                        for k in range(CT):
                            sp.wait_ge(v_proj, CT * u + k + 1)
                            context.load(sp, b + 1, k)

                def finish():
                    sp.wait_ge(v_proj, CT * UNITS)
                    for n in range(2, wo.RING):
                        wo.load(sp, n)
                run(sp, step, finish)

            @block.gpsimd
            def _(pool):
                nc.gpsimd.memset(const[:, 0, :], -0.5).then_inc(const_set, 1)
                nc.gpsimd.memset(const[:, 1, :], eps).then_inc(const_set, 1)

                def step(b, hf):
                    _, _, u = parts(b, hf)
                    mine = qT[:, bass.ds(b, 1), hf * 16:(hf + 1) * 16, :].rearrange("p b h q -> p (b h q)")

                    def flat(ap):
                        return ap[:, hf, :, :].rearrange("p h n -> p (h n)")
                    need(pool, s_done, UNIT_H * (u - 1))
                    if tail:
                        nc.gpsimd.tensor_copy(flat(q_whole), mine)
                    nc.gpsimd.tensor_copy(flat(q[0]), mine).then_inc(q_hi, 1)
                    for k in range(CT):
                        n = CT * u + k
                        pool.wait_ge(const_set, 2)
                        if k == 0:
                            pool.wait_ge(q_hi, u + 1)
                        pool.wait_ge(k_summed, n + 1)
                        nc.gpsimd.tensor_tensor(ms[:, k % 2, :], ss[:, k % 2, :], const[:, 1, :],
                                                ALU.add).then_inc(k_mean, 1)
                        pool.wait_ge(k_mean, n + 1)
                        nc.gpsimd.tensor_tensor(rstd[:, k % 2, :], ms[:, k % 2, :], const[:, 0, :],
                                                ALU.pow).then_inc(k_rstd, 1)
                        if k == 0:
                            nc.gpsimd.tensor_tensor(flat(q[1]), mine, as_f32(flat(q[0])),
                                                    ALU.subtract).then_inc(q_lo, 1)

                def finish():
                    wo.make_lo(pool, 0, nc.gpsimd.tensor_tensor)
                run(pool, step, finish)

            @block.tensor
            def _(pe):
                def project(k, col, bank):
                    for c in range(DC):
                        a = tuple(h[:, k, c * P:(c + 1) * P] for h in context.split)
                        last = mm3(nc, bank[:, :], a, tuple(h[:, col, c * UW:(c + 1) * UW] for h in wkv),
                                   c == 0, c == DC - 1)
                    return last

                def score(a, bank, ahf, k, at):
                    last = mm3(nc, bank[:, 0:CTX], tuple(h[:, ahf, k, :] for h in q),
                               tuple(h[:, ahf, k, :] for h in kT), True, True)
                    if tail:
                        last = nc.tensor.matmul(bank[:, CTX:KEYS], q_whole[:, ahf, k, :],
                                                klatT[:, ahf * UNIT_H + k, bass.ds(at, SEQ)],
                                                start=True, stop=True)
                    last.then_inc(s_done, 1)

                def p_transpose(k, bank, tail_bank):
                    for t in range(CT):
                        last = nc.tensor.transpose(bank[:, t * P:(t + 1) * P],
                                                   p[:, k % 2, t * P:(t + 1) * P], ident[:])
                    if tail:
                        last = nc.tensor.transpose(tail_bank[0:SEQ, TAIL_T:TAIL_T + P],
                                                   p[:, k % 2, CTX:KEYS], ident[:])
                    last.then_inc(pt_done, 1)

                def pv(a, ahf, k, bank):
                    pe.wait_ge(pt_ready, a + 1)
                    for t in range(CT):
                        last = nc.tensor.matmul(bank[:, 0:HD], pT[:, k % 2, t, :],
                                                v[:, ahf, t, k * HD:(k + 1) * HD],
                                                start=(t == 0), stop=(t == CT - 1 and not tail))
                    if tail:
                        last = nc.tensor.matmul(bank[:, 0:HD], pT[0:SEQ, k % 2, CT, :],
                                                vlat[:, ahf, k * HD:(k + 1) * HD], start=False, stop=True)
                    last.then_inc(o_done, 1)

                def o_transpose(a, k, bank):
                    pe.wait_ge(o_normed, a + 1)
                    nc.tensor.transpose(bank[:, OT:OT + P], on[:, k % 2, :], ident[:]).then_inc(ot_done, 1)

                def kt(n, kb):
                    pe.wait_ge(k_normed, n + 1)
                    need(pe, kt_lo, n)
                    for h in range(UNIT_H):
                        last = nc.tensor.transpose(ktbank[:, h * P:(h + 1) * P],
                                                   kn[:, kb, h * P:(h + 1) * P], ident[:])
                    last.then_inc(kt_done, 1)

                def wait_unit(u, ahf, b_loads):
                    pe.wait_ge(kt_lo, CT * u)
                    pe.wait_ge(q_lo, u)
                    pe.wait_ge(v_ready, CT * u)
                    if tail:
                        pe.wait_ge(vlat_loaded[ahf], 16 * b_loads)

                def step(b, hf):
                    attends, lags, u = parts(b, hf)
                    ahf = 1 - hf
                    for k in range(CT):
                        n = CT * u + k
                        a = n - UNIT_H
                        lag = attends and (lags or k > 0)
                        if hf == 0:
                            context.wait_tile(pe, b, k)
                        need(pe, k_normed, n - 1)
                        project(k, hf, kbank[k % 2]).then_inc(k_proj, 1)
                        if lag:
                            need(pe, ot_ready, a - 1)
                            pv(a - 1, ahf if k else hf, (k - 1) % UNIT_H, obank)
                        if attends:
                            if k == 0:
                                wait_unit(u, ahf, b if hf == 0 else b + 1)
                            need(pe, p_ready, a)
                            need(pe, pt_ready, a)
                            score(a, sbank, ahf, k, (b - 1 if hf == 0 else b) * SEQ)
                        elif k > 0:
                            kt(n - 1, (k - 1) % 2)
                        need(pe, v_ready, n)
                        project(k, 2 + hf, vbank).then_inc(v_proj, 1)
                        if attends:
                            pe.wait_ge(p_ready, a + 1)
                            p_transpose(k, ptbank, sbank)
                        if attends or k == CT - 1:
                            kt(n, k % 2)
                        if lag:
                            o_transpose(a - 1, (k - 1) % 2, obank)

                def finish():
                    at = (B - 1) * SEQ
                    pe.wait_ge(ot_ready, LAST - 1)
                    pv(LAST - 1, 0, UNIT_H - 1, obank)
                    wait_unit(UNITS, 1, B)
                    pe.wait_ge(p_ready, LAST)
                    pe.wait_ge(pt_ready, LAST)
                    for k in range(2):
                        score(LAST + k, scores[k], 1, k, at)
                    o_transpose(LAST - 1, 1, obank)
                    for pair in range(0, UNIT_H, 2):
                        for k in (pair, pair + 1):
                            pe.wait_ge(p_ready, LAST + k + 1)
                            p_transpose(k, ptbanks[k % 2], scores[k % 2])
                        for k in (pair, pair + 1):
                            pe.wait_ge(ot_ready, LAST + max(0, k - 1))
                            pv(LAST + k, 1, k, obanks[k % 2])
                            if k + 2 < UNIT_H:
                                score(LAST + k + 2, scores[k % 2], 1, k + 2, at)
                        for k in (pair, pair + 1):
                            o_transpose(LAST + k, k, obanks[k % 2])
                run(pe, step, finish)

            @block.scalar
            def _(act):
                def place_k(n, kb, kk, u):
                    act.wait_ge(kt_done, n + 1)
                    need(act, s_done, UNIT_H * (u - 1))
                    nc.scalar.activation(kT[0][:, kb, :, kk * P:(kk + 1) * P],
                                         ktbank[:, :].rearrange("p (h n) -> p h n", h=UNIT_H),
                                         ACT.Copy).then_inc(kt_hi, 1)

                def exponential(a, k, bank):
                    act.wait_ge(m_done, a + 1)
                    need(act, pt_done, a - 1)
                    src = sm[:, k % 2, :] if mask is not None else bank[:, 0:KEYS]
                    nc.scalar.activation(p[:, k % 2, :], src, ACT.Exp, bias=nmax[:, k:k + 1],
                                         accum_out=rsum[:, k:k + 1]).then_inc(p_ready, 1)

                def step(b, hf):
                    attends, _, u = parts(b, hf)
                    for k in range(CT):
                        n = CT * u + k
                        act.wait_ge(k_proj, n + 1)
                        need(act, k_summed, n)
                        nc.scalar.activation(sq[:], kbank[k % 2], ACT.Square, scale=HD ** -0.5).then_inc(k_squared, 1)
                        if attends:
                            exponential(n - UNIT_H, k, sbank)
                        act.wait_ge(v_proj, n + 1)
                        need(act, o_done, UNIT_H * (u - 1))
                        nc.scalar.activation(v[:, hf, k, :], vbank[:], ACT.Copy).then_inc(v_ready, 1)
                        place_k(n, hf, k, u)
                        if hf == 1 and k > 0 and not is_at(b, B - 1):
                            context.make_hi(act, b + 1, k - 1)
                        if hf == 0 and k == 0 and not is_at(b, 0):
                            context.make_hi(act, b, CT - 1)

                def finish():
                    for k in range(UNIT_H):
                        exponential(LAST + k, k, scores[k % 2])
                        if k % 2:
                            wo.make_hi(act, k // 2)
                run(act, step, finish)

            @block.vector
            def _(dve):
                def lo_of_k(n, kb, kk):
                    dve.wait_ge(kt_hi, n + 1)
                    nc.vector.tensor_tensor(kT[1][:, kb, :, kk * P:(kk + 1) * P],
                                            ktbank[:, :].rearrange("p (h n) -> p h n", h=UNIT_H),
                                            as_f32(kT[0][:, kb, :, kk * P:(kk + 1) * P]),
                                            ALU.subtract).then_inc(kt_lo, 1)

                def inverse_sum(k):
                    nc.vector.reciprocal(rinv[:, k:k + 1], rsum[:, k:k + 1]).then_inc(r_inv, 1)

                def maximum(a, k, bank):
                    if mask is None:
                        nc.vector.tensor_reduce(nmax[:, k:k + 1], bank[:, 0:KEYS], AX.X, ALU.max,
                                                negate=True).then_inc(m_done, 1)
                    else:
                        nc.vector.tensor_tensor_reduce(
                            out=sm[:, k % 2, :], in0=bank[:, 0:CTX], in1=mask[:], scale=1.0, scalar=-3.4e38,
                            op0=ALU.add, op1=ALU.max, accum_out=smax[:, k:k + 1]).then_inc(m_raw, 1)
                        dve.wait_ge(m_raw, a + 1)
                        nc.vector.tensor_scalar(nmax[:, k:k + 1], smax[:, k:k + 1], -1.0, None,
                                                ALU.mult).then_inc(m_done, 1)

                def o_norm(a, kk, bank):
                    dve.wait_ge(o_done, a + 1)
                    dve.wait_ge(r_inv, a + 1)
                    need(dve, ot_done, a - 1)
                    nc.vector.tensor_scalar(on[:, kk % 2, :], bank[:, 0:HD], rinv[:, kk:kk + 1], None,
                                            ALU.mult).then_inc(o_normed, 1)

                def pt_copy(a, k, bank, tail_bank):
                    dve.wait_ge(pt_done, a + 1)
                    need(dve, o_done, a - 1)
                    last = nc.vector.tensor_copy(pT[:, k % 2, 0:CT, :],
                                                 bank[:, :].rearrange("p (t n) -> p t n", t=CT))
                    if tail:
                        last = nc.vector.tensor_copy(pT[0:SEQ, k % 2, CT, :], tail_bank[0:SEQ, TAIL_T:TAIL_T + P])
                    last.then_inc(pt_ready, 1)

                def ot_place(a, b, hf, kk, bank):
                    dve.wait_ge(ot_done, a + 1)
                    nc.vector.tensor_copy(
                        qT[:, bass.ds(b, 1), (hf * UNIT_H + kk) * GROUP:(hf * UNIT_H + kk + 1) * GROUP, :]
                        .rearrange("p b h q -> p (b h q)"),
                        bank[:, OT:OT + P]).then_inc(ot_ready, 1)

                def step(b, hf):
                    attends, lags, u = parts(b, hf)
                    for k in range(CT):
                        n = CT * u + k
                        a = n - UNIT_H
                        lag = attends and (lags or k > 0)
                        if k:
                            lb, lhf, lk = (b, 0, k - 1) if hf == 1 else (b - 1, 1, k - 1)
                        else:
                            lb, lhf, lk = b - 1, hf, CT - 1
                        dve.wait_ge(k_squared, n + 1)
                        nc.vector.tensor_reduce(ss[:, k % 2, :],
                                                sq[:, :].rearrange("p (h d) -> p h d", h=UNIT_H),
                                                AX.X, ALU.add).then_inc(k_summed, 1)
                        if attends:
                            if mask is not None:
                                dve.wait_ge(mask_loaded, 16 * GROUP)
                            dve.wait_ge(s_done, a + 1)
                            need(dve, p_ready, a)
                        if lag:
                            inverse_sum(lk)
                        if attends:
                            maximum(a, k, sbank)
                        if lag:
                            o_norm(a - 1, lk, obank)
                        dve.wait_ge(k_rstd, n + 1)
                        need(dve, kt_done, n - 1)
                        nc.vector.tensor_tensor(
                            kn[:, k % 2, :].rearrange("p (h d) -> p h d", h=UNIT_H),
                            kbank[k % 2].rearrange("p (h d) -> p h d", h=UNIT_H),
                            rstd[:, k % 2, :].unsqueeze(2).broadcast_to([P, UNIT_H, HD]),
                            ALU.mult).then_inc(k_normed, 1)
                        if attends:
                            pt_copy(a, k, ptbank, sbank)
                        lo_of_k(n, hf, k)
                        if lag:
                            ot_place(a - 1, lb, lhf, lk, obank)
                        if hf == 1 and k > 0 and not is_at(b, B - 1):
                            context.make_lo(dve, b + 1, k - 1)
                        if hf == 0 and k == 0 and not is_at(b, 0):
                            context.make_lo(dve, b, CT - 1)

                def finish():
                    dve.wait_ge(p_ready, LAST)
                    inverse_sum(UNIT_H - 1)
                    o_norm(LAST - 1, UNIT_H - 1, obank)
                    for k in range(2):
                        dve.wait_ge(s_done, LAST + k + 1)
                        maximum(LAST + k, k, scores[k])
                    ot_place(LAST - 1, B - 1, 0, UNIT_H - 1, obank)
                    for pair in range(0, UNIT_H, 2):
                        for k in (pair, pair + 1):
                            pt_copy(LAST + k, k, ptbanks[k % 2], scores[k % 2])
                        for k in (pair, pair + 1):
                            dve.wait_ge(p_ready, LAST + k + 1)
                            inverse_sum(k)
                            if k + 2 < UNIT_H:
                                dve.wait_ge(s_done, LAST + k + 3)
                                maximum(LAST + k + 2, k + 2, scores[k % 2])
                            o_norm(LAST + k, k, obanks[k % 2])
                        for k in (pair, pair + 1):
                            ot_place(LAST + k, B - 1, 1, k, obanks[k % 2])
                    dve.wait_ge(ot_ready, LAST + UNIT_H)
                if tail:
                    dve.wait_ge(vl_stored, 16)
                run(dve, step, finish)


def project_out(nc, tag, g, w, oT, wo):
    x = g["x"]
    NW = HEADS // GROUP
    HI, LO = 2, 1
    with ExitStack() as ctx:
        s = Space(nc, ctx, tag)
        o = s.pair("o", [P, 2, GROUP, TOK])
        ybank = [s.ps(f"ybank{t}") for t in range(TT)]
        o_hi = s.sem("o_hi")
        o_lo = s.sem("o_lo")
        used = s.sem("used")
        added = s.sem("added")

        def heads_of(n):
            return oT[:, :, n * GROUP:(n + 1) * GROUP, :].rearrange("p b h q -> p h b q")

        def split_of(half, n):
            return half[:, n % 2, :, :].rearrange("p h (b q) -> p h b q", b=B)

        with nc.Block() as block:
            @block.sync
            def _(sp):
                for n in range(wo.RING, NW):
                    sp.wait_ge(used, n - wo.RING + 1)
                    wo.load(sp, n)

            @block.scalar
            def _(act):
                for n in range(NW):
                    need(act, used, n - 1)
                    nc.scalar.activation(split_of(o[0], n), heads_of(n), ACT.Copy).then_inc(o_hi, 1)
                    if n >= HI:
                        wo.make_hi(act, n)

            @block.vector
            def _(dve):
                for n in range(NW):
                    dve.wait_ge(o_hi, n + 1)
                    nc.vector.tensor_tensor(split_of(o[1], n), heads_of(n), as_f32(split_of(o[0], n)),
                                            ALU.subtract).then_inc(o_lo, 1)
                    if n >= LO:
                        wo.make_lo(dve, n, nc.vector.tensor_tensor)
                dve.wait_ge(used, NW)
                for t in range(TT):
                    nc.vector.tensor_tensor(x[:, t, :], x[:, t, :], ybank[t][:], ALU.add).then_inc(added, 1)
                dve.wait_ge(added, TT)

            @block.tensor
            def _(pe):
                for n in range(NW):
                    pe.wait_ge(o_lo, n + 1)
                    pe.wait_ge(wo.lo_ready, n + 1)
                    wt = wo.tile(n)
                    for h in range(GROUP):
                        for t in range(TT):
                            last = mm3(nc, ybank[t][:],
                                       tuple(half[:, n % 2, h, t * P:(t + 1) * P] for half in o),
                                       tuple(half[:, h * D:(h + 1) * D] for half in wt),
                                       n == 0 and h == 0, n == NW - 1 and h == GROUP - 1)
                    last.then_inc(used, 1)


class GatedTiles:
    RING = 4
    GU = 2 * DC * P
    WIDTH = GU + D

    def __init__(self, nc, s, xT, tiles):
        self.nc, self.xT, self.tiles = nc, xT, tiles
        self.stage = s.sb("stage", [P, self.RING, self.WIDTH])
        self.gu = s.pair("gu", [P, 2, self.GU])
        self.dn = s.pair("dn", [P, 2, D])
        self.sg = s.sb("sg", [P, 2, TOK])
        self.a = s.sb("a", [P, 2, TOK])
        self.raw = s.sb("raw", [P, TOK])
        self.act = s.pair("act", [P, 2, TOK])
        self.gubank = [s.ps(f"gubank{i}") for i in range(2)]
        self.ybank = [s.ps(f"ybank{i}") for i in range(TT)]
        self.loaded = [s.sem(f"loaded{i}") for i in range(self.RING)]
        self.gu_hi_sem = s.sem("gu_hi")
        self.gu_lo_sem = s.sem("gu_lo")
        self.dn_hi_sem = s.sem("dn_hi")
        self.dn_lo_sem = s.sem("dn_lo")
        self.gu_done_sem = s.sem("gu_done")
        self.silu_done_sem = s.sem("silu_done")
        self.a_raw_sem = s.sem("a_raw")
        self.a_done_sem = s.sem("a_done")
        self.act_hi_sem = s.sem("act_hi")
        self.act_lo_sem = s.sem("act_lo")
        self.down_done_sem = s.sem("down_done")

    def load(self, sp, src, f, k):
        need(sp, self.dn_lo_sem, f - self.RING + 1)
        sp.dma_start(self.stage[:, k, :], src).then_inc(self.loaded[k], 16)

    def gu_hi(self, act, f, i, k):
        act.wait_ge(self.loaded[k], i * 16 + 16)
        need(act, self.gu_done_sem, f - 1)
        self.nc.scalar.activation(self.gu[0][:, k % 2, :], self.stage[:, k, :self.GU],
                                  ACT.Copy).then_inc(self.gu_hi_sem, 1)

    def gu_lo(self, dve, f, k):
        dve.wait_ge(self.gu_hi_sem, f + 1)
        self.nc.vector.tensor_tensor(self.gu[1][:, k % 2, :], self.stage[:, k, :self.GU],
                                     as_f32(self.gu[0][:, k % 2, :]), ALU.subtract).then_inc(self.gu_lo_sem, 1)

    def scalar(self, act, f, i, k, last):
        nc, h = self.nc, k % 2
        if not last:
            self.gu_hi(act, f + 1, i + (k + 1) // self.RING, (k + 1) % self.RING)
        act.wait_ge(self.gu_done_sem, f + 1)
        need(act, self.a_done_sem, f - 1)
        nc.scalar.activation(self.sg[:, h, :], self.gubank[h][:, 0:TOK], ACT.Silu).then_inc(self.silu_done_sem, 1)
        need(act, self.down_done_sem, f - 1)
        nc.scalar.activation(self.dn[0][:, h, :], self.stage[:, k, self.GU:], ACT.Copy).then_inc(self.dn_hi_sem, 1)
        act.wait_ge(self.a_done_sem, f + 1)
        nc.scalar.activation(self.act[0][:, h, :], self.a[:, h, :], ACT.Copy).then_inc(self.act_hi_sem, 1)

    def vector(self, dve, f, k, last, combine=None):
        nc, h = self.nc, k % 2
        if not last:
            self.gu_lo(dve, f + 1, (k + 1) % self.RING)
        dve.wait_ge(self.silu_done_sem, f + 1)
        need(dve, self.act_hi_sem, f - 1)
        if combine is None:
            nc.vector.tensor_tensor(self.a[:, h, :], self.sg[:, h, :], self.gubank[h][:, TOK:2 * TOK],
                                    ALU.mult).then_inc(self.a_done_sem, 1)
        else:
            bank, sem, value, before = combine
            nc.vector.tensor_tensor(self.raw[:], self.sg[:, h, :], self.gubank[h][:, TOK:2 * TOK],
                                    ALU.mult).then_inc(self.a_raw_sem, 1)
            dve.wait_ge(sem, value)
            dve.wait_ge(self.a_raw_sem, before + 1)
            nc.vector.tensor_tensor(self.a[:, h, :], self.raw[:], bank, ALU.mult).then_inc(self.a_done_sem, 1)
        dve.wait_ge(self.dn_hi_sem, f + 1)
        nc.vector.tensor_tensor(self.dn[1][:, h, :], self.stage[:, k, self.GU:], as_f32(self.dn[0][:, h, :]),
                                ALU.subtract).then_inc(self.dn_lo_sem, 1)
        dve.wait_ge(self.act_hi_sem, f + 1)
        nc.vector.tensor_tensor(self.act[1][:, h, :], self.a[:, h, :], as_f32(self.act[0][:, h, :]),
                                ALU.subtract).then_inc(self.act_lo_sem, 1)

    def gate_up(self, pe, f, k):
        nc, h = self.nc, k % 2
        pe.wait_ge(self.gu_lo_sem, f + 1)
        need(pe, self.a_done_sem, f - 1)
        for part in range(2):
            for c in range(DC):
                at = (part * DC + c) * P
                last = mm3(nc, self.gubank[h][:, part * TOK:(part + 1) * TOK],
                           tuple(w[:, h, at:at + P] for w in self.gu),
                           tuple(v[:, c, :] for v in self.xT), c == 0, c == DC - 1)
        last.then_inc(self.gu_done_sem, 1)

    def down(self, pe, f, k, start, stop):
        nc, h = self.nc, k % 2
        pe.wait_ge(self.act_lo_sem, f + 1)
        pe.wait_ge(self.dn_lo_sem, f + 1)
        for t in range(TT):
            last = mm3(nc, self.ybank[t][:], tuple(v[:, h, t * P:(t + 1) * P] for v in self.act),
                       tuple(w[:, h, :] for w in self.dn), start, stop)
        last.then_inc(self.down_done_sem, 1)


def split_tile(nc, act=None, dve=None, dst=None, src=None, hi_done=None, lo_done=None):
    if act is not None:
        nc.scalar.activation(dst[0], src, ACT.Copy).then_inc(hi_done, 1)
    else:
        nc.vector.tensor_tensor(dst[1], src, as_f32(dst[0]), ALU.subtract).then_inc(lo_done, 1)


def mixer(nc, tag, g, a):
    x, ident = g["x"], g["ident"]
    NF = a["mix_ffn"].shape[0]
    NT = TAYLOR + 1
    with ExitStack() as ctx:
        s = Space(nc, ctx, tag)
        xT = s.pair("xT", [P, DC, TOK])
        tbank = [s.ps(f"tbank{i}") for i in range(2)]
        ln = LayerNormT(nc, s, x, ident, xT, tbank)
        G = GatedTiles(nc, s, xT, NF)
        praw = s.sb("praw", [P, 2 * DC * P])
        pw = s.pair("pw", [P, 2 * DC * P])
        traw = s.sb("traw", [P, NT, D])
        tw = s.pair("tw", [P, NT, D])
        point = s.sb("point", [P, 1])
        disc = s.sb("disc", [P, TAYLOR])
        factor = s.sb("factor", [P, TAYLOR])
        delta = s.sb("delta", [P, TOK])
        power = s.sb("power", [P, TAYLOR, TOK])
        keep = s.sb("keep", [P, 3, TOK])
        term = s.sb("term", [P, NT, TOK])
        term_s = s.pair("terms", [P, NT, TOK])
        mbank = s.ps("mbank")

        w_loaded = s.sem("w_loaded")
        t_loaded = s.sem("t_loaded")
        pw_hi = s.sem("pw_hi")
        pw_lo = s.sem("pw_lo")
        tw_hi = s.sem("tw_hi")
        tw_lo = s.sem("tw_lo")
        factor_done = s.sem("factor_done")
        m_proj = s.sem("m_proj")
        m_read = s.sem("m_read")
        poly = s.sem("poly")
        terms_done = s.sem("terms_done")
        term_hi = s.sem("term_hi")
        term_lo = s.sem("term_lo")
        t_done = s.sem("t_done")
        added = s.sem("added")

        assert NT <= NF - 2

        def order_of(pair, m):
            return tuple(h[:, m, :] for h in pair)

        def orders_at(f):
            i = f - (NF - 4)
            return range(i * NT // 4, (i + 1) * NT // 4)

        with nc.Block() as block:
            @block.sync
            def _(sp):
                sp.dma_start(praw[:], a["mix_proj"]).then_inc(w_loaded, 16)
                sp.dma_start(point[:], a["mix_point"]).then_inc(w_loaded, 16)
                sp.dma_start(disc[:], a["mix_disc"].partition_broadcast(P)).then_inc(w_loaded, 16)
                for f in range(NF):
                    G.load(sp, a["mix_ffn"][f], f, f % G.RING)
                    if f == 1:
                        sp.dma_start(traw[:], a["mix_out"]).then_inc(t_loaded, 16)

            @block.gpsimd
            def _(pool):
                ln.gpsimd(pool)
                pool.wait_ge(m_read, 2)
                pool.wait_ge(factor_done, 1)
                count = [0]

                def chain(ins):
                    ins.then_inc(poly, 1)
                    count[0] += 1
                    pool.wait_ge(poly, count[0])
                nc.gpsimd.tensor_scalar(keep[:, 0, :], delta[:], TAYLOR_KEEP, None, ALU.is_le).then_inc(poly, 1)
                count[0] += 1
                chain(nc.gpsimd.tensor_scalar(keep[:, 1, :], delta[:], -TAYLOR_KEEP, None, ALU.is_ge))
                chain(nc.gpsimd.tensor_tensor(keep[:, 2, :], keep[:, 0, :], keep[:, 1, :], ALU.mult))
                before = term[:, 0, :]
                for m in range(1, TAYLOR + 1):
                    chain(nc.gpsimd.tensor_tensor(power[:, m - 1, :], before, delta[:], ALU.mult))
                    before = power[:, m - 1, :]
                    if m > TAYLOR_MIN:
                        chain(nc.gpsimd.tensor_tensor(keep[:, m % 2, :], before, keep[:, 2, :], ALU.mult))
                        before = keep[:, m % 2, :]
                    last = nc.gpsimd.tensor_scalar(term[:, m, :], before, factor[:, m - 1:m], None, ALU.mult)
                last.then_inc(terms_done, 1)

            @block.tensor
            def _(pe):
                ln.tensor(pe)
                ln.wait_ready(pe)
                pe.wait_ge(pw_lo, 1)
                for part in range(2):
                    for c in range(DC):
                        at = (part * DC + c) * P
                        last = mm3(nc, mbank[:, part * TOK:(part + 1) * TOK],
                                   tuple(w[:, at:at + P] for w in pw),
                                   tuple(v[:, c, :] for v in xT), c == 0, c == DC - 1)
                last.then_inc(m_proj, 1)
                for f in range(NF):
                    G.gate_up(pe, f, f % G.RING)
                    if f:
                        G.down(pe, f - 1, (f - 1) % G.RING, f == 1, False)
                G.down(pe, NF - 1, (NF - 1) % G.RING, False, False)
                pe.wait_ge(term_lo, NT)
                pe.wait_ge(tw_lo, NT)
                for t in range(TT):
                    for m in range(NT):
                        last = mm3(nc, G.ybank[t][:], tuple(v[:, m, t * P:(t + 1) * P] for v in term_s),
                                   tuple(w[:, m, :] for w in tw), False, m == NT - 1)
                    last.then_inc(t_done, 1)

            @block.scalar
            def _(act):
                act.wait_ge(w_loaded, 48)
                split_tile(nc, act=act, dst=(pw[0][:], pw[1][:]), src=praw[:], hi_done=pw_hi)
                nc.scalar.activation(factor[:], disc[:], ACT.Exp, scale=-1.0).then_inc(factor_done, 1)
                ln.scalar(act)
                G.gu_hi(act, 0, 0, 0)
                act.wait_ge(m_proj, 1)
                nc.scalar.activation(term[:, 0, :], mbank[:, TOK:2 * TOK], ACT.Copy).then_inc(m_read, 1)
                for f in range(NF):
                    G.scalar(act, f, f // G.RING, f % G.RING, f == NF - 1)
                    if f == 1:
                        act.wait_ge(t_loaded, 16)
                    if 1 <= f <= NT:
                        split_tile(nc, act=act, dst=order_of(tw, f - 1), src=traw[:, f - 1, :], hi_done=tw_hi)
                    if f == NF - 4:
                        act.wait_ge(terms_done, 1)
                    if f >= NF - 4:
                        for m in orders_at(f):
                            split_tile(nc, act=act, dst=order_of(term_s, m), src=term[:, m, :], hi_done=term_hi)

            @block.vector
            def _(dve):
                ln.vector(dve)
                dve.wait_ge(pw_hi, 1)
                split_tile(nc, dve=dve, dst=(pw[0][:], pw[1][:]), src=praw[:], lo_done=pw_lo)
                G.gu_lo(dve, 0, 0)
                dve.wait_ge(m_read, 1)
                nc.vector.tensor_scalar(delta[:], mbank[:, 0:TOK], point[:, 0:1], None,
                                        ALU.subtract).then_inc(m_read, 1)
                for f in range(NF):
                    G.vector(dve, f, f % G.RING, f == NF - 1)
                    if 1 <= f <= NT:
                        dve.wait_ge(tw_hi, f)
                        split_tile(nc, dve=dve, dst=order_of(tw, f - 1), src=traw[:, f - 1, :], lo_done=tw_lo)
                    if f >= NF - 4:
                        for m in orders_at(f):
                            dve.wait_ge(term_hi, m + 1)
                            split_tile(nc, dve=dve, dst=order_of(term_s, m), src=term[:, m, :], lo_done=term_lo)
                for t in range(TT):
                    dve.wait_ge(t_done, t + 1)
                    nc.vector.tensor_tensor(x[:, t, :], x[:, t, :], G.ybank[t][:], ALU.add).then_inc(added, 1)


LORA_H, LORA_R = 1376, 2
LORA_REP = 4
LORA_HQ = LORA_H // LORA_REP
LORA_M = -(-LORA_HQ // P)
LORA_F = LORA_REP * LORA_M


def lora_ffn(nc, tag, g, a):
    x, ident = g["x"], g["ident"]
    with ExitStack() as ctx:
        s = Space(nc, ctx, tag)
        xT = s.pair("xT", [P, DC, TOK])
        tbank = [s.ps(f"tbank{i}") for i in range(2)]
        ln = LayerNormT(nc, s, x, ident, xT, tbank)
        graw = s.sb("graw", [P, 2, LORA_F * P])
        gw = s.pair("gw", [P, 2, LORA_F * P])
        draw = s.sb("draw", [P, LORA_M, D])
        dw = s.pair("dw", [P, LORA_M, D])
        araw = s.sb("araw", [P, DC, P])
        aw = s.pair("aw", [P, DC, P])
        bw = s.sb("bw", [2 * LORA_R, 2, LORA_F * P])
        a2 = s.sb("a2", [P, LORA_F, LORA_R])
        b2 = s.sb("b2", [LORA_R, D])
        la = s.sb("la", [2 * LORA_R, TOK])
        l2 = s.sb("l2", [LORA_R, TOK])
        xs = s.sb("xs", [P, TT, P])
        xsT = s.pair("xsT", [P, TOK])
        sg = s.sb("sg", [P, 2, TOK])
        hid = s.sb("hid", [P, LORA_F, TOK])
        hs = s.sb("hs", [P, LORA_M, TOK])
        hs_s = s.pair("hss", [P, LORA_M, TOK])
        gubank = [s.ps(f"gubank{i}") for i in range(2)]
        lbank = s.ps("lbank")
        ybank = [s.ps(f"ybank{i}") for i in range(TT)]

        g_loaded = s.sem("g_loaded")
        d_loaded = s.sem("d_loaded")
        next_loaded = s.sem("next_loaded")
        a_loaded = s.sem("a_loaded")
        small_loaded = s.sem("small_loaded")
        g_hi, g_lo = s.sem("g_hi"), s.sem("g_lo")
        d_hi, d_lo = s.sem("d_hi"), s.sem("d_lo")
        a_hi, a_lo = s.sem("a_hi"), s.sem("a_lo")
        xs_done = s.sem("xs_done")
        xs_tr = s.sem("xs_tr")
        xs_hi, xs_lo = s.sem("xs_hi"), s.sem("xs_lo")
        la_done, la_read = s.sem("la_done"), s.sem("la_read")
        gu_done, silu_done, hid_done = s.sem("gu_done"), s.sem("silu_done"), s.sem("hid_done")
        l2_done, l2_read = s.sem("l2_done"), s.sem("l2_read")
        hs_done, hs_hi, hs_lo = s.sem("hs_done"), s.sem("hs_hi"), s.sem("hs_lo")
        y_done, added = s.sem("y_done"), s.sem("added")

        with nc.Block() as block:
            @block.sync
            def _(sp):
                sp.dma_start(araw[:], a["lora_a"]).then_inc(a_loaded, 16)
                sp.dma_start(graw[:], a["lora_g"]).then_inc(g_loaded, 16)
                sp.dma_start(bw[:], a["lora_b"]).then_inc(small_loaded, 16)
                sp.dma_start(a2[:], a["lora_a2"]).then_inc(small_loaded, 16)
                sp.dma_start(b2[:], a["lora_b2"]).then_inc(small_loaded, 16)
                sp.dma_start(draw[:], a["lora_d"]).then_inc(d_loaded, 16)
                sp.wait_ge(d_loaded, 16)
                for slot in range(2):
                    sp.dma_start(g["stage"][:, slot, :], a["l1_wq"][slot]).then_inc(next_loaded, 16)
                sp.wait_ge(next_loaded, 32)

            @block.gpsimd
            def _(pool):
                ln.gpsimd(pool)

            @block.tensor
            def _(pe):
                ln.tensor(pe)
                for t in range(TT):
                    pe.wait_ge(xs_done, t + 1)
                    nc.tensor.transpose(lbank[:, t * P:(t + 1) * P], xs[:, t, :], ident[:]).then_inc(xs_tr, 1)
                ln.wait_ready(pe)
                pe.wait_ge(a_lo, 1)
                for c in range(DC):
                    last = mm3(nc, gubank[0][:, 0:TOK], tuple(w[:, c, :] for w in aw),
                               tuple(v[:, c, :] for v in xT), c == 0, c == DC - 1)
                last.then_inc(la_done, 1)
                pe.wait_ge(small_loaded, 48)
                pe.wait_ge(xs_lo, 1)
                pe.wait_ge(la_read, 1)
                for f in range(LORA_F):
                    if f % LORA_REP == 0 and f // LORA_REP < 3:
                        pe.wait_ge(g_lo, f // LORA_REP + 1)
                    need(pe, hid_done, f - 1)
                    for part in range(2):
                        out = gubank[f % 2][:, part * TOK:(part + 1) * TOK]
                        mm3(nc, out, tuple(w[:, part, f * P:(f + 1) * P] for w in gw),
                            tuple(v[:] for v in xsT), True, False)
                        last = nc.tensor.matmul(out, bw[:, part, f * P:(f + 1) * P], la[:], start=False, stop=True)
                    last.then_inc(gu_done, 1)
                pe.wait_ge(xs_hi, 1)
                for f in range(LORA_F):
                    pe.wait_ge(hid_done, f + 1)
                    last = nc.tensor.matmul(lbank[0:LORA_R, 0:TOK], a2[:, f, :], hid[:, f, :],
                                            start=(f == 0), stop=(f == LORA_F - 1))
                last.then_inc(l2_done, 1)
                pe.wait_ge(hs_lo, 1)
                pe.wait_ge(d_lo, 1)
                pe.wait_ge(l2_read, 1)
                for t in range(TT):
                    for m in range(LORA_M):
                        mm3(nc, ybank[t][:], tuple(v[:, m, t * P:(t + 1) * P] for v in hs_s),
                            tuple(w[:, m, :] for w in dw), m == 0, False)
                    nc.tensor.matmul(ybank[t][:], l2[:, t * P:(t + 1) * P], b2[:], start=False,
                                     stop=True).then_inc(y_done, 1)

            def thirds(ap, m):
                n = LORA_REP * P
                return ap[:, :, m * n:(m + 1) * n]

            @block.scalar
            def _(act):
                act.wait_ge(a_loaded, 16)
                nc.scalar.activation(aw[0][:], araw[:], ACT.Copy).then_inc(a_hi, 1)
                ln.scalar(act)
                act.wait_ge(xs_tr, TT)
                nc.scalar.activation(xsT[0][:], lbank[:, 0:TOK], ACT.Copy).then_inc(xs_hi, 1)
                act.wait_ge(g_loaded, 16)
                nc.scalar.activation(thirds(gw[0], 0), thirds(graw, 0), ACT.Copy).then_inc(g_hi, 1)
                act.wait_ge(la_done, 1)
                nc.scalar.activation(la[:], gubank[0][0:2 * LORA_R, 0:TOK], ACT.Copy, scale=0.5).then_inc(la_read, 1)
                for m in range(1, LORA_M):
                    nc.scalar.activation(thirds(gw[0], m), thirds(graw, m), ACT.Copy).then_inc(g_hi, 1)
                for f in range(LORA_F):
                    act.wait_ge(gu_done, f + 1)
                    need(act, hid_done, f - 1)
                    nc.scalar.activation(sg[:, f % 2, :], gubank[f % 2][:, 0:TOK], ACT.Silu).then_inc(silu_done, 1)
                    if f == 2:
                        act.wait_ge(d_loaded, 16)
                        nc.scalar.activation(dw[0][:], draw[:], ACT.Copy).then_inc(d_hi, 1)
                act.wait_ge(hs_done, LORA_M)
                nc.scalar.activation(hs_s[0][:], hs[:], ACT.Copy).then_inc(hs_hi, 1)
                act.wait_ge(l2_done, 1)
                nc.scalar.activation(l2[:], lbank[0:LORA_R, 0:TOK], ACT.Copy, scale=0.5).then_inc(l2_read, 1)

            @block.vector
            def _(dve):
                ln.vector(dve)
                for t in range(TT):
                    dve.wait_ge(ln.normed, t + 1)
                    nc.vector.tensor_reduce(xs[:, t, :], ln.xn[:, t, :].rearrange("p (c k) -> p k c", c=DC),
                                            AX.X, ALU.add).then_inc(xs_done, 1)
                dve.wait_ge(a_hi, 1)
                nc.vector.tensor_tensor(aw[1][:], araw[:], as_f32(aw[0][:]), ALU.subtract).then_inc(a_lo, 1)
                dve.wait_ge(xs_hi, 1)
                nc.vector.tensor_tensor(xsT[1][:], lbank[:, 0:TOK], as_f32(xsT[0][:]), ALU.subtract).then_inc(xs_lo, 1)
                for m in range(LORA_M):
                    dve.wait_ge(g_hi, m + 1)
                    nc.vector.tensor_tensor(thirds(gw[1], m), thirds(graw, m), as_f32(thirds(gw[0], m)),
                                            ALU.subtract).then_inc(g_lo, 1)
                for f in range(LORA_F):
                    dve.wait_ge(silu_done, f + 1)
                    nc.vector.tensor_tensor(hid[:, f, :], sg[:, f % 2, :], gubank[f % 2][:, TOK:2 * TOK],
                                            ALU.mult).then_inc(hid_done, 1)
                    if f == 2:
                        dve.wait_ge(d_hi, 1)
                        nc.vector.tensor_tensor(dw[1][:], draw[:], as_f32(dw[0][:]), ALU.subtract).then_inc(d_lo, 1)
                    if f % LORA_REP == LORA_REP - 1:
                        m = f // LORA_REP
                        dve.wait_ge(hid_done, f + 1)
                        nc.vector.tensor_reduce(hs[:, m, :], hid[:, m * LORA_REP:(m + 1) * LORA_REP, :]
                                                .rearrange("p j k -> p k j"), AX.X, ALU.add).then_inc(hs_done, 1)
                dve.wait_ge(hs_hi, 1)
                nc.vector.tensor_tensor(hs_s[1][:], hs[:], as_f32(hs_s[0][:]), ALU.subtract).then_inc(hs_lo, 1)
                for t in range(TT):
                    dve.wait_ge(y_done, t + 1)
                    nc.vector.tensor_tensor(x[:, t, :], x[:, t, :], ybank[t][:], ALU.add).then_inc(added, 1)


SH, SKV = 32, 8
SREP = SH // SKV
SD = D // SH
SKW = SKV * SD
SHALF = P // SEQ


def self_attention(nc, tag, g, a):
    x, ident = g["x"], g["ident"]
    NG = BT * SKV
    with ExitStack() as ctx:
        s = Space(nc, ctx, tag)
        xT = s.pair("xT", [P, DC, TOK])
        bank = [s.ps(f"bank{t}", 2) for t in range(TT)]
        sbank = s.ps("sbank", 2)
        obank = s.ps("obank")
        ybank = s.ps("ybank")
        KV = D
        ln = LayerNormT(nc, s, x, ident, xT, [b[:, 0:D] for b in bank])
        NWR = 3
        wraw = s.sb("wraw", [P, NWR, DC * D])
        ws = s.pair("ws", [P, NWR, DC * D])
        rope = s.sb("rope", [P, 2, SD])
        blocks = s.sb("blocks", [P, SKV])
        vblocks = s.sb("vblocks", [P, 2, SKV])
        spread = s.sb("spread", [P, BT, P])
        causal = s.sb("causal", [P, SEQ])
        rot = s.sb("rot", [P, TT, SH + SKV, SD])
        q = s.sb("q", [P, TT, SH, SD])
        k = s.sb("k", [P, TT, SKV, SD])
        v = s.sb("v", [P, TT, SKW])
        qT = s.sb("qT", [P, TT, BT, SREP, SEQ])
        kT = s.sb("kT", [P, TT, BT, SKV, SEQ])
        vb = s.sb("vb", [P, TT, 2, BT, SKW])
        sc = s.sb("sc", [P, TT, NG, SEQ])
        mx = s.sb("mx", [P, TT, NG])
        sm = s.sb("sm", [P, TT, NG])
        inv = s.sb("inv", [P, TT, NG])
        pr = s.sb("pr", [P, TT, NG, SEQ])
        pn = s.sb("pn", [P, TT, NG, SEQ])
        pT = s.sb("pT", [P, TT, BT * 2, P])
        oT = s.pair("oT", [P, TT, DC, P])

        loaded = [s.sem(f"loaded{i}") for i in range(NWR)]
        small_loaded = s.sem("small_loaded")
        w_hi, wq_lo, w_lo = s.sem("w_hi"), s.sem("wq_lo"), s.sem("w_lo")
        proj, roped = s.sem("proj"), s.sem("roped")
        v_read = s.sem("v_read")
        chain = s.sem("chain")
        qk_tr, q_read, k_read = s.sem("qk_tr"), s.sem("q_read"), s.sem("k_read")
        s_done = s.sem("s_done")
        s_read = s.sem("s_read")
        e_in, e_done = s.sem("e_in"), s.sem("e_done")
        v_spread, vb_ready = s.sem("v_spread"), s.sem("vb_ready")
        p_normed, p_tr = s.sem("p_normed"), s.sem("p_tr")
        pt_first, pt_second = s.sem("pt_first"), s.sem("pt_second")
        o_done, o_hi, o_lo = s.sem("o_done"), s.sem("o_hi"), s.sem("o_lo")
        y_done, added = s.sem("y_done"), s.sem("added")

        WIDTHS = [DC * D, DC * 2 * SKW, DC * D]
        with nc.Block() as block:
            @block.sync
            def _(sp):
                sp.dma_start(wraw[:, 0, :], a["s_wq"]).then_inc(loaded[0], 16)
                sp.dma_start(wraw[:, 1, 0:DC * 2 * SKW], a["s_wkv"]).then_inc(loaded[1], 16)
                sp.dma_start(rope[:], a["s_rope"]).then_inc(small_loaded, 16)
                sp.dma_start(blocks[:], a["s_blocks"]).then_inc(small_loaded, 16)
                sp.dma_start(causal[:], a["s_causal"]).then_inc(small_loaded, 16)
                sp.dma_start(vblocks[:], a["s_vblocks"]).then_inc(small_loaded, 16)
                sp.dma_start(spread[:], a["s_spread"]).then_inc(small_loaded, 16)
                sp.dma_start(wraw[:, 2, :], a["s_wo"]).then_inc(loaded[2], 16)

            @block.gpsimd
            def _(pool):
                ln.gpsimd(pool)
                for i in range(1, NWR):
                    pool.wait_ge(w_hi, i + 1)
                    nc.gpsimd.tensor_tensor(ws[1][:, i, :WIDTHS[i]], wraw[:, i, :WIDTHS[i]],
                                            as_f32(ws[0][:, i, :WIDTHS[i]]), ALU.subtract).then_inc(w_lo, 1)

            @block.scalar
            def _(act):
                def w_part(i):
                    act.wait_ge(loaded[i], 16)
                    nc.scalar.activation(ws[0][:, i, :WIDTHS[i]], wraw[:, i, :WIDTHS[i]],
                                         ACT.Copy).then_inc(w_hi, 1)
                w_part(0)
                ln.scalar(act)
                w_part(1)
                for t in range(TT):
                    act.wait_ge(proj, t + 1)
                    nc.scalar.activation(v[:, t, :], bank[t][:, KV + SKW:KV + 2 * SKW], ACT.Copy).then_inc(v_read, 1)
                w_part(2)
                for t in range(TT):
                    act.wait_ge(qk_tr, t + 1)
                    nc.scalar.activation(qT[:, t, :, :, :],
                                         bank[t][:, 0:D].rearrange("p (r b n) -> p b r n", r=SREP, b=BT),
                                         ACT.Copy).then_inc(q_read, 1)
                for t in range(TT):
                    act.wait_ge(e_in, t + 1)
                    nc.scalar.activation(pr[:, t, :, :], sc[:, t, :, :], ACT.Exp).then_inc(e_done, 1)
                for t in range(TT):
                    act.wait_ge(p_tr, t + 1)
                    nc.scalar.activation(pT[:, t, 0:BT, :], bank[t][:, 0:D].rearrange("p (i n) -> p i n", i=BT),
                                         ACT.Copy).then_inc(pt_first, 1)
                    act.wait_ge(o_done, t + 1)
                    nc.scalar.activation(oT[0][:, t, :, :].rearrange("p r (b n) -> p r b n", b=BT),
                                         obank[:, :].rearrange("p (b r n) -> p r b n", b=BT, r=SREP),
                                         ACT.Copy).then_inc(o_hi, 1)

            @block.tensor
            def _(pe):
                ln.tensor(pe)
                ln.wait_ready(pe)
                for t in range(TT):
                    for i, n, at in ((0, D, 0), (1, 2 * SKW, KV)):
                        pe.wait_ge(w_lo if i else wq_lo, 1)
                        for c in range(DC):
                            last = mm3(nc, bank[t][:, at:at + n], tuple(h[:, c, t * P:(t + 1) * P] for h in xT),
                                       tuple(w[:, i, c * n:(c + 1) * n] for w in ws), c == 0, c == DC - 1)
                    last.then_inc(proj, 1)
                for t in range(TT):
                    pe.wait_ge(roped, t + 1)
                    pe.wait_ge(v_read, t + 1)
                    nc.tensor.transpose(bank[t][:, KV:KV + P], k[:, t, :, :].rearrange("p h d -> p (h d)"), ident[:])
                    for r in range(SREP):
                        last = nc.tensor.transpose(bank[t][:, r * P:(r + 1) * P],
                                                   q[:, t, r * SKV:(r + 1) * SKV, :].rearrange("p h d -> p (h d)"),
                                                   ident[:])
                    last.then_inc(qk_tr, 1)
                pe.wait_ge(small_loaded, 80)
                for t in range(TT):
                    pe.wait_ge(q_read, t + 1)
                    pe.wait_ge(k_read, t + 1)
                    need(pe, s_read, t)
                    for b in range(BT):
                        last = nc.tensor.matmul(sbank[:, b * SKV * SEQ:(b + 1) * SKV * SEQ],
                                                qT[:, t, b, :, :].rearrange("p r n -> p (r n)"),
                                                kT[:, t, b, :, :].rearrange("p h n -> p (h n)"), start=True, stop=True)
                    last.then_inc(s_done, 1)
                    for b in range(BT):
                        last = nc.tensor.matmul(bank[t][:, b * SKW:(b + 1) * SKW], spread[:, b, :], v[:, t, :],
                                                start=True, stop=True)
                    last.then_inc(v_spread, 1)

                def values(t):
                    pe.wait_ge(p_normed, t + 1)
                    pe.wait_ge(vb_ready, t + 1)
                    for i in range(2 * BT):
                        last = nc.tensor.transpose(bank[t][:, i * P:(i + 1) * P],
                                                   pn[:, t, i * SHALF:(i + 1) * SHALF, :]
                                                   .rearrange("p h n -> p (h n)"), ident[:])
                    last.then_inc(p_tr, 1)
                    pe.wait_ge(pt_first, t + 1)
                    pe.wait_ge(pt_second, t + 1)
                    need(pe, o_lo, t)
                    for b in range(BT):
                        for half in range(2):
                            last = nc.tensor.matmul(obank[:, b * P:(b + 1) * P], vb[:, t, half, b, :],
                                                    pT[:, t, 2 * b + half, :], start=(half == 0), stop=(half == 1))
                    last.then_inc(o_done, 1)

                def out(t):
                    pe.wait_ge(o_lo, t + 1)
                    pe.wait_ge(w_lo, 2)
                    need(pe, added, t)
                    for c in range(DC):
                        last = mm3(nc, ybank[:], tuple(h[:, t, c, :] for h in oT),
                                   tuple(w[:, 2, c * D:(c + 1) * D] for w in ws), c == 0, c == DC - 1)
                    last.then_inc(y_done, 1)
                values(0)
                out(0)
                values(1)
                out(1)

            @block.vector
            def _(dve):
                links = [0]

                def link(ins):
                    ins.then_inc(chain, 1)
                    links[0] += 1
                    dve.wait_ge(chain, links[0])

                def wq_rest():
                    dve.wait_ge(w_hi, 1)
                    nc.vector.tensor_tensor(ws[1][:, 0, :], wraw[:, 0, :], as_f32(ws[0][:, 0, :]),
                                            ALU.subtract).then_inc(wq_lo, 1)

                def rotate(t):
                    H2 = SD // 2
                    dve.wait_ge(proj, t + 1)
                    parts = []
                    for src, dst, heads, at in ((bank[t][:, 0:D], q, SH, 0), (bank[t][:, KV:KV + SKW], k, SKV, SH)):
                        halves = src.rearrange("p (h d) -> p h d", d=SD)
                        if heads == SKV:
                            dve.wait_ge(v_read, t + 1)

                        def table(i, lo, hi):
                            return rope[:, i, lo:hi].unsqueeze(1).broadcast_to([P, heads, hi - lo])
                        nc.vector.tensor_tensor(rot[:, t, at:at + heads, 0:H2], halves[:, :, H2:SD],
                                                table(1, 0, H2), ALU.mult)
                        nc.vector.tensor_tensor(rot[:, t, at:at + heads, H2:SD], halves[:, :, 0:H2],
                                                table(1, H2, SD), ALU.mult)
                        parts.append((nc.vector.tensor_tensor(dst[:, t, :, :], halves, table(0, 0, SD), ALU.mult),
                                      dst, heads, at))
                    link(parts[-1][0])
                    for _, dst, heads, at in parts:
                        last = nc.vector.tensor_tensor(dst[:, t, :, :], dst[:, t, :, :],
                                                       rot[:, t, at:at + heads, :], ALU.add)
                    last.then_inc(roped, 1)

                def key_blocks(t):
                    dve.wait_ge(qk_tr, t + 1)
                    nc.vector.tensor_tensor(
                        kT[:, t, :, :, :],
                        bank[t][:, KV:KV + P].rearrange("p (b n) -> p b n", b=BT).unsqueeze(2)
                        .broadcast_to([P, BT, SKV, SEQ]),
                        blocks[:, :].unsqueeze(1).unsqueeze(3).broadcast_to([P, BT, SKV, SEQ]),
                        ALU.mult).then_inc(k_read, 1)

                def wide(ap):
                    return ap.unsqueeze(2).broadcast_to([P, NG, SEQ])

                def shifted(t):
                    dve.wait_ge(s_done, t + 1)
                    last = nc.vector.scalar_tensor_tensor(
                        out=sc[:, t, :, :], in0=sbank[:, :].rearrange("p (h n) -> p h n", h=NG), scalar=SD ** -0.5,
                        in1=causal[:, :].unsqueeze(1).broadcast_to([P, NG, SEQ]), op0=ALU.mult, op1=ALU.add)
                    last.then_inc(s_read, 1)
                    dve.wait_ge(s_read, t + 1)
                    link(nc.vector.tensor_reduce(mx[:, t, :], sc[:, t, :, :], AX.X, ALU.max))
                    nc.vector.tensor_tensor(sc[:, t, :, :], sc[:, t, :, :], wide(mx[:, t, :]),
                                            ALU.subtract).then_inc(e_in, 1)

                def value_blocks(t):
                    dve.wait_ge(v_spread, t + 1)
                    for half in range(2):
                        last = nc.vector.tensor_tensor(
                            vb[:, t, half, :, :].rearrange("p b (h d) -> p b h d", d=SD),
                            bank[t][:, 0:BT * SKW].rearrange("p (b h d) -> p b h d", b=BT, d=SD),
                            vblocks[:, half, :].unsqueeze(1).unsqueeze(3).broadcast_to([P, BT, SKV, SD]), ALU.mult)
                    last.then_inc(vb_ready, 1)

                def normalised(t):
                    dve.wait_ge(e_done, t + 1)
                    link(nc.vector.tensor_reduce(sm[:, t, :], pr[:, t, :, :], AX.X, ALU.add))
                    link(nc.vector.reciprocal(inv[:, t, :], sm[:, t, :]))
                    nc.vector.tensor_tensor(pn[:, t, :, :], pr[:, t, :, :], wide(inv[:, t, :]),
                                            ALU.mult).then_inc(p_normed, 1)

                def second_pt(t):
                    dve.wait_ge(p_tr, t + 1)
                    nc.vector.tensor_copy(pT[:, t, BT:2 * BT, :],
                                          bank[t][:, D:2 * D].rearrange("p (i n) -> p i n", i=BT)).then_inc(pt_second, 1)

                def o_rest(t):
                    dve.wait_ge(o_hi, t + 1)
                    nc.vector.tensor_tensor(oT[1][:, t, :, :].rearrange("p r (b n) -> p r b n", b=BT),
                                            obank[:, :].rearrange("p (b r n) -> p r b n", b=BT, r=SREP),
                                            as_f32(oT[0][:, t, :, :]).rearrange("p r (b n) -> p r b n", b=BT),
                                            ALU.subtract).then_inc(o_lo, 1)

                def add(t):
                    dve.wait_ge(y_done, t + 1)
                    nc.vector.tensor_tensor(x[:, t, :], x[:, t, :], ybank[:], ALU.add).then_inc(added, 1)

                ln.vector(dve, wq_rest)
                dve.wait_ge(small_loaded, 80)
                rotate(0)
                rotate(1)
                key_blocks(0)
                key_blocks(1)
                shifted(0)
                value_blocks(0)
                normalised(0)
                shifted(1)
                second_pt(0)
                value_blocks(1)
                normalised(1)
                o_rest(0)
                second_pt(1)
                add(0)
                o_rest(1)
                add(1)


EXPERTS = 16
SHARED_T = 4


def experts(nc, tag, g, a):
    x, ident = g["x"], g["ident"]
    NF = SHARED_T + EXPERTS
    assert SHARED_T == GatedTiles.RING and NF % GatedTiles.RING == 0
    E = EXPERTS
    with ExitStack() as ctx:
        s = Space(nc, ctx, tag)
        xT = s.pair("xT", [P, DC, TOK])
        tbank = [s.ps(f"tbank{i}") for i in range(2)]
        rbank = s.ps("rbank")
        ln = LayerNormT(nc, s, x, ident, xT, tbank)
        G = GatedTiles(nc, s, xT, NF)
        cbank = tbank
        rraw = s.sb("rraw", [P, DC, E])
        rw = s.pair("rw", [P, DC, E])
        rank = s.sb("rank", [P, E])
        mine = s.sb("mine", [E, E])
        ones = s.sb("ones", [E, P])
        nmx = s.sb("nmx", [P, TT])
        pe_ = s.sb("prob", [P, TT, E])
        tot = s.sb("tot", [P, TT])
        inv = s.sb("inv", [P, TT])
        prob = s.sb("p", [P, TT, E])
        rest = s.sb("rest", [P, TT, E])
        hot = s.sb("hot", [P, 2, TT, E])
        tmp = s.sb("tmp", [P, TT, E])
        best = s.sb("best", [P, 2, TT])
        top = s.sb("top", [P, TT])
        comb = s.sb("comb", [P, TT, E])
        combT = s.sb("combT", [E, TOK])
        diag = s.sb("diag", [E, E, TOK])

        r_loaded = s.sem("r_loaded")
        r_hi, r_lo = s.sem("r_hi"), s.sem("r_lo")
        ones_set = s.sem("ones_set")
        logits, nmx_done, exp_done = s.sem("logits"), s.sem("nmx_done"), s.sem("exp_done")
        chain = s.sem("chain")
        comb_done, comb_tr, comb_read = s.sem("comb_done"), s.sem("comb_tr"), s.sem("comb_read")
        diag_done = s.sem("diag_done")
        cast_done = s.sem("cast_done")
        added = s.sem("added")

        with nc.Block() as block:
            @block.sync
            def _(sp):
                sp.dma_start(rraw[:], a["e_router"]).then_inc(r_loaded, 16)
                sp.dma_start(rank[:], a["e_rank"]).then_inc(r_loaded, 16)
                sp.dma_start(mine[:], a["ident"][0:E, 0:E]).then_inc(r_loaded, 16)

                def step(i):
                    for k in range(G.RING):
                        f = G.RING * i + k
                        G.load(sp, a["e_w"][bass.ds(f, 1), :, :].rearrange("a p n -> p (a n)"), f, k)
                peeled(sp, NF // G.RING, step)

            @block.gpsimd
            def _(pool):
                ln.gpsimd(pool)
                nc.gpsimd.memset(ones[:], 1.0).then_inc(ones_set, 1)

            @block.tensor
            def _(pe):
                ln.tensor(pe)
                ln.wait_ready(pe)
                pe.wait_ge(ones_set, 1)
                pe.wait_ge(r_lo, 1)
                for t in range(TT):
                    for c in range(DC):
                        last = mm3(nc, rbank[:, t * E:(t + 1) * E], tuple(h[:, c, t * P:(t + 1) * P] for h in xT),
                                   tuple(w[:, c, :] for w in rw), c == 0, c == DC - 1)
                last.then_inc(logits, 1)

                def step(i):
                    for k in range(G.RING):
                        f = G.RING * i + k
                        if not is_at(i, 0):
                            e = f - SHARED_T
                            if k == 0:
                                pe.wait_ge(diag_done, i)
                            pe.wait_ge(G.a_done_sem, f - 1)
                            nc.tensor.matmul(cbank[k % 2][:, 0:TOK], ones[:],
                                             diag[:, bass.ds(e, 1), :].rearrange("p a n -> p (a n)"),
                                             start=True, stop=True).then_inc(cast_done, 1)
                        G.gate_up(pe, f, k)
                        if is_at(f, G.RING - 1):
                            for t in range(TT):
                                pe.wait_ge(comb_done, 1)
                                last = nc.tensor.transpose(rbank[0:E, t * P:(t + 1) * P], comb[:, t, :], ident[:])
                            last.then_inc(comb_tr, 1)
                        if not is_at(f, 0):
                            G.down(pe, f - 1, (k - 1) % G.RING, is_at(f, 1), False)
                peeled(pe, NF // G.RING, step)
                G.down(pe, NF - 1, (NF - 1) % G.RING, False, True)

            @block.scalar
            def _(act):
                act.wait_ge(r_loaded, 48)
                nc.scalar.activation(rw[0][:], rraw[:], ACT.Copy).then_inc(r_hi, 1)
                ln.scalar(act)
                G.gu_hi(act, 0, 0, 0)
                act.wait_ge(nmx_done, 1)
                for t in range(TT):
                    last = nc.scalar.activation(pe_[:, t, :], rbank[:, t * E:(t + 1) * E], ACT.Exp,
                                                bias=nmx[:, t:t + 1], accum_out=tot[:, t:t + 1])
                    last.then_inc(exp_done, 1)

                def step(i):
                    for k in range(G.RING):
                        f = G.RING * i + k
                        G.scalar(act, f, i, k, is_at(f, NF - 1))
                peeled(act, NF // G.RING, step)

            @block.vector
            def _(dve):
                links = [0]

                def link(ins):
                    ins.then_inc(chain, 1)
                    links[0] += 1
                    dve.wait_ge(chain, links[0])

                def wide(ap):
                    return ap.unsqueeze(2).broadcast_to([P, TT, E])

                ranks = rank[:, :].unsqueeze(1).broadcast_to([P, TT, E])
                ln.vector(dve)
                dve.wait_ge(r_hi, 1)
                nc.vector.tensor_tensor(rw[1][:], rraw[:], as_f32(rw[0][:]), ALU.subtract).then_inc(r_lo, 1)
                G.gu_lo(dve, 0, 0)
                dve.wait_ge(logits, 1)
                nc.vector.tensor_reduce(nmx[:], rbank[:, 0:TT * E].rearrange("p (t e) -> p t e", t=TT), AX.X,
                                        ALU.max, negate=True).then_inc(nmx_done, 1)

                def probabilities():
                    dve.wait_ge(exp_done, TT)
                    link(nc.vector.reciprocal(inv[:], tot[:]))
                    link(nc.vector.tensor_tensor(prob[:], pe_[:], wide(inv[:, :]), ALU.mult))

                def choose(r, left):
                    link(nc.vector.tensor_reduce(best[:, r, :], left[:], AX.X, ALU.max))
                    link(nc.vector.tensor_tensor(tmp[:], left[:], wide(best[:, r, :]), ALU.is_equal))
                    link(nc.vector.tensor_tensor(tmp[:], tmp[:], ranks, ALU.mult))
                    link(nc.vector.tensor_reduce(top[:], tmp[:], AX.X, ALU.max))
                    link(nc.vector.tensor_tensor(hot[:, r, :, :], tmp[:], wide(top[:, :]), ALU.is_equal))

                def weigh():
                    link(nc.vector.tensor_tensor(top[:], best[:, 0, :], best[:, 1, :], ALU.add))
                    link(nc.vector.reciprocal(top[:], top[:]))
                    link(nc.vector.tensor_tensor(hot[:, 0, :, :], hot[:, 0, :, :], wide(best[:, 0, :]), ALU.mult))
                    link(nc.vector.tensor_tensor(hot[:, 1, :, :], hot[:, 1, :, :], wide(best[:, 1, :]), ALU.mult))
                    link(nc.vector.tensor_tensor(tmp[:], hot[:, 0, :, :], hot[:, 1, :, :], ALU.add))
                    nc.vector.tensor_tensor(comb[:], tmp[:], wide(top[:, :]), ALU.mult).then_inc(comb_done, 1)

                def route(f):
                    if f == 0:
                        probabilities()
                        choose(0, prob)
                    elif f == 1:
                        link(nc.vector.tensor_scalar(tmp[:], hot[:, 0, :, :], -2.0, None, ALU.mult))
                        link(nc.vector.tensor_tensor(rest[:], prob[:], tmp[:], ALU.add))
                        choose(1, rest)
                    elif f == 2:
                        weigh()

                def spread(i):
                    four = bass.ds(G.RING * i, G.RING)
                    nc.vector.tensor_tensor(diag[:, four, :], combT[:, :].unsqueeze(1).broadcast_to([E, G.RING, TOK]),
                                            mine[:, four].unsqueeze(2).broadcast_to([E, G.RING, TOK]),
                                            ALU.mult).then_inc(diag_done, 1)

                def step(i):
                    for k in range(G.RING):
                        f = G.RING * i + k
                        e = f - SHARED_T
                        combine = None if is_at(i, 0) else (cbank[k % 2][:, 0:TOK], cast_done, e + 1, e)
                        if is_at(f, G.RING - 1):
                            dve.wait_ge(comb_tr, 1)
                            nc.vector.tensor_copy(combT[:], rbank[0:E, 0:TOK]).then_inc(comb_read, 1)
                            dve.wait_ge(comb_read, 1)
                            spread(0)
                        G.vector(dve, f, k, is_at(f, NF - 1), combine)
                        if is_at(i, 0):
                            route(f)
                        if k == 1 and not is_at(i, 0) and not is_at(i, NF // G.RING - 1):
                            spread(i)
                peeled(dve, NF // G.RING, step)
                dve.wait_ge(G.down_done_sem, NF)
                for t in range(TT):
                    nc.vector.tensor_tensor(x[:, t, :], x[:, t, :], G.ybank[t][:], ALU.add).then_inc(added, 1)


def build_program(nc, phases=99, **a):
    with ExitStack() as ctx:
        s = Space(nc, ctx, "g")
        x = s.sb("x", [P, TT, D])
        ident = s.sb("ident", [P, P])
        stage, stage_r = s.twins("stage", [P, 2, DC * UW])
        g = {"x": x, "ident": ident, "stage": stage, "stage_r": stage_r, "vlat_dram": a["vlat_dram"], "a": a}
        loaded = s.sem("loaded")
        stored = s.sem("stored")
        SEMAPHORES.clear()
        with nc.Block() as block:
            @block.sync
            def _(sp):
                sp.dma_start(x[:], a["x"].rearrange("(t p) d -> p t d", p=P)).then_inc(loaded, 16)
                sp.dma_start(ident[:], a["ident"]).then_inc(loaded, 16)
                sp.wait_ge(loaded, 32)
        L0 = {"wkv": a["l0_wkv"], "wq": a["l0_wq"], "wo": a["l0_wo"], "norm": a["l0_norm"], "ctx": a["ctx"], "mask": None,
              "preloaded": False}
        L1 = {"wkv": a["l1_wkv"], "wq": a["l1_wq"], "wo": a["l1_wo"], "norm": a["l1_norm"], "ctx": a["ctx"], "mask": a["mask"],
              "preloaded": True}
        if phases >= 1:
            cross_attention(nc, "c0", g, L0, 1e-6, True)
            clear_semaphores(nc)
        if phases >= 2:
            mixer(nc, "m0", g, a)
            clear_semaphores(nc)
        if phases >= 3:
            lora_ffn(nc, "f0", g, a)
            clear_semaphores(nc)
        if phases >= 4:
            cross_attention(nc, "c1", g, L1, 1e-5, False)
            clear_semaphores(nc)
        if phases >= 5:
            self_attention(nc, "s1", g, a)
            clear_semaphores(nc)
        if phases >= 6:
            experts(nc, "e1", g, a)
        with nc.Block() as block:
            @block.sync
            def _(sp):
                sp.dma_start(a["out"].rearrange("(t p) d -> p t d", p=P), x[:]).then_inc(stored, 16)
                sp.wait_ge(stored, 16)


def lay_out(i):
    def c_major(w_cn):
        n = w_cn.shape[1]
        return w_cn.reshape(DC, P, n).transpose(1, 0, 2).reshape(P, DC * n)

    def halves(w_cn, width):
        return np.stack([c_major(w_cn[:, k:k + width]) for k in range(0, w_cn.shape[1], width)])

    def wkv(wk, wv):
        return np.concatenate([halves(wk, UW), halves(wv, UW)])

    def heads(wo):
        return wo.reshape(HEADS // GROUP, GROUP, HD, D).transpose(0, 2, 1, 3).reshape(HEADS // GROUP, P, GROUP * D)

    o = {"x": i["x"].reshape(TOK, D), "ident": np.eye(P, dtype=np.float32)}
    o["ctx"] = i["ctx_4096"].reshape(B, CT, P, DC, P).transpose(0, 4, 1, 3, 2).reshape(B, P, CT * DC * P)
    o["mask"] = i["mask_1x1xSxS2_ff0"].reshape(SEQ, CTX)
    o["l0_wkv"] = wkv(i["L0_xattn_Wk"], i["L0_xattn_Wv"])
    o["l0_wq"] = halves(i["L0_xattn_Wq"], UW)
    o["l0_wo"] = heads(i["L0_xattn_Wo"])
    o["l0_norm"] = np.stack([i["L0_xattn_q_norm_w"], i["L0_xattn_k_norm_w"]], 1)
    o["l1_wkv"] = wkv(i["L1_xattn_Wk"].T, i["L1_xattn_Wv"].T)
    o["l1_wq"] = halves(i["L1_xattn_Wq"].T, UW)
    o["l1_wo"] = heads(i["L1_xattn_Wo"].T)
    o["l1_norm"] = np.stack([i["L1_xattn_q_norm_w"], i["L1_xattn_k_norm_w"]], 1)
    return lay_out_rest(i, o)


def lay_out_rest(i, o):
    def tile_gud(gate, up, down):
        n = gate.shape[0]
        out = np.zeros((P, GatedTiles.WIDTH), np.float32)
        for part, w in enumerate((gate, up)):
            view = out[:, part * DC * P:(part + 1) * DC * P].reshape(P, DC, P)
            view[:, :, :n] = w.T.reshape(DC, P, n).transpose(1, 0, 2)
        out[:n, GatedTiles.GU:] = down.T
        return out

    def c_major(w_cn):
        n = w_cn.shape[1]
        return w_cn.reshape(DC, P, n).transpose(1, 0, 2).reshape(P, DC * n)

    gw, uw, dw = i["L0_attn_ffn_gate_w"], i["L0_attn_ffn_up_w"], i["L0_attn_ffn_down_w"]
    F = gw.shape[0]
    o["mix_ffn"] = np.stack([tile_gud(gw[k:k + P], uw[k:k + P], dw[:, k:k + P]) for k in range(0, F, P)])
    o["mix_proj"] = np.concatenate([c_major(i["L0_attn_gate_w"].T), c_major(i["L0_attn_up_w"].T)], 1)
    o["mix_point"] = i["L0_attn_local_point"].reshape(P, 1)
    o["mix_disc"] = i["L0_attn_discount_factor"]
    o["mix_out"] = np.concatenate([i["L0_attn_local_approx_output"].T[:, None, :],
                                   i["L0_attn_fuse_weight"].transpose(1, 2, 0)], 1)
    padded = LORA_M * P

    def by_tile(w):
        lead = w.shape[:-1]
        out = np.zeros(lead + (LORA_REP, padded), np.float32)
        out[..., :LORA_HQ] = w.reshape(lead + (LORA_REP, LORA_HQ))
        out = out.reshape(lead + (LORA_REP, LORA_M, P))
        return np.swapaxes(out, -3, -2).reshape(lead + (LORA_F * P,))

    o["lora_g"] = np.stack([by_tile(i["L0_ffn_w1q"].T), by_tile(i["L0_ffn_w3q"].T)], 1)
    d = np.zeros((padded, D), np.float32)
    d[:LORA_HQ] = i["L0_ffn_w2q"].T
    o["lora_d"] = d.reshape(LORA_M, P, D).transpose(1, 0, 2)
    la = np.zeros((D, P), np.float32)
    la[:, 0:LORA_R] = i["L0_ffn_a1"].T
    la[:, LORA_R:2 * LORA_R] = i["L0_ffn_a3"].T
    o["lora_a"] = la.reshape(DC, P, P).transpose(1, 0, 2)
    lb = np.zeros((2 * LORA_R, 2, LORA_F * P), np.float32)
    lb[0:LORA_R, 0] = by_tile(i["L0_ffn_b1"].T)
    lb[LORA_R:, 1] = by_tile(i["L0_ffn_b3"].T)
    o["lora_b"] = lb
    o["lora_a2"] = by_tile(i["L0_ffn_a2"]).reshape(LORA_R, LORA_F, P).transpose(2, 1, 0)
    o["lora_b2"] = i["L0_ffn_b2"].T
    def by_repeat(w):
        return w.reshape(SKV, SREP, SD, -1).transpose(1, 0, 2, 3).reshape(D, -1)

    o["s_wq"] = c_major(by_repeat(i["L1_attn_Wq"]).T)
    o["s_wkv"] = c_major(np.concatenate([i["L1_attn_Wk"].T, i["L1_attn_Wv"].T], 1))
    o["s_wo"] = c_major(by_repeat(i["L1_attn_Wo"].T))
    o["s_rope"], o["s_blocks"], o["s_vblocks"], o["s_spread"], o["s_causal"] = tables()
    sg, su = np.split(i["L1_ffn_shared_w_gate_up"], 2)
    sd = i["L1_ffn_shared_w_down"]
    tiles = [tile_gud(sg[k:k + P], su[k:k + P], sd[:, k:k + P]) for k in range(0, SHARED_T * P, P)]
    for e in range(EXPERTS):
        eg, eu = np.split(i["L1_ffn_w_gate_up"][e], 2)
        tiles.append(tile_gud(eg, eu, i["L1_ffn_w_down"][e]))
    o["e_w"] = np.stack(tiles)
    o["e_router"] = i["L1_ffn_gate_w"].T.reshape(DC, P, EXPERTS).transpose(1, 0, 2)
    o["e_rank"] = np.tile(np.arange(EXPERTS, 0, -1, dtype=np.float32), (P, 1))
    return o


def tables():
    theta, factor, hi_f, lo_f, orig = 500000.0, 32.0, 4.0, 1.0, 1024
    f32 = np.float32
    inv = (f32(1.0) / f32(theta) ** (np.arange(0, SD, 2, dtype=f32) / f32(SD))).astype(f32)
    wavelen = (f32(2.0 * np.pi) / inv).astype(f32)
    base = np.where(wavelen > orig / lo_f, inv / f32(factor), inv).astype(f32)
    smooth = ((orig / wavelen - lo_f) / (hi_f - lo_f)).astype(f32)
    smoothed = ((1.0 - smooth) * base / f32(factor) + smooth * base).astype(f32)
    medium = ~(wavelen < orig / lo_f) & ~(wavelen > orig / hi_f)
    freqs = np.arange(SEQ, dtype=f32)[:, None] * np.where(medium, smoothed, base).astype(f32)[None, :]
    freqs = freqs.astype(f32)
    cos, sin = np.cos(freqs), np.sin(freqs)
    rope = np.stack([np.concatenate([cos, cos], 1), np.concatenate([-sin, sin], 1)], 1)
    rope = np.tile(rope, (BT, 1, 1)).astype(f32)
    rows = np.arange(P)
    blocks = (rows[:, None] // SD == np.arange(SKV)[None, :]).astype(f32)
    vblocks = (rows[:, None, None] // SEQ + SHALF * np.arange(2)[None, :, None]
               == np.arange(SKV)[None, None, :]).astype(f32)
    spread = (rows[:, None, None] == SEQ * np.arange(BT)[None, :, None] + rows[None, None, :] % SEQ).astype(f32)
    causal = np.where(np.arange(SEQ)[None, :] <= np.arange(SEQ)[:, None], 0.0, -3.0e38)
    return rope, blocks, vblocks, spread, np.tile(causal, (BT, 1)).astype(f32)


def kernel(**inputs):
    import concourse.bacc as bacc
    from concourse.bass_utils import run_bass_kernel_spmd

    given = {name: np.asarray(v) for name, v in inputs.items()}
    nc = bacc.Bacc("TRN2", target_bir_lowering=False, num_devices=1)
    arrays, aps = {}, {}
    for name, v in lay_out(given).items():
        v = np.ascontiguousarray(v)
        arrays[f"in_{name}"] = v
        aps[name] = nc.dram_tensor(f"in_{name}", v.shape, mybir.dt.from_np(v.dtype), kind="ExternalInput").ap()
    aps["vlat_dram"] = nc.dram_tensor("vlat_dram", (TOK, 2 * UW), F32).ap()
    aps["out"] = nc.dram_tensor("out_dram", (TOK, D), F32, kind="ExternalOutput").ap()
    build_program(nc, **aps)
    r = run_bass_kernel_spmd(nc, [arrays], core_ids=[0])
    return r.results[0]["out_dram"].reshape(B, SEQ, D)
```
